# Optimizing a Trainium2 kernel written in Bass

```python
import numpy as np
import jax
import jax.numpy as jnp

def _softmax(x, axis=-1):
    return jax.nn.softmax(x, axis=axis)

def _gelu(x):
    return jax.nn.gelu(x, approximate=True)

def _silu(x):
    return jax.nn.silu(x)

def _sigmoid(x):
    return jax.nn.sigmoid(x)

def _layernorm(x, axis=-1, eps=1e-05):
    m = jnp.mean(x, axis=axis, keepdims=True)
    v = jnp.var(x, axis=axis, keepdims=True)
    return (x - m) / jnp.sqrt(v + eps)

def _scatter_add(tgt, idx, src, axis=0):
    return tgt.at[idx].add(src)

def _segment_sum(src, seg, n):
    return jax.ops.segment_sum(src, seg, n)
kernel_name = 'mk_decoder_postln_d2_seqx_r4_b58be7'

def setup_inputs(seed: int=0):
    np.random.seed(seed)
    _w = jnp.asarray

    def _rec_inputs():
        import jax
        import jax.numpy as jnp
        _rk = jax.random.key(seed)
        x = 7.22e-05 + 1 * jax.random.normal(jax.random.fold_in(_rk, 1), (32, 128, 256), jnp.float32)
        _lenS = 128 - jax.random.randint(jax.random.fold_in(_rk, 7), (32,), 0, max(1, 128 // 4) + 1, jnp.int32)
        _lenS2 = 128 - jax.random.randint(jax.random.fold_in(_rk, 8), (32,), 0, max(1, 128 // 4) + 1, jnp.int32)
        _ctx_1024P = jax.random.normal(jax.random.fold_in(_rk, 11), (32, 16, 256), jnp.float32)
        _ctx_1024c = jax.random.dirichlet(jax.random.fold_in(_rk, 511), 0.3 * jnp.ones((16,), jnp.float32), (32, 128))
        _ctx_1024t = jnp.einsum('bsk,bkd->bsd', _ctx_1024c, _ctx_1024P)
        _ctx_1024t = _ctx_1024t * jax.lax.rsqrt(jnp.mean(jnp.square(_ctx_1024t)) + 1e-12) * 0.953939
        ctx_1024 = 4.13588e-05 + 0.999923 * (_ctx_1024t + 0.3 * jax.random.normal(jax.random.fold_in(_rk, 611), (32, 128, 256), jnp.float32))
        _validS = jnp.arange(128)[None, :] < _lenS[:, None]
        _validS2 = jnp.arange(128)[None, :] < _lenS2[:, None]
        _causal = jnp.tril(jnp.ones((128, 128), dtype=bool))
        mask_SxS2_fk0 = jnp.where(jnp.broadcast_to(_validS2[0:1, :], (128, 128)), -1000000000.0, 0.0).astype(jnp.float32)
        return (x, ctx_1024, mask_SxS2_fk0)
    x, ctx_1024, mask_SxS2_fk0 = _rec_inputs()

    def _L0_attn_setup():
        import jax, jax.numpy as jnp
        import numpy as np
        D_MODEL = 256
        H = 16
        DH = D_MODEL // H
        WIN = 7
        PAD = WIN // 2
        B, L = (2, 1024)
        key = jax.random.key(seed)
        ks = jax.random.split(key, 12)
        s = lambda k, shape: jax.random.normal(k, shape, dtype=jnp.float32) * 0.02
        return {'x': jax.random.normal(ks[0], (B, L, D_MODEL), dtype=jnp.float32), 'wq': s(ks[1], (D_MODEL, D_MODEL)), 'wk': s(ks[2], (D_MODEL, D_MODEL)), 'wv': s(ks[3], (D_MODEL, D_MODEL)), 'wo': s(ks[4], (D_MODEL, D_MODEL)), 'bo': s(ks[5], (D_MODEL,)), 'cw1': s(ks[6], (H, 32, 1)), 'cb1': s(ks[7], (H, 32)), 'cw2': s(ks[8], (H, 32, 32)), 'cb2': s(ks[9], (H, 32)), 'cw3': s(ks[10], (H, 1, 32)), 'cb3': s(ks[11], (H, 1))}
    _L0_attn_all = _L0_attn_setup()
    _L0_attn_in = {k: v for k, v in _L0_attn_all.items() if k in ('wq', 'wk', 'wv', 'wo', 'bo', 'cw1', 'cb1', 'cw2', 'cb2', 'cw3', 'cb3')}
    del _L0_attn_all

    def _L0_xattn_setup():
        import jax, jax.numpy as jnp
        import numpy as np
        M = 256
        N = 256
        B, S = (4, 512)
        key = jax.random.key(seed)
        ks = jax.random.split(key, 7)
        scale = 1.0 / np.sqrt(M)
        q = jax.random.normal(ks[0], (B, S, M), dtype=jnp.float32)
        k = jax.random.normal(ks[1], (B, S, M), dtype=jnp.float32)
        v = jax.random.normal(ks[2], (B, S, N), dtype=jnp.float32)
        causal = jnp.tril(jnp.ones((S, S), dtype=bool))
        attn_mask = jnp.where(causal, 0.0, -1000000000.0).astype(jnp.float32)
        Wq = jax.random.normal(ks[3], (N, M), dtype=jnp.float32) * scale
        Wk = jax.random.normal(ks[4], (N, M), dtype=jnp.float32) * scale
        Wv = jax.random.normal(ks[5], (N, N), dtype=jnp.float32) * scale
        bv = jax.random.normal(ks[6], (N,), dtype=jnp.float32) * scale
        return {'q': q, 'k': k, 'v': v, 'attn_mask': attn_mask, 'Wq': Wq, 'Wk': Wk, 'Wv': Wv, 'bv': bv}
    _L0_xattn_all = _L0_xattn_setup()
    _L0_xattn_in = {k: v for k, v in _L0_xattn_all.items() if k in ('Wq', 'Wk', 'Wv', 'bv')}
    del _L0_xattn_all

    def _L0_ffn_setup():
        import math
        import jax, jax.numpy as jnp
        import numpy as np
        E = 8
        H = 256
        HP = 128
        SPARSITY = 8
        N_ROTATE = 64
        ROPE_BASE = 10000.0

        def _rope(x, pos):
            half = N_ROTATE // 2
            inv_freq = 1.0 / ROPE_BASE ** (jnp.arange(half, dtype=jnp.float32) * 2.0 / N_ROTATE)
            ang = pos.astype(jnp.float32)[..., None] * inv_freq
            sin, cos = (jnp.sin(ang), jnp.cos(ang))
            x1, x2 = (x[..., :half], x[..., half:])
            return jnp.concatenate([x1 * cos - x2 * sin, x2 * cos + x1 * sin], axis=-1)
        key = jax.random.key(seed)
        k1, k2, k3, k4 = jax.random.split(key, 4)
        B, T = (4, 2048)
        X = jax.random.normal(k1, (B, T, H), dtype=jnp.float32)
        Wr = jax.random.uniform(k2, (E, H), minval=-1 / math.sqrt(H), maxval=1 / math.sqrt(H), dtype=jnp.float32)
        bq = 1 / math.sqrt(3 * HP)
        Wqkv = jax.random.uniform(k3, (E, H, 3 * HP), minval=-bq, maxval=bq, dtype=jnp.float32)
        bo = 1 / math.sqrt(H * E)
        Wo = jax.random.uniform(k4, (E, HP, H), minval=-bo, maxval=bo, dtype=jnp.float32)
        return {'X': X, 'Wr': Wr, 'Wqkv': Wqkv, 'Wo': Wo}
    _L0_ffn_all = _L0_ffn_setup()
    _L0_ffn_in = {k: v for k, v in _L0_ffn_all.items() if k in ('Wr', 'Wqkv', 'Wo')}
    del _L0_ffn_all

    def _L1_attn_setup():
        import jax, jax.numpy as jnp
        import numpy as np
        import math
        D = 256
        W = 128

        def _decay_mask(L, gamma, dtype):
            i = jnp.arange(L)
            diff = i[:, None] - i[None, :]
            same_block = i[:, None] // W == i[None, :] // W
            safe_exp = jnp.maximum(diff, 0).astype(dtype)
            in_block = jnp.where(diff >= 0, gamma ** safe_exp, jnp.zeros((), dtype))
            return jnp.where(same_block, in_block, jnp.ones((), dtype))
        key = jax.random.key(seed)
        ks = jax.random.split(key, 5)
        B, L = (2, 1024)
        x = jax.random.normal(ks[0], (B, L, D), dtype=jnp.float32)
        Wqkv = jax.random.normal(ks[1], (D, 3 * D), dtype=jnp.float32) * 0.02
        bqkv = jnp.zeros((3 * D,), dtype=jnp.float32)
        Wproj = jax.random.normal(ks[2], (D, D), dtype=jnp.float32) * 0.02
        bproj = jnp.zeros((D,), dtype=jnp.float32)
        gamma = jnp.float32(0.9)
        return {'x': x, 'Wqkv': Wqkv, 'bqkv': bqkv, 'Wproj': Wproj, 'bproj': bproj, 'gamma': gamma}
    _L1_attn_all = _L1_attn_setup()
    _L1_attn_in = {k: v for k, v in _L1_attn_all.items() if k in ('Wqkv', 'bqkv', 'Wproj', 'bproj', 'gamma')}
    del _L1_attn_all

    def _L1_xattn_setup():
        import jax, jax.numpy as jnp
        import numpy as np
        N_HEAD = 16
        key = jax.random.key(seed)
        ks = jax.random.split(key, 5)
        b, l, d = (4, 512, 256)
        dh = d // N_HEAD
        return {'q': jax.random.normal(ks[0], (b, l, d), dtype=jnp.float32), 'kv': jax.random.normal(ks[1], (b, l, d), dtype=jnp.float32), 'Wq': jax.random.normal(ks[2], (d, d), dtype=jnp.float32) * 0.02, 'Wkv': jax.random.normal(ks[3], (2 * dh, d), dtype=jnp.float32) * 0.02, 'Wc': jax.random.normal(ks[4], (d, d), dtype=jnp.float32) * 0.02}
    _L1_xattn_all = _L1_xattn_setup()
    _L1_xattn_in = {k: v for k, v in _L1_xattn_all.items() if k in ('Wq', 'Wkv', 'Wc')}
    del _L1_xattn_all

    def _L1_ffn_setup():
        import jax, jax.numpy as jnp
        import numpy as np
        B, S, D_MODEL, D_HIDDEN = (4, 512, 256, 1024)

        def act_quant(x):
            scale = 127.0 / jnp.clip(jnp.max(jnp.abs(x), axis=-1, keepdims=True), 1e-05)
            return jnp.clip(jnp.round(x * scale), -128, 127) / scale

        def weight_quant(w):
            scale = 1.0 / jnp.clip(jnp.mean(jnp.abs(w)), 1e-05)
            return jnp.clip(jnp.round(w * scale), -1, 1) / scale

        def bit_linear(x, w):
            xq = x + jax.lax.stop_gradient(act_quant(x) - x)
            wq = w + jax.lax.stop_gradient(weight_quant(w) - w)
            return jnp.einsum('bsd,hd->bsh', xq, wq)

        def depthwise_conv1d(x_bcl, w, b):
            y = jax.lax.conv_general_dilated(x_bcl, w, window_strides=(1,), padding=[(1, 1)], dimension_numbers=('NCH', 'OIH', 'NCH'), feature_group_count=x_bcl.shape[1])
            return y + b[None, :, None]
        key = jax.random.key(seed)
        ks = jax.random.split(key, 5)
        lim1 = 1.0 / np.sqrt(D_MODEL)
        lim2 = 1.0 / np.sqrt(D_HIDDEN)
        limc = 1.0 / np.sqrt(3.0)
        return {'x': jax.random.normal(ks[0], (B, S, D_MODEL), dtype=jnp.float32), 'w1': jax.random.uniform(ks[1], (D_HIDDEN, D_MODEL), jnp.float32, -lim1, lim1), 'conv_w': jax.random.uniform(ks[2], (D_HIDDEN, 1, 3), jnp.float32, -limc, limc), 'conv_b': jax.random.uniform(ks[3], (D_HIDDEN,), jnp.float32, -limc, limc), 'w2': jax.random.uniform(ks[4], (D_MODEL, D_HIDDEN), jnp.float32, -lim2, lim2)}
    _L1_ffn_all = _L1_ffn_setup()
    _L1_ffn_in = {k: v for k, v in _L1_ffn_all.items() if k in ('w1', 'conv_w', 'conv_b', 'w2')}
    del _L1_ffn_all
    return {'x': x, 'ctx_1024': ctx_1024, 'mask_SxS2_fk0': mask_SxS2_fk0, 'L0_attn_wq': _L0_attn_in['wq'], 'L0_attn_wk': _L0_attn_in['wk'], 'L0_attn_wv': _L0_attn_in['wv'], 'L0_attn_wo': _L0_attn_in['wo'], 'L0_attn_bo': _L0_attn_in['bo'], 'L0_attn_cw1': _L0_attn_in['cw1'], 'L0_attn_cb1': _L0_attn_in['cb1'], 'L0_attn_cw2': _L0_attn_in['cw2'], 'L0_attn_cb2': _L0_attn_in['cb2'], 'L0_attn_cw3': _L0_attn_in['cw3'], 'L0_attn_cb3': _L0_attn_in['cb3'], 'L0_xattn_Wq': _L0_xattn_in['Wq'], 'L0_xattn_Wk': _L0_xattn_in['Wk'], 'L0_xattn_Wv': _L0_xattn_in['Wv'], 'L0_xattn_bv': _L0_xattn_in['bv'], 'L0_ffn_Wr': _L0_ffn_in['Wr'], 'L0_ffn_Wqkv': _L0_ffn_in['Wqkv'], 'L0_ffn_Wo': _L0_ffn_in['Wo'], 'L1_attn_Wqkv': _L1_attn_in['Wqkv'], 'L1_attn_bqkv': _L1_attn_in['bqkv'], 'L1_attn_Wproj': _L1_attn_in['Wproj'], 'L1_attn_bproj': _L1_attn_in['bproj'], 'L1_attn_gamma': _L1_attn_in['gamma'], 'L1_xattn_Wq': _L1_xattn_in['Wq'], 'L1_xattn_Wkv': _L1_xattn_in['Wkv'], 'L1_xattn_Wc': _L1_xattn_in['Wc'], 'L1_ffn_w1': _L1_ffn_in['w1'], 'L1_ffn_conv_w': _L1_ffn_in['conv_w'], 'L1_ffn_conv_b': _L1_ffn_in['conv_b'], 'L1_ffn_w2': _L1_ffn_in['w2']}

def reference(x, ctx_1024, mask_SxS2_fk0, L0_attn_wq, L0_attn_wk, L0_attn_wv, L0_attn_wo, L0_attn_bo, L0_attn_cw1, L0_attn_cb1, L0_attn_cw2, L0_attn_cb2, L0_attn_cw3, L0_attn_cb3, L0_xattn_Wq, L0_xattn_Wk, L0_xattn_Wv, L0_xattn_bv, L0_ffn_Wr, L0_ffn_Wqkv, L0_ffn_Wo, L1_attn_Wqkv, L1_attn_bqkv, L1_attn_Wproj, L1_attn_bproj, L1_attn_gamma, L1_xattn_Wq, L1_xattn_Wkv, L1_xattn_Wc, L1_ffn_w1, L1_ffn_conv_w, L1_ffn_conv_b, L1_ffn_w2):
    import jax
    import jax.numpy as jnp

    def _L0_attn_ref(x, wq, wk, wv, wo, bo, cw1, cb1, cw2, cb2, cw3, cb3):
        import jax, jax.numpy as jnp
        import numpy as np
        D_MODEL = 256
        H = 16
        DH = D_MODEL // H
        WIN = 7
        PAD = WIN // 2
        B, L = (2, 1024)
        b, l, d = x.shape

        def heads(w):
            return (x @ w.T).reshape(b, l, H, DH).transpose(0, 2, 1, 3)
        Q, K, V = (heads(wq), heads(wk), heads(wv))
        Kp = jnp.pad(K, ((0, 0), (0, 0), (PAD, PAD), (0, 0)))
        Vp = jnp.pad(V, ((0, 0), (0, 0), (PAD, PAD), (0, 0)))
        idx = jnp.arange(l)[:, None] + jnp.arange(WIN)[None, :]
        Kw = Kp[:, :, idx]
        Vw = Vp[:, :, idx]
        scores = jnp.einsum('bhld,bhlwd->bhlw', Q, Kw) / np.float32(np.sqrt(DH))
        attn = jax.nn.softmax(scores, axis=-1)
        pos = jnp.linspace(0.0, 1.0, WIN, dtype=jnp.float32)[:, None]
        gelu = lambda z: jax.nn.gelu(z, approximate=False)
        h = gelu(jnp.einsum('wi,hji->hwj', pos, cw1) + cb1[:, None, :])
        h = gelu(jnp.einsum('hwi,hji->hwj', h, cw2) + cb2[:, None, :])
        cwt = (jnp.einsum('hwi,hji->hwj', h, cw3) + cb3[:, None, :])[..., 0]
        conn = jax.nn.softmax(cwt, axis=-1)[None, :, None, :]
        fw = attn * conn
        fw = fw / (fw.sum(axis=-1, keepdims=True) + 1e-09)
        out = jnp.einsum('bhlw,bhlwd->bhld', fw, Vw)
        out = out.transpose(0, 2, 1, 3).reshape(b, l, d)
        return out @ wo.T + bo

    def _L0_xattn_ref(q, k, v, attn_mask, Wq, Wk, Wv, bv):
        import jax, jax.numpy as jnp
        import numpy as np
        M = 256
        N = 256
        B, S = (4, 512)
        qp = jnp.einsum('bsm,nm->bsn', q, Wq)
        kp = jnp.einsum('bsm,nm->bsn', k, Wk)
        vp = jnp.einsum('bsn,on->bso', v, Wv) + bv
        scores = jnp.einsum('bqn,bkn->bqk', qp, kp) / jnp.sqrt(jnp.float32(N))
        scores = scores + attn_mask
        w = jax.nn.softmax(scores, axis=-1)
        return jnp.einsum('bqk,bkn->bqn', w, vp)

    def _L0_ffn_ref(X, Wr, Wqkv, Wo):
        import math
        import jax, jax.numpy as jnp
        import numpy as np
        E = 8
        H = 256
        HP = 128
        SPARSITY = 8
        N_ROTATE = 64
        ROPE_BASE = 10000.0

        def _rope(x, pos):
            half = N_ROTATE // 2
            inv_freq = 1.0 / ROPE_BASE ** (jnp.arange(half, dtype=jnp.float32) * 2.0 / N_ROTATE)
            ang = pos.astype(jnp.float32)[..., None] * inv_freq
            sin, cos = (jnp.sin(ang), jnp.cos(ang))
            x1, x2 = (x[..., :half], x[..., half:])
            return jnp.concatenate([x1 * cos - x2 * sin, x2 * cos + x1 * sin], axis=-1)
        B, T, _ = X.shape
        k = min(max(T // SPARSITY, 2), T)
        logits = jax.nn.sigmoid(jnp.einsum('bth,eh->bte', X, Wr))
        topk_vals, topk_I = jax.lax.top_k(logits.transpose(0, 2, 1), k)
        idx_flat = topk_I.reshape(B, E * k)
        Xg = jnp.take_along_axis(X, idx_flat[:, :, None], axis=1).reshape(B, E, k, H)
        QKV = jnp.einsum('beki,eij->bekj', Xg, Wqkv)
        Q, K, V = jnp.split(QKV, 3, axis=-1)
        Q = jnp.concatenate([_rope(Q[..., :N_ROTATE], topk_I), Q[..., N_ROTATE:]], axis=-1)
        K = jnp.concatenate([_rope(K[..., :N_ROTATE], topk_I), K[..., N_ROTATE:]], axis=-1)
        M = topk_I[..., :, None] >= topk_I[..., None, :]
        scores = jnp.einsum('bekd,bemd->bekm', Q, K) / math.sqrt(HP)
        scores = jnp.where(M, scores, -jnp.inf)
        A = jax.nn.softmax(scores, axis=-1)
        AV = jnp.einsum('bekm,bemd->bekd', A, V)
        AV = AV * topk_vals[..., None]
        Xpre = jnp.einsum('bekj,eji->beki', AV, Wo)
        out = jnp.zeros((B, T, H), dtype=X.dtype)
        out = out.at[jnp.arange(B)[:, None], idx_flat].add(Xpre.reshape(B, E * k, H))
        return out

    def _L1_attn_ref(x, Wqkv, bqkv, Wproj, bproj, gamma):
        import jax, jax.numpy as jnp
        import numpy as np
        import math
        D = 256
        W = 128

        def _decay_mask(L, gamma, dtype):
            i = jnp.arange(L)
            diff = i[:, None] - i[None, :]
            same_block = i[:, None] // W == i[None, :] // W
            safe_exp = jnp.maximum(diff, 0).astype(dtype)
            in_block = jnp.where(diff >= 0, gamma ** safe_exp, jnp.zeros((), dtype))
            return jnp.where(same_block, in_block, jnp.ones((), dtype))
        B, L, d = x.shape
        qkv = x @ Wqkv + bqkv
        q, k, v = jnp.split(qkv, 3, axis=-1)
        attn = jnp.einsum('bqd,bkd->bqk', q, k) / math.sqrt(d)
        mask = _decay_mask(L, gamma, x.dtype)
        attn = attn * mask[None, :, :]
        attn = jax.nn.softmax(attn, axis=-1)
        out = jnp.einsum('bqk,bkd->bqd', attn, v)
        return out @ Wproj + bproj

    def _L1_xattn_ref(q, kv, Wq, Wkv, Wc):
        import jax, jax.numpy as jnp
        import numpy as np
        N_HEAD = 16
        b, l, d = q.shape
        h = N_HEAD
        dh = d // h
        qp = jnp.einsum('bld,ed->ble', q, Wq)
        scores = jnp.einsum('bld,bmd->blm', qp, kv)
        idx = jnp.argmax(scores, axis=-1)
        mem = jnp.take_along_axis(kv, idx[..., None], axis=1)
        mkv = jnp.einsum('bld,ed->ble', mem, Wkv)
        mk, mv = jnp.split(mkv, 2, axis=-1)
        qh = qp.reshape(b, l, h, dh).transpose(0, 2, 1, 3)
        scale = 1.0 / np.sqrt(dh).astype(np.float32)
        logits = jnp.einsum('bhld,bmd->bhlm', qh, mk) * scale
        attn = jax.nn.softmax(logits, axis=-1)
        out = jnp.einsum('bhlm,bmd->bhld', attn, mv)
        out = out.transpose(0, 2, 1, 3).reshape(b, l, d)
        return jnp.einsum('bld,ed->ble', out, Wc)

    def _L1_ffn_ref(x, w1, conv_w, conv_b, w2):
        import jax, jax.numpy as jnp
        import numpy as np
        B, S, D_MODEL, D_HIDDEN = (4, 512, 256, 1024)

        def act_quant(x):
            scale = 127.0 / jnp.clip(jnp.max(jnp.abs(x), axis=-1, keepdims=True), 1e-05)
            return jnp.clip(jnp.round(x * scale), -128, 127) / scale

        def weight_quant(w):
            scale = 1.0 / jnp.clip(jnp.mean(jnp.abs(w)), 1e-05)
            return jnp.clip(jnp.round(w * scale), -1, 1) / scale

        def bit_linear(x, w):
            xq = x + jax.lax.stop_gradient(act_quant(x) - x)
            wq = w + jax.lax.stop_gradient(weight_quant(w) - w)
            return jnp.einsum('bsd,hd->bsh', xq, wq)

        def depthwise_conv1d(x_bcl, w, b):
            y = jax.lax.conv_general_dilated(x_bcl, w, window_strides=(1,), padding=[(1, 1)], dimension_numbers=('NCH', 'OIH', 'NCH'), feature_group_count=x_bcl.shape[1])
            return y + b[None, :, None]
        h = bit_linear(x, w1)
        h = depthwise_conv1d(h.transpose(0, 2, 1), conv_w, conv_b)
        h = h.transpose(0, 2, 1)
        h = jax.nn.silu(h)
        return bit_linear(h, w2)
    x = _layernorm(x + _L0_attn_ref(x, L0_attn_wq, L0_attn_wk, L0_attn_wv, L0_attn_wo, L0_attn_bo, L0_attn_cw1, L0_attn_cb1, L0_attn_cw2, L0_attn_cb2, L0_attn_cw3, L0_attn_cb3), axis=-1)
    x = _layernorm(x + _L0_xattn_ref(x, ctx_1024, ctx_1024, mask_SxS2_fk0, L0_xattn_Wq, L0_xattn_Wk, L0_xattn_Wv, L0_xattn_bv), axis=-1)
    x = _layernorm(x + _L0_ffn_ref(x, L0_ffn_Wr, L0_ffn_Wqkv, L0_ffn_Wo), axis=-1)
    x = _layernorm(x + _L1_attn_ref(x, L1_attn_Wqkv, L1_attn_bqkv, L1_attn_Wproj, L1_attn_bproj, L1_attn_gamma), axis=-1)
    x = _layernorm(x + _L1_xattn_ref(x, ctx_1024, L1_xattn_Wq, L1_xattn_Wkv, L1_xattn_Wc), axis=-1)
    x = _layernorm(x + _L1_ffn_ref(x, L1_ffn_w1, L1_ffn_conv_w, L1_ffn_conv_b, L1_ffn_w2), axis=-1)
    return x

_drawn_inputs = setup_inputs


def setup_inputs(seed=0):
    import zlib

    import numpy as np

    out = dict(_drawn_inputs(seed))
    spreads = {'mask_SxS2_fk0': (-1000000000.0, 0.2),
     'L1_attn_bqkv': (0.0, 0.1),
     'L1_attn_bproj': (0.0, 0.1)}
    factors = {'L0_attn_wq': 8.0,
     'L0_attn_wk': 8.0,
     'L0_attn_bo': 3.718,
     'L0_attn_cw1': 64.0,
     'L0_attn_cb1': 64.0,
     'L0_attn_cw2': 64.0,
     'L0_attn_cb2': 177.985,
     'L0_attn_cw3': 64.0,
     'L0_attn_cb3': 64.0}
    for name, (base, spread) in spreads.items():
        noise = np.random.default_rng([zlib.crc32(name.encode()), seed]).standard_normal(out[name].shape)
        drawn = base * np.exp(spread * noise) if base else spread * noise
        out[name] = jnp.asarray(drawn.astype(out[name].dtype))
    for name, factor in factors.items():
        out[name] = (out[name] * factor).astype(out[name].dtype)
    return out
```

```python
from contextlib import ExitStack

import numpy as np

import concourse.bass as bass
from concourse import mybir

F32 = mybir.dt.float32
BF16 = mybir.dt.bfloat16
U32 = mybir.dt.uint32
ALU = mybir.AluOpType
ACT = mybir.ActivationFunctionType
X = mybir.AxisListType.X

P = 128
D = 256
DC = D // P
NSEQ = 32
GB = 4
NG = NSEQ // GB
T = GB * P
H = 16
DH = D // H
HC = H // DC
WIN = 7
PAD = WIN // 2
NE = 8
NS = P // 8
HP = 128
ROT = 64
EJ = NE // 2
ES = GB * NS
HID = 1024
HJ = HID // P
CH = 32
EPS = 1e-5
MAGIC = 12582912.0
FAR = -1e30


class Mark:

    def __init__(self, sem, value):
        self.sem, self.value = sem, value


class Stream:

    def __init__(self, sem):
        self.sem, self.count, self.queue, self.seen = sem, 0, [], {}

    def wait(self, *marks):
        for mark in marks:
            if self.seen.get(mark.sem.name, 0) < mark.value:
                self.seen[mark.sem.name] = mark.value
                self.queue.append((None, (mark.sem, mark.value), {}, None))

    def put(self, builder, *args, after=(), mark=True, **kw):
        self.wait(*after)
        self.queue.append((builder, args, kw, (self.sem, 1) if mark else None))
        if mark:
            self.count += 1
            return Mark(self.sem, self.count)

    def play(self, engine):
        for builder, args, kw, inc in self.queue:
            if builder is None:
                engine.wait_ge(*args)
            else:
                instruction = builder(*args, **kw)
                if inc:
                    instruction.then_inc(*inc)


class Landing:

    def __init__(self, sem):
        self.sem, self.count = sem, 0

    def dma(self, stream, start, out, in_, after=()):
        stream.wait(*after)
        self.count += 16
        stream.queue.append((start, (out, in_), {}, (self.sem, 16)))
        return Mark(self.sem, self.count)


class Bank:
    def __init__(self, tensor):
        self.tensor, self.released = tensor, []


class Banks:

    def __init__(self, tensors):
        self.free = [Bank(t) for t in tensors]

    def take(self):
        return self.free.pop(0)

    def give(self, bank, *marks):
        bank.released = list(marks)
        self.free.append(bank)


class Area:

    def __init__(self, tensor, size):
        self.tensor, self.size, self.at = tensor, size, 0

    def reset(self):
        self.at = 0

    def carve(self, n):
        assert self.at + n <= self.size, (self.at, n, self.size)
        self.at += n
        return self.tensor[:, self.at - n:self.at]


def bc(ap, axis, n):
    v = ap.unsqueeze(axis)
    shape = list(v.shape)
    shape[axis] = n
    return v.broadcast_to(shape)


def build(nc, io, out):
    ctx = ExitStack()
    with ctx:
        def sb(name, shape, dt=F32):
            return ctx.enter_context(nc.sbuf_tensor(name, shape, dt))

        def sem(name):
            return ctx.enter_context(nc.semaphore(name))

        PE, DVE, SC, POOL, SP = (Stream(sem(f"{n}_done")) for n in ("pe", "dve", "act", "pool", "sp"))
        banks = Banks([ctx.enter_context(nc.psum_tensor(f"bank{i}", [P, 512], F32)) for i in range(8)])
        dve, act, pool, pe, sp = nc.vector, nc.scalar, nc.gpsimd, nc.tensor, nc.sync

        xs = [sb(f"x{i}", [P, GB, D]) for i in range(4)]
        areaA = Area(sb("areaA", [P, 9700]), 9700)
        areaB = Area(sb("areaB", [P, 8100]), 8100)
        areaC = Area(sb("areaC", [P, 11300]), 11300)
        w = {}
        for name, cols in (("wq0", DC * D), ("wk0", DC * D), ("wv0", DC * D), ("wo0", DC * D),
                           ("wv0x", DC * D), ("wqkv_e", DC * NE * 3 * HP), ("wo_e", NE * D),
                           ("wqkv1", DC * 3 * D), ("wp1", DC * D), ("wq1x", DC * D), ("wkrep", DC * P),
                           ("wv1x", DC * DH), ("wc1x", DC * D), ("rows", D), ("bqk", 4),
                           ("convw", HJ * 3), ("convb", HJ), ("xmask", P), ("ident", P), ("swap", ROT),
                           ("cos", ROT), ("sin", ROT), ("blk", ES), ("headsum", HC), ("parity", 2),
                           ("iota16", NS), ("iota128", P), ("pos", 1)):
            w[name] = sb("w_" + name, [P, cols])
        onesb = sb("onesb", [P, P])
        wr_pad = sb("wr_pad", [P, DC, 32])
        w_cross = sb("w_cross", [P, DC, D])
        conn = sb("conn", [P, WIN * H])
        decay = sb("decay", [P, P])
        w1q = sb("w1q", [P, DC, HID], BF16)
        w2q = sb("w2q", [P, HJ, D], BF16)
        wmean = sb("wmean", [P, 2])
        small = sb("small", [P, 64])
        halves = sb("halves", [P, 4])

        def chunked(name):
            return w[name][:, :].rearrange("p (c n) -> p c n", c=DC)

        s_w, s_wb, s_x = Landing(sem("weights_in")), Landing(sem("setup_in")), [Landing(sem(f"x_in{i}")) for i in range(4)]
        s_xt, s_ctxb, s_ctxc = Landing(sem("xt_in")), Landing(sem("ctx_b_in")), Landing(sem("ctx_c_in"))
        s_shift, s_out = [Landing(sem("shift_in0")), Landing(sem("shift_in1"))], Landing(sem("y_out"))

        ident = w["ident"]
        I = ident[:, :]

        def mm(bank_ap, pairs, after=(), mark=False):
            PE.wait(*after)
            n = len(pairs)
            for i, (l, r) in enumerate(pairs):
                m = PE.put(pe.matmul, bank_ap, l, r, start=i == 0, stop=i == n - 1, mark=mark and i == n - 1)
            return m

        def tp(out_ap, in_ap, after=(), mark=False, identity=None):
            return PE.put(pe.transpose, out_ap, in_ap, I if identity is None else identity, after=after, mark=mark)

        def take():
            bank = banks.take()
            PE.wait(*bank.released)
            return bank

        def setup():
            areaA.reset(), areaB.reset(), areaC.reset()
            order = ("ident", "headsum", "pos", "iota16", "iota128", "parity", "rows", "wq0", "wk0", "wv0", "wo0",
                     "xmask", "wv0x", "cos", "sin", "swap", "blk", "wqkv_e", "wo_e", "wqkv1", "bqk", "wp1",
                     "wq1x", "wkrep", "wv1x", "wc1x", "convw", "convb")
            m_zero = POOL.put(pool.memset, wr_pad[:, :, :], 0.0)
            m_ones = POOL.put(pool.memset, onesb[:, :], 1.0)
            m_half = POOL.put(pool.memset, halves[:, :], -0.5)
            raw_q, raw_k = areaB.carve(DC * D), areaB.carve(DC * D)
            c1, b1, c2, b2, c3, b3, gam = (areaB.carve(n) for n in (CH, CH, CH * CH, CH, CH, 1, 1))
            bits = areaB.carve(15 * P)
            raw1, raw2 = areaC.carve(DC * HID), areaC.carve(HJ * D)
            tmp = areaC.carve(DC * HID)
            cw = areaA.carve(CH * CH)
            h1, h2, cwt, s1, s2 = (areaA.carve(n) for n in (CH, CH, 1, 1, 1))
            n112 = WIN * H
            for dst, src in ((raw_q, "raw_q"), (raw_k, "raw_k"), (c1[0:n112], "c1"), (b1[0:n112], "b1"),
                             (c2[0:n112], "c2"), (b2[0:n112], "b2"), (c3[0:n112], "c3"), (b3[0:n112], "b3"),
                             (gam, "gamma"), (bits, "bits"), (raw1, "raw1"), (raw2, "raw2")):
                m_setup = s_wb.dma(SP, sp.dma_start, dst, io[src])
            m_setup = s_wb.dma(SP, sp.dma_start, wr_pad[:, :, 0:NE], io["wr"].rearrange("p (c n) -> p c n", c=DC),
                               after=(m_zero,))
            for name in order:
                m_w = s_w.dma(SP, sp.dma_start, w[name][:, :], io[name])

            DVE.wait(m_setup, m_w)
            m = DVE.put(dve.scalar_tensor_tensor, h1[0:n112], c1[0:n112], w["pos"][0:n112, 0:1], b1[0:n112], ALU.mult, ALU.add)
            SC.wait(m)
            m = SC.put(act.activation, h1[0:n112], h1[0:n112], ACT.Gelu)
            DVE.wait(m)
            m = DVE.put(dve.tensor_tensor, cw[0:n112].rearrange("p (j i) -> p j i", i=CH),
                        c2[0:n112].rearrange("p (j i) -> p j i", i=CH), bc(h1[0:n112], 1, CH), ALU.mult)
            DVE.wait(m)
            m = DVE.put(dve.tensor_reduce, h2[0:n112], cw[0:n112].rearrange("p (j i) -> p j i", i=CH), X, ALU.add)
            DVE.wait(m)
            m = DVE.put(dve.tensor_tensor, h2[0:n112], h2[0:n112], b2[0:n112], ALU.add)
            SC.wait(m)
            m = SC.put(act.activation, h2[0:n112], h2[0:n112], ACT.Gelu)
            DVE.wait(m)
            m = DVE.put(dve.tensor_tensor, h1[0:n112], h2[0:n112], c3[0:n112], ALU.mult)
            DVE.wait(m)
            m = DVE.put(dve.tensor_reduce, s1[0:n112], h1[0:n112], X, ALU.add)
            DVE.wait(m)
            m = DVE.put(dve.tensor_tensor, cwt[0:n112], s1[0:n112], b3[0:n112], ALU.add)
            DVE.wait(m)
            diag = areaA.carve(n112)
            m = DVE.put(dve.tensor_scalar, diag[0:n112], I[0:n112, 0:n112], cwt[0:n112, 0:1], None, ALU.mult)
            bank = take()
            m = mm(bank.tensor[:, 0:n112], [(onesb[0:n112, :], diag[0:n112])], after=(m, m_ones), mark=True)
            DVE.wait(m)
            m = DVE.put(dve.tensor_copy, conn[:, :], bank.tensor[:, 0:n112])
            banks.give(bank, m)
            mx, den = areaA.carve(H), areaA.carve(H)
            by_head = conn[:, :].rearrange("p (w h) -> p h w", h=H)
            conn3 = conn[:, :].rearrange("p (w h) -> p w h", h=H)
            DVE.wait(m)
            m = DVE.put(dve.tensor_reduce, mx, by_head, X, ALU.max)
            DVE.wait(m)
            m = DVE.put(dve.tensor_tensor, conn3, conn3, bc(mx, 1, WIN), ALU.subtract)
            SC.wait(m)
            m = SC.put(act.activation, conn[:, :], conn[:, :], ACT.Exp)
            DVE.wait(m)
            m = DVE.put(dve.tensor_reduce, den, by_head, X, ALU.add)
            DVE.wait(m)
            m = DVE.put(dve.reciprocal, den, den)
            DVE.wait(m)
            m = DVE.put(dve.tensor_tensor, conn3, conn3, bc(den, 1, WIN), ALU.mult)

            powers = areaA.carve(7)
            fac = areaA.carve(P)
            m = DVE.put(dve.tensor_copy, powers[:, 0:1], gam)
            for i in range(1, 7):
                DVE.wait(m)
                m = DVE.put(dve.tensor_tensor, powers[:, i:i + 1], powers[:, i - 1:i], powers[:, i - 1:i], ALU.mult)
            DVE.wait(m)
            m = DVE.put(dve.tensor_scalar, decay[:, :], bits[:, 14 * P:15 * P], 1.0 / np.sqrt(D).item(), None, ALU.mult)
            for i in range(7):
                m2 = DVE.put(dve.scalar_tensor_tensor, fac, bits[:, i * P:(i + 1) * P], powers[:, i:i + 1],
                             bits[:, (7 + i) * P:(8 + i) * P], ALU.mult, ALU.add, after=(m,))
                m = DVE.put(dve.tensor_tensor, decay[:, :], decay[:, :], fac, ALU.mult, after=(m2,))

            PE.wait(m_setup, m_w)
            for c in range(DC):
                bank = take()
                m = mm(bank.tensor[:, 0:D], [(raw_k[:, n * D + c * P:n * D + (c + 1) * P], raw_q[:, n * D:(n + 1) * D])
                                             for n in range(DC)], mark=True)
                m = SC.put(act.activation, w_cross[:, c, :], bank.tensor[:, 0:D], ACT.Copy, after=(m,))
                banks.give(bank, m)

            for i, (raw, q) in enumerate(((raw1, w1q[:, :, :].rearrange("p c n -> p (c n)")),
                                          (raw2, w2q[:, :, :].rearrange("p c n -> p (c n)")))):
                m = DVE.put(dve.tensor_reduce, small[:, i:i + 1], raw, X, ALU.add, apply_absolute_value=True)
                bank = take()
                m = mm(bank.tensor[:, 0:1], [(onesb[:, :], small[:, i:i + 1])], after=(m,), mark=True)
                m = DVE.put(dve.tensor_scalar, wmean[:, i:i + 1], bank.tensor[:, 0:1], 1.0 / (HID * D), 1e-5,
                            ALU.mult, ALU.max, after=(m,))
                banks.give(bank, m)
                m = DVE.put(dve.reciprocal, small[:, 2 + i:3 + i], wmean[:, i:i + 1], after=(m,))
                m = DVE.put(dve.tensor_scalar, tmp, raw, small[:, 2 + i:3 + i], MAGIC, ALU.mult, ALU.add, after=(m,))
                m = DVE.put(dve.tensor_scalar, tmp, tmp, MAGIC, 1.0, ALU.subtract, ALU.min, after=(m,))
                m = DVE.put(dve.tensor_scalar, q, tmp, -1.0, None, ALU.max, after=(m,))
            for s in (PE, SC, POOL, SP):
                s.wait(m)
            PE.wait(m_half)
            POOL.wait(m_half, m_w)
            SC.wait(m_w)

        def to_channels(x, ready, xT):
            marks = []
            for c in range(DC):
                bank = take()
                for b in range(GB):
                    m = tp(bank.tensor[:, b * P:(b + 1) * P], x[:, b, c * P:(c + 1) * P], after=(ready[b],),
                           mark=b == GB - 1)
                m = SC.put(act.activation, xT[:, c, :], bank.tensor[:, :], ACT.Copy, after=(m,))
                banks.give(bank, m)
                marks.append(m)
                yield
            return marks

        def norm(x, pairs, scale=None, after_scale=()):
            stats, mv, nmr = norm_bufs
            DVE.wait(*after_scale)
            added = []
            for i, (bank, m) in enumerate(pairs):
                rows = bank.tensor[:, :].rearrange("p (b d) -> p b d", d=D)
                DVE.wait(m)
                if scale is None:
                    m = DVE.put(dve.tensor_tensor, x[:, 2 * i:2 * i + 2, :], rows, x[:, 2 * i:2 * i + 2, :], ALU.add)
                    added += [m, m]
                else:
                    for b in (2 * i, 2 * i + 1):
                        m = DVE.put(dve.scalar_tensor_tensor, x[:, b, :], rows[:, b - 2 * i, :], scale[:, b:b + 1],
                                    x[:, b, :], ALU.mult, ALU.add)
                        added.append(m)
                banks.give(bank, m)
            yield
            slot = norm_slot[0] % NORM_SLOTS
            norm_slot[0] += 1
            st, agg, sc = stats[:, slot], mv[:, slot], nmr[:, slot]
            DVE.wait(*norm_free[slot])
            for b in range(GB):
                m_st = DVE.put(dve.bn_stats, st[:, b, :], x[:, b, :], after=(added[b],))
            DVE.wait(m_st)
            for b in range(GB):
                m = DVE.put(dve.bn_aggr, agg[:, b, :], st[:, b, :])
            yield
            rstd, shift = sc[:, 0, :], sc[:, 1, :]
            POOL.wait(m)
            m1 = POOL.put(pool.tensor_scalar, rstd, agg[:, :, 1], 1.0, EPS, ALU.mult, ALU.add)
            m2 = POOL.put(pool.tensor_scalar, shift, agg[:, :, 0], -1.0, 0.0, ALU.mult, ALU.add)
            m1 = POOL.put(pool.tensor_tensor, rstd, rstd, halves[:, :], ALU.pow, after=(m1, m2))
            m2 = POOL.put(pool.tensor_tensor, shift, shift, rstd, ALU.mult, after=(m1,))
            POOL.wait(m2)
            done = []
            for b in range(GB):
                done.append(POOL.put(pool.tensor_scalar, x[:, b, :], x[:, b, :], rstd[:, b:b + 1], shift[:, b:b + 1],
                                     ALU.mult, ALU.add))
            norm_free[slot] = [done[-1]]
            yield
            return done

        NORM_SLOTS = 4
        norm_bufs = (sb("bn_parts", [P, NORM_SLOTS, GB, 6]), sb("bn_mv", [P, NORM_SLOTS, GB, 2]),
                     sb("bn_scale", [P, NORM_SLOTS, 2, GB]))
        norm_slot, norm_free = [0], [[] for _ in range(NORM_SLOTS)]

        def project(weights, col, actT, ready):
            pairs = []
            PE.wait(*ready)
            for m in range(DC):
                bank = take()
                mk = mm(bank.tensor[:, :], [(weights[:, c, col + m * P:col + (m + 1) * P], actT[:, c, :])
                                            for c in range(DC)], mark=True)
                pairs.append((bank, mk))
            return pairs

        ones_row = {0: onesb[0:1, :], 32: onesb[32:33, :], 64: onesb[64:65, :], 96: onesb[96:97, :]}

        def project_rows(weights, col, actT, ready, bias=None):
            pairs = []
            PE.wait(*ready)
            for h in range(GB // 2):
                bank = take()
                for b in (2 * h, 2 * h + 1):
                    terms = [(actT[:, c, b * P:(b + 1) * P], weights[:, c, col:col + D]) for c in range(DC)]
                    if bias is not None:
                        terms.append((ones_row[bias], w["rows"][bias:bias + 1, :]))
                    mk = mm(bank.tensor[:, (b - 2 * h) * D:(b - 2 * h + 1) * D], terms, mark=b % 2 == 1)
                pairs.append((bank, mk))
            return pairs

        def key_softmax(s, ready, scale, sums, negmax):
            n = s.shape[1]
            m = DVE.put(dve.tensor_reduce, negmax, s, X, ALU.max, negate=True, after=ready)
            if scale != 1.0:
                m = DVE.put(dve.tensor_scalar, negmax, negmax, scale, None, ALU.mult, after=(m,))
            SC.wait(m)
            yield
            for j in range(n):
                m = SC.put(act.activation, s[:, j, :], s[:, j, :], ACT.Exp, bias=negmax[:, j:j + 1], scale=scale,
                           accum_out=sums[:, j:j + 1])
            return m

        def windowed(g, x, x_ready, free):
            areaA.reset()
            xT = areaA.carve(DC * T).rearrange("p (c t) -> p c t", c=DC)
            qT = areaA.carve(DC * T).rearrange("p (c t) -> p c t", c=DC)
            LP = P + 2 * PAD
            kT = areaA.carve(DC * GB * LP).rearrange("p (c b t) -> p c b t", c=DC, b=GB)
            prods = [areaA.carve(T) for _ in range(4)]
            vw = areaA.carve(WIN * 2 * D).rearrange("p (w b d) -> p w b d", w=WIN, b=2)
            e = areaA.carve(GB * WIN * H)
            den = areaA.carve(3 * GB * H).rearrange("p (k n) -> p k n", k=3)
            if g == 0:
                POOL.put(pool.memset, vw, 0.0)
                zeroed = POOL.put(pool.memset, kT, 0.0)
                kv_zero.append(zeroed)
            m_xt = s_xt.dma(SP, sp.dma_start, xT, io["xT"][g].rearrange("p (c t) -> p c t", c=DC), after=free)
            q = project(chunked("wq0"), 0, xT, (m_xt,))
            SC.wait(*free)
            for c, (bank, m) in enumerate(q):
                m_q = SC.put(act.activation, qT[:, c, :], bank.tensor[:, :], ACT.Copy, after=(m,))
                banks.give(bank, m_q)
            yield
            k = project(chunked("wk0"), 0, xT, ())
            for c, (bank, m) in enumerate(k):
                m_k = SC.put(act.activation, kT[:, c, :, PAD:PAD + P],
                             bank.tensor[:, :].rearrange("p (b t) -> p b t", b=GB), ACT.Copy, after=(m, kv_zero[0]))
                banks.give(bank, m_k)
            yield
            sbank = take()
            scores = sbank.tensor[:, 0:GB * WIN * H].rearrange("p (b w h) -> p b w h", b=GB, w=WIN)
            prod_free = [list(free) for _ in prods]
            n = 0
            for c in range(DC):
                for wi in range(WIN):
                    r = n % 4
                    stream, eng = (POOL, pool) if n % 7 in POOL_SCORES else (DVE, dve)
                    m = stream.put(eng.tensor_tensor, prods[r].rearrange("p (b t) -> p b t", b=GB),
                                   qT[:, c, :].rearrange("p (b t) -> p b t", b=GB), kT[:, c, :, wi:wi + P], ALU.mult,
                                   after=(m_q, m_k, *prod_free[r]))
                    PE.wait(m)
                    for b in range(GB):
                        m = mm(scores[:, b, wi, c * HC:(c + 1) * HC],
                               [(prods[r][:, b * P:(b + 1) * P], w["headsum"][:, :])], mark=b == GB - 1)
                    prod_free[r] = [m]
                    n += 1
                    if n % 3 == 0:
                        yield
            m_scores = m
            s4 = scores.rearrange("p b w h -> p b h w")
            e4 = e.rearrange("p (b w h) -> p b w h", b=GB, w=WIN)
            mx, den1, den2 = (den[:, i, :].rearrange("p (b h) -> p b h", b=GB) for i in range(3))
            m = DVE.put(dve.tensor_reduce, mx, s4, X, ALU.max, after=(m_scores,))
            m = DVE.put(dve.tensor_tensor, e4, scores, bc(mx, 2, WIN), ALU.subtract, after=(m,))
            banks.give(sbank, m)
            yield
            m = SC.put(act.activation, e, e, ACT.Exp, scale=float(DH) ** -0.5, after=(m,))
            m = DVE.put(dve.tensor_reduce, den1, e4.rearrange("p b w h -> p b h w"), X, ALU.add, after=(m,))
            m = DVE.put(dve.tensor_tensor, e.rearrange("p (b n) -> p b n", b=GB), e.rearrange("p (b n) -> p b n", b=GB),
                        bc(conn[:, :], 1, GB), ALU.mult, after=(m,))
            m = DVE.put(dve.tensor_reduce, den2, e4.rearrange("p b w h -> p b h w"), X, ALU.add, after=(m,))
            m = DVE.put(dve.scalar_tensor_tensor, den[:, 0, :], den[:, 1, :], 1e-9, den[:, 2, :], ALU.mult, ALU.add, after=(m,))
            m = DVE.put(dve.reciprocal, den[:, 0, :], den[:, 0, :], after=(m,))
            m_fw = DVE.put(dve.tensor_tensor, e4, e4, bc(mx, 2, WIN), ALU.mult, after=(m,))
            yield
            acc = qT.rearrange("p c t -> p (c t)").rearrange("p (b d) -> p b d", b=GB)
            ring = [prods[0], prods[1]]
            pacc, ptmp = prods[2], prods[3]
            vfree = [list(free), None]
            done = []
            for hf in range(2):
                bank = take()
                for b in (2 * hf, 2 * hf + 1):
                    m = mm(bank.tensor[:, (b % 2) * D:(b % 2 + 1) * D],
                           [(xT[:, c, b * P:(b + 1) * P], chunked("wv0")[:, c, :]) for c in range(DC)], mark=b % 2 == 1)
                m_v = SC.put(act.activation, vw[:, PAD, :, :], bank.tensor[:, :].rearrange("p (b d) -> p b d", b=2),
                             ACT.Copy, after=(m, kv_zero[0], *vfree[hf]))
                banks.give(bank, m_v)
                for wi in range(WIN):
                    o = wi - PAD
                    if o:
                        lo, hi = max(0, -o), P - max(0, o)
                        m_sh = s_shift[hf].dma(SP, sp.dma_start, vw[lo:hi, wi, :, :], vw[lo + o:hi + o, PAD, :, :],
                                               after=(m_v, *vfree[hf]))
                yield
                yield
                def weigh(stream, eng, dst, wi, after):
                    f = e4[:, 2 * hf:2 * hf + 2, wi, :]
                    return stream.put(eng.tensor_tensor, dst.rearrange("p (b h d) -> p b h d", b=2, h=H),
                                      vw[:, wi, :, :].rearrange("p b (h d) -> p b h d", h=H),
                                      bc(f, 3, DH), ALU.mult, after=after)
                POOL.wait(m_fw, m_v, m_sh)
                mp = weigh(POOL, pool, pacc, 0, ())
                mp2 = weigh(POOL, pool, ptmp, 1, ())
                m_pool = POOL.put(pool.tensor_tensor, pacc, pacc, ptmp, ALU.add, after=(mp, mp2))
                a2 = acc[:, 2 * hf:2 * hf + 2, :].rearrange("p b d -> p (b d)")
                DVE.wait(m_fw, m_v)
                m = weigh(DVE, dve, a2, PAD, ())
                DVE.wait(m_sh)
                for i, wi in enumerate((2, 4, 5, 6)):
                    m1 = weigh(DVE, dve, ring[i % 2], wi, ())
                    m = DVE.put(dve.tensor_tensor, a2, a2, ring[i % 2], ALU.add, after=(m, m1))
                    yield
                m = DVE.put(dve.tensor_tensor, a2, a2, pacc, ALU.add, after=(m, m_pool))
                vfree[1] = [m]
                done.append(m)
                POOL.wait(m)
                yield
            aT = xT
            m_a = yield from to_channels(acc, [done[0], done[0], done[1], done[1]], aT)
            y = project_rows(chunked("wo0"), 0, aT, m_a, bias=0)
            yield
            return (yield from norm(x, y))

        kv_zero = []
        POOL_SCORES = (3, 6)

        def cross(g, x, ready, free):
            areaB.reset()
            xT, ctxT, ka, v = (areaB.carve(DC * T) for _ in range(4))
            xT, ctxT, ka = (t.rearrange("p (c t) -> p c t", c=DC) for t in (xT, ctxT, ka))
            v = v.rearrange("p (b d) -> p b d", b=GB)
            s, pT = areaB.carve(T), areaB.carve(T)
            sums, negmax, rec = areaB.carve(GB), areaB.carve(GB), areaB.carve(GB)
            m_c = s_ctxb.dma(SP, sp.dma_start, ctxT, io["ctxT"][g].rearrange("p (c t) -> p c t", c=DC), after=free)
            SC.wait(*free)
            DVE.wait(*free)
            k = project(w_cross, 0, ctxT, (m_c,))
            for c, (bank, m) in enumerate(k):
                m_ka = SC.put(act.activation, ka[:, c, :], bank.tensor[:, :], ACT.Copy, after=(m,))
                banks.give(bank, m_ka)
            yield
            vb = project_rows(chunked("wv0x"), 0, ctxT, (), bias=32)
            for i, (bank, m) in enumerate(vb):
                m_v = SC.put(act.activation, v[:, 2 * i:2 * i + 2, :], bank.tensor[:, :].rearrange("p (b d) -> p b d", b=2),
                             ACT.Copy, after=(m,))
                banks.give(bank, m_v)
            yield
            m_x = yield from to_channels(x, ready, xT)
            bank = take()
            PE.wait(*m_x, m_ka)
            for b in range(GB):
                m = mm(bank.tensor[:, b * P:(b + 1) * P], [(xT[:, c, b * P:(b + 1) * P], ka[:, c, b * P:(b + 1) * P])
                                                            for c in range(DC)], mark=b == GB - 1)
            s3 = s.rearrange("p (b k) -> p b k", b=GB)
            yield
            m = DVE.put(dve.scalar_tensor_tensor, s3, bank.tensor[:, :].rearrange("p (b k) -> p b k", b=GB),
                        float(D) ** -0.5, bc(w["xmask"][:, :], 1, GB), ALU.mult, ALU.add, after=(m,))
            banks.give(bank, m)
            m_e = yield from key_softmax(s3, (m,), 1.0, sums, negmax)
            yield
            m_r = DVE.put(dve.reciprocal, rec, sums, after=(m_e,))
            bank = take()
            for b in range(GB):
                m = tp(bank.tensor[:, b * P:(b + 1) * P], s3[:, b, :], after=(m_e,), mark=b == GB - 1)
            m = SC.put(act.activation, pT, bank.tensor[:, :], ACT.Copy, after=(m,))
            banks.give(bank, m)
            yield
            PE.wait(m, m_v)
            pairs = []
            for h in range(2):
                bank = take()
                for b in (2 * h, 2 * h + 1):
                    m = mm(bank.tensor[:, (b % 2) * D:(b % 2 + 1) * D], [(pT[:, b * P:(b + 1) * P], v[:, b, :])], mark=b % 2 == 1)
                pairs.append((bank, m))
            yield
            return (yield from norm(x, pairs, rec, (m_r,)))

        def experts(g, x, ready):
            areaB.reset()
            xT_ = areaB.carve(DC * T)
            xT = xT_.rearrange("p (c t) -> p c t", c=DC)
            pick, picked = areaB.carve(GB * P), areaB.carve(GB * P)
            cs = areaB.carve(2 * T)
            qk = areaB.carve(2 * T)
            t1, v, s, pT, pickT = areaB.carve(T), areaB.carve(T), areaB.carve(2 * P), areaB.carve(2 * P), areaB.carve(T)
            sig, r1, r2 = areaB.carve(P), areaB.carve(P), areaB.carve(P)
            m8 = areaB.carve(16)
            sums, negmax, rec = areaB.carve(EJ), areaB.carve(EJ), areaB.carve(EJ)
            sigt = areaB.carve(GB * NE)
            m_x = yield from to_channels(x, ready, xT)
            bank = take()
            PE.wait(*m_x)
            for b in range(GB):
                m = mm(bank.tensor[32 * b:32 * b + 32, 0:P], [(wr_pad[:, c, :], xT[:, c, b * P:(b + 1) * P]) for c in range(DC)],
                       mark=b == GB - 1)
            yield
            m = SC.put(act.activation, sig, bank.tensor[:, 0:P], ACT.Exp, scale=-1.0, after=(m,))
            banks.give(bank, m)
            m = DVE.put(dve.tensor_scalar, sig, sig, 1.0, None, ALU.add, after=(m,))
            m_sig = DVE.put(dve.reciprocal, sig, sig, after=(m,))
            m = DVE.put(dve.max, m8[:, 0:8], sig, after=(m_sig,))
            m = DVE.put(dve.match_replace, r1, m8[:, 0:8], sig, -1.0, after=(m,))
            m = DVE.put(dve.max, m8[:, 8:16], r1, after=(m,))
            m = DVE.put(dve.match_replace, r2, m8[:, 8:16], r1, -1.0, after=(m,))
            m = DVE.put(dve.tensor_scalar, r1, r2, 0.0, None, ALU.is_lt, after=(m,))
            m = DVE.put(dve.tensor_tensor_scan, r2, onesb[:, :], r1, 0.0, ALU.mult, ALU.add, after=(m,))
            m = DVE.put(dve.tensor_tensor, r2, r2, r1, ALU.mult, after=(m,))
            yield
            bank = take()
            tp(bank.tensor[:, 0:P], r2, after=(m,))
            m = tp(bank.tensor[:, P:2 * P], sig, after=(m_sig,), mark=True)
            rank4 = bank.tensor[:, 0:P].rearrange("p (b e) -> p b e", b=GB)[:, :, 0:NE]
            sig4 = bank.tensor[:, P:2 * P].rearrange("p (b e) -> p b e", b=GB)[:, :, 0:NE]
            pick4 = pick.rearrange("p (b e s) -> p b e s", b=GB, e=NE)
            picked4 = picked.rearrange("p (b e s) -> p b e s", b=GB, e=NE)
            DVE.wait(m)
            iota = bc(bc(w["iota16"][:, :], 1, NE), 1, GB)
            m_sg = DVE.put(dve.tensor_copy, sigt.rearrange("p (b e) -> p b e", b=GB), sig4)
            m_pick = DVE.put(dve.tensor_tensor, pick4, bc(rank4, 3, NS), iota, ALU.is_equal)
            banks.give(bank, m_pick)
            m_picked = POOL.put(pool.tensor_tensor, picked4, pick4, bc(sigt.rearrange("p (b e) -> p b e", b=GB), 3, NS),
                                ALU.mult, after=(m_pick, m_sg))
            yield
            xg = xT_.rearrange("p (c e b s) -> p c e b s", c=DC, e=NE, b=GB)
            PE.wait(m_pick)
            for c in range(DC):
                bank = take()
                for b in range(GB):
                    m = mm(bank.tensor[:, b * P:(b + 1) * P], [(x[:, b, c * P:(c + 1) * P], pick[:, b * P:(b + 1) * P])],
                           mark=b == GB - 1)
                src = bank.tensor[:, :].rearrange("p (b e s) -> p e b s", b=GB, e=NE)
                m_xg = SC.put(act.activation, xg[:, c], src, ACT.Copy, after=(m,))
                banks.give(bank, m_xg)
            yield
            for i, name in enumerate(("cos", "sin")):
                bank = take()
                m = mm(bank.tensor[0:ROT, :], [(w[name][:, :], pick)], mark=True)
                src = bank.tensor[0:ROT, :].rearrange("p (b e s) -> p e b s", b=GB, e=NE)
                m_cs = SC.put(act.activation, cs[0:ROT, i * T:(i + 1) * T].rearrange("p (e b s) -> p e b s", b=GB, e=NE),
                              src, ACT.Copy, after=(m,))
                banks.give(bank, m_cs)
            yield
            wq = w["wqkv_e"][:, :].rearrange("p (c e n) -> p c e n", c=DC, e=NE)
            xgf = xT_.rearrange("p (c e n) -> p c e n", c=DC, e=NE)
            PE.wait(m_xg)
            m_qk = []
            for i in range(2):
                bank = take()
                for e in range(NE):
                    m = mm(bank.tensor[:, e * ES:(e + 1) * ES], [(wq[:, c, e, i * HP:(i + 1) * HP], xgf[:, c, e, :])
                                                                  for c in range(DC)], mark=e == NE - 1)
                m = SC.put(act.activation, qk[:, i * T:(i + 1) * T], bank.tensor[:, :], ACT.Copy, after=(m,))
                m_qk.append(m)
                banks.give(bank, m)
                yield
            bank = take()
            vb = bank.tensor[:, :].rearrange("p (jj par d) -> p jj par d", jj=2, par=2)
            for half in range(2):
                for e in range(NE):
                    j, par = e // 2, e % 2
                    if j % 2 == half:
                        m = mm(vb[64 * half:64 * half + 64, j // 2, par, :],
                               [(xgf[:, c, e, :], wq[:, c, e, 2 * HP:3 * HP]) for c in range(DC)], mark=True)
            m_v = SC.put(act.activation, v, bank.tensor[:, :], ACT.Copy, after=(m,))
            banks.give(bank, m_v)
            yield
            m_rot = []
            for i in range(2):
                a = qk[0:ROT, i * T:(i + 1) * T]
                bank = take()
                m = mm(bank.tensor[0:ROT, :], [(w["swap"][0:ROT, :], a)], after=(m_qk[i],), mark=True)
                m1 = DVE.put(dve.tensor_tensor, t1[0:ROT], bank.tensor[0:ROT, :], cs[0:ROT, T:2 * T], ALU.mult,
                             after=(m, m_cs))
                banks.give(bank, m1)
                m2 = POOL.put(pool.tensor_tensor, a, a, cs[0:ROT, 0:T], ALU.mult, after=(m, m_cs))
                m = DVE.put(dve.tensor_tensor, a, a, t1[0:ROT], ALU.add, after=(m1, m2))
                DVE.wait(m)
                m_rot.append(m)
                yield
            bank = take()
            PE.wait(*m_rot)
            for par in range(2):
                for j in range(EJ):
                    e = 2 * j + par
                    m = mm(bank.tensor[64 * par:64 * par + 64, j * ES:(j + 1) * ES],
                           [(qk[:, e * ES:(e + 1) * ES], qk[:, T + e * ES:T + (e + 1) * ES])], mark=True)
            s3 = s.rearrange("p (j k) -> p j k", j=EJ)
            yield
            m = DVE.put(dve.scalar_tensor_tensor, s3, bank.tensor[:, 0:EJ * ES].rearrange("p (j k) -> p j k", j=EJ),
                        float(HP) ** -0.5, bc(w["blk"][:, :], 1, EJ), ALU.mult, ALU.add, after=(m,))
            banks.give(bank, m)
            m_e = yield from key_softmax(s3, (m,), 1.0, sums, negmax)
            yield
            m = DVE.put(dve.reciprocal, rec, sums, after=(m_e,))
            m = DVE.put(dve.tensor_tensor, s3, s3, bc(rec, 2, ES), ALU.mult, after=(m,))
            bank = take()
            for jj in range(2):
                mt = tp(bank.tensor[:, jj * P:(jj + 1) * P], s[:, jj * P:(jj + 1) * P], after=(m,), mark=jj == 1)
            m = SC.put(act.activation, pT, bank.tensor[:, 0:2 * P], ACT.Copy, after=(mt,))
            banks.give(bank, m)
            yield
            pT4 = pT.rearrange("p (jj par q) -> p jj par q", jj=2, par=2)
            v4 = v.rearrange("p (jj par d) -> p jj par d", jj=2, par=2)
            av_banks = []
            PE.wait(m, m_v)
            av = t1
            for half in range(2):
                bank = take()
                for jj in range(2):
                    for par in range(2):
                        o = (jj * 2 + par) * ES
                        r = slice(64 * half, 64 * half + 64)
                        m = mm(bank.tensor[:, o:o + ES], [(v4[r, jj, par, :], pT4[r, jj, par, :])], mark=jj + par == 2)
                dst = av.rearrange("p (jj h par n) -> p h jj par n", jj=2, h=2, par=2)[:, half]
                m_av = SC.put(act.activation, dst, bank.tensor[:, 0:EJ * ES].rearrange("p (jj par n) -> p jj par n", jj=2, par=2),
                              ACT.Copy, after=(m,))
                banks.give(bank, m_av)
            yield
            wo = w["wo_e"][:, :].rearrange("p (e n) -> p e n", e=NE)
            PE.wait(m_av)
            upT = xT_.rearrange("p (c b e s) -> p c b e s", c=DC, e=NE, b=GB)
            for c in range(DC):
                bank = take()
                for e in range(NE):
                    m = mm(bank.tensor[:, e * ES:(e + 1) * ES], [(wo[:, e, c * P:(c + 1) * P], av[:, e * ES:(e + 1) * ES])],
                           mark=e == NE - 1)
                src = bank.tensor[:, :].rearrange("p (e b s) -> p b e s", b=GB, e=NE)
                m_up = SC.put(act.activation, upT[:, c], src, ACT.Copy, after=(m,))
                banks.give(bank, m_up)
                yield
            bank = take()
            for b in range(GB):
                m = tp(bank.tensor[:, b * P:(b + 1) * P], picked[:, b * P:(b + 1) * P], after=(m_picked,), mark=b == GB - 1)
            m_pt = DVE.put(dve.tensor_copy, pickT, bank.tensor[:, :], after=(m,))
            banks.give(bank, m_pt)
            upf = xT_.rearrange("p (c n) -> p c n", c=DC)
            up = cs
            for h in range(2):
                bank = take()
                for b in (2 * h, 2 * h + 1):
                    for c in range(DC):
                        o = (b % 2) * D + c * P
                        m = tp(bank.tensor[:, o:o + P], upf[:, c, b * P:(b + 1) * P], after=(m_up,), mark=b % 2 + c == 2)
                m_u = SC.put(act.activation, up[:, h * T:(h + 1) * T], bank.tensor[:, :], ACT.Copy, after=(m,))
                banks.give(bank, m_u)
            yield
            pairs = []
            PE.wait(m_pt, m_u)
            for h in range(2):
                bank = take()
                for b in (2 * h, 2 * h + 1):
                    m = mm(bank.tensor[:, (b % 2) * D:(b % 2 + 1) * D],
                           [(pickT[:, b * P:(b + 1) * P], up[:, b * D:(b + 1) * D])], mark=b % 2 == 1)
                pairs.append((bank, m))
            yield
            return (yield from norm(x, pairs))

        def decayed(g, x, ready):
            areaB.reset()
            xT, qT, kT, v = (areaB.carve(DC * T) for _ in range(4))
            xT, qT, kT = (t.rearrange("p (c t) -> p c t", c=DC) for t in (xT, qT, kT))
            v = v.rearrange("p (b d) -> p b d", b=GB)
            s, pT = areaB.carve(T), areaB.carve(T)
            sums, negmax, rec = areaB.carve(GB), areaB.carve(GB), areaB.carve(GB)
            m_x = yield from to_channels(x, ready, xT)
            w1 = w["wqkv1"][:, :].rearrange("p (c n) -> p c n", c=DC)
            for i, dst in enumerate((qT, kT)):
                for c, (bank, m) in enumerate(project(w1, i * D, xT, m_x)):
                    m_qk = SC.put(act.activation, dst[:, c, :], bank.tensor[:, :], ACT.Identity,
                                  bias=w["bqk"][:, 2 * i + c:2 * i + c + 1], after=(m,))
                    banks.give(bank, m_qk)
                yield
            for i, (bank, m) in enumerate(project_rows(w1, 2 * D, xT, (), bias=64)):
                m_v = SC.put(act.activation, v[:, 2 * i:2 * i + 2, :], bank.tensor[:, :].rearrange("p (b d) -> p b d", b=2),
                             ACT.Copy, after=(m,))
                banks.give(bank, m_v)
            yield
            bank = take()
            PE.wait(m_qk)
            for b in range(GB):
                m = mm(bank.tensor[:, b * P:(b + 1) * P], [(qT[:, c, b * P:(b + 1) * P], kT[:, c, b * P:(b + 1) * P])
                                                            for c in range(DC)], mark=b == GB - 1)
            s3 = s.rearrange("p (b k) -> p b k", b=GB)
            m = DVE.put(dve.tensor_tensor, s3, bank.tensor[:, :].rearrange("p (b k) -> p b k", b=GB),
                        bc(decay[:, :], 1, GB), ALU.mult, after=(m,))
            banks.give(bank, m)
            yield
            m_e = yield from key_softmax(s3, (m,), 1.0, sums, negmax)
            yield
            m = DVE.put(dve.reciprocal, rec, sums, after=(m_e,))
            m = POOL.put(pool.tensor_tensor, s3, s3, bc(rec, 2, P), ALU.mult, after=(m,))
            bank = take()
            for b in range(GB):
                mt = tp(bank.tensor[:, b * P:(b + 1) * P], s3[:, b, :], after=(m,), mark=b == GB - 1)
            m = SC.put(act.activation, pT, bank.tensor[:, :], ACT.Copy, after=(mt,))
            banks.give(bank, m)
            yield
            oT = qT
            PE.wait(m, m_v)
            for c in range(DC):
                bank = take()
                for b in range(GB):
                    m = mm(bank.tensor[:, b * P:(b + 1) * P], [(v[:, b, c * P:(c + 1) * P], pT[:, b * P:(b + 1) * P])],
                           mark=b == GB - 1)
                m_o = SC.put(act.activation, oT[:, c, :], bank.tensor[:, :], ACT.Copy, after=(m,))
                banks.give(bank, m_o)
            yield
            y = project_rows(chunked("wp1"), 0, oT, (m_o,), bias=96)
            yield
            return (yield from norm(x, y))

        def memory(g, x, ready, free):
            areaC.reset()
            xT, ctxT, qT = (areaC.carve(DC * T) for _ in range(3))
            att = xT.rearrange("p (b d) -> p b d", b=GB)
            xT, ctxT, qT = (t.rearrange("p (c t) -> p c t", c=DC) for t in (xT, ctxT, qT))
            KV = P + DH + 1
            kv = areaC.carve(GB * KV).rearrange("p (b n) -> p b n", b=GB)
            o, oT = areaC.carve(T), areaC.carve(T)
            mk = [areaC.carve(2 * P) for _ in range(2)]
            mv = areaC.carve(GB * (DH + 1)).rearrange("p (b n) -> p b n", b=GB)
            e, pT = areaC.carve(H * P), areaC.carve(H * P)
            m8, i8 = areaC.carve(8 * GB), areaC.carve(8 * GB)
            mx, rec = areaC.carve(H), areaC.carve(H)
            m_c = s_ctxc.dma(SP, sp.dma_start, ctxT, io["ctxT"][g].rearrange("p (c t) -> p c t", c=DC), after=free)
            for s in (SC, DVE, POOL):
                s.wait(*free)
            wk, wv = w["wkrep"][:, :].rearrange("p (c n) -> p c n", c=DC), w["wv1x"][:, :].rearrange("p (c n) -> p c n", c=DC)
            PE.wait(m_c)
            m_one = POOL.put(pool.memset, kv[:, :, P + DH:KV], 1.0)
            for h in range(2):
                bank = take()
                for b in (2 * h, 2 * h + 1):
                    r = (b % 2) * D
                    mm(bank.tensor[:, r:r + P], [(ctxT[:, c, b * P:(b + 1) * P], wk[:, c, :]) for c in range(DC)])
                    m = mm(bank.tensor[:, r + P:r + P + DH], [(ctxT[:, c, b * P:(b + 1) * P], wv[:, c, :]) for c in range(DC)],
                           mark=b % 2 == 1)
                m_kv = SC.put(act.activation, kv[:, 2 * h:2 * h + 2, 0:P + DH],
                              bank.tensor[:, :].rearrange("p (b n) -> p b n", b=2)[:, :, 0:P + DH], ACT.Copy, after=(m,))
                banks.give(bank, m_kv)
            yield
            m_x = yield from to_channels(x, ready, xT)
            for c, (bank, m) in enumerate(project(chunked("wq1x"), 0, xT, m_x)):
                m_q = SC.put(act.activation, qT[:, c, :], bank.tensor[:, :], ACT.Copy, after=(m,))
                banks.give(bank, m_q)
            yield
            bank = take()
            PE.wait(m_q)
            for b in range(GB):
                m = mm(bank.tensor[:, b * P:(b + 1) * P], [(qT[:, c, b * P:(b + 1) * P], ctxT[:, c, b * P:(b + 1) * P])
                                                            for c in range(DC)], mark=b == GB - 1)
            m_s = SC.put(act.activation, o, bank.tensor[:, :], ACT.Copy, after=(m,))
            banks.give(bank, m_s)
            DVE.wait(m_s)
            yield
            for b in range(GB):
                m = DVE.put(dve.max, m8[:, 8 * b:8 * b + 8], o[:, b * P:(b + 1) * P])
            i8u = i8.bitcast(U32)
            DVE.wait(m)
            for b in range(GB):
                m = DVE.put(dve.max_index, i8u[:, 8 * b:8 * b + 8], m8[:, 8 * b:8 * b + 8], o[:, b * P:(b + 1) * P])
            first = i8u.rearrange("p (b n) -> p b n", b=GB)[:, :, 0]
            o3 = o.rearrange("p (b n) -> p b n", b=GB)
            m = DVE.put(dve.tensor_tensor, o3, bc(first, 2, P), bc(w["iota128"][:, :], 1, GB), ALU.is_equal, after=(m,))
            yield
            bank = take()
            for b in range(GB):
                mt = tp(bank.tensor[:, b * P:(b + 1) * P], o[:, b * P:(b + 1) * P], after=(m,), mark=b == GB - 1)
            m_ot = SC.put(act.activation, oT, bank.tensor[:, :], ACT.Copy, after=(mt,))
            banks.give(bank, m_ot)
            yield
            bank = take()
            PE.wait(m_ot, m_kv, m_one)
            for b in range(GB):
                m = mm(bank.tensor[:, b * (DH + 1):(b + 1) * (DH + 1)], [(oT[:, b * P:(b + 1) * P], kv[:, b, P:KV])],
                       mark=b == GB - 1)
            m_mv = SC.put(act.activation, mv, bank.tensor[:, 0:GB * (DH + 1)].rearrange("p (b n) -> p b n", b=GB), ACT.Copy,
                          after=(m,))
            banks.give(bank, m_mv)
            mkbank = take()
            for b in range(GB):
                m_mk = mm(mkbank.tensor[:, b * P:(b + 1) * P], [(kv[:, b, 0:P], oT[:, b * P:(b + 1) * P])], mark=b == GB - 1)
            yield
            mk_free = [[], []]
            e_free, p_free = [], []
            m_att = []
            for b in range(GB):
                key = mk[b % 2].rearrange("p (par k) -> p par k", par=2)
                m_key = DVE.put(dve.tensor_tensor, key, bc(mkbank.tensor[:, b * P:(b + 1) * P], 1, 2),
                                bc(w["parity"][:, :], 2, P), ALU.mult, after=(m_mk, *mk_free[b % 2]))
                if b == GB - 1:
                    banks.give(mkbank, m_key)
                quads = []
                for r in range(4):
                    bank = take()
                    PE.wait(m_key)
                    for c in range(DC):
                        m = mm(bank.tensor[:, c * 2 * P:(c + 1) * 2 * P],
                               [(qT[32 * r:32 * r + 32, c, b * P:(b + 1) * P], mk[b % 2][32 * r:32 * r + 32])], mark=True)
                    s3 = bank.tensor[:, :].rearrange("p (h k) -> p h k", h=4)
                    er = e[:, r * T:(r + 1) * T].rearrange("p (h k) -> p h k", h=4)
                    m1 = DVE.put(dve.tensor_reduce, mx[:, 4 * r:4 * r + 4], s3, X, ALU.max, after=(m,))
                    m1 = DVE.put(dve.tensor_tensor, er, s3, bc(mx[:, 4 * r:4 * r + 4], 2, P), ALU.subtract,
                                 after=(m1, *e_free))
                    banks.give(bank, m1)
                    m1 = SC.put(act.activation, er, er, ACT.Exp, scale=float(DH) ** -0.5, after=(m1,))
                    quads.append(m1)
                    if r % 2:
                        yield
                mk_free[b % 2] = [m]
                for r in range(4):
                    bank = take()
                    for h in range(4):
                        m = tp(bank.tensor[:, h * P:(h + 1) * P], e[:, (4 * r + h) * P:(4 * r + h + 1) * P], after=(quads[r],),
                               mark=h == 3)
                    stream, put = (DVE, dve.tensor_copy) if r % 2 else (SC, act.copy)
                    m_pt = stream.put(put, pT[:, r * T:(r + 1) * T], bank.tensor[:, :], after=(m, *p_free))
                    banks.give(bank, m_pt)
                    quads[r] = m_pt
                    if r % 2:
                        yield
                e_free = [m]
                bank = take()
                PE.wait(m_mv, *quads)
                for r in range(4):
                    for c in range(DC):
                        for par in range(2):
                            head = c * HC + 2 * r + par
                            at = 4 * r + 2 * c + par
                            m = mm(bank.tensor[:, head * (DH + 1):(head + 1) * (DH + 1)],
                                   [(pT[:, at * P:(at + 1) * P], mv[:, b, :])], mark=at == H - 1)
                p_free = [m]
                yield
                a3 = bank.tensor[:, 0:H * (DH + 1)].rearrange("p (h n) -> p h n", h=H)
                m1 = DVE.put(dve.reciprocal, rec, a3[:, :, DH], after=(m,))
                m1 = DVE.put(dve.tensor_tensor, att[:, b, :].rearrange("p (h d) -> p h d", h=H), a3[:, :, 0:DH],
                             bc(rec, 2, DH), ALU.mult, after=(m1,))
                DVE.wait(m1)
                banks.give(bank, m1)
                m_att.append(m1)
            aT = qT
            m_a = yield from to_channels(att, m_att, aT)
            y = project_rows(chunked("wc1x"), 0, aT, m_a)
            yield
            return (yield from norm(x, y))

        def feed_forward(g, x, ready):
            areaC.reset()
            n1 = areaC.carve(T).bitcast(BF16)
            n1T = areaC.carve(T).bitcast(BF16).rearrange("p (c t) -> p c t", c=DC)
            tmp = areaC.carve(GB * D)
            dg = areaC.carve(P)
            rsb = areaC.carve(T)
            LP = P + 2
            hs = [areaC.carve(GB * LP).rearrange("p (b t) -> p b t", b=GB) for _ in range(2)]
            c_ = [areaC.carve(T) for _ in range(HJ)]
            n2 = [areaC.carve(T // 2).bitcast(BF16) for _ in range(HJ)]
            th, top = [tmp[:, 0:T], tmp[:, T:2 * T]], areaC.carve(T)
            am, sc1, rs1, rs2 = (areaC.carve(GB) for _ in range(4))
            m = DVE.put(dve.tensor_reduce, am, x[:, :, :], X, ALU.max, apply_absolute_value=True, after=ready)
            m = DVE.put(dve.tensor_scalar, am, am, 1e-5, None, ALU.max, after=(m,))
            m1 = DVE.put(dve.reciprocal, sc1, am, after=(m,))
            m1 = DVE.put(dve.tensor_scalar, sc1, sc1, 127.0, None, ALU.mult, after=(m1,))
            m2 = DVE.put(dve.tensor_scalar, rs1, am, wmean[:, 0:1], 1.0 / 127.0, ALU.mult, ALU.mult, after=(m1,))
            POOL.wait(m1, *ready)
            DVE.wait(m1)
            for b in range(GB):
                m = DVE.put(dve.tensor_scalar, tmp[:, b * D:(b + 1) * D], x[:, b, :], sc1[:, b:b + 1], MAGIC, ALU.mult, ALU.add)
            m_n = DVE.put(dve.tensor_scalar, n1, tmp, MAGIC, None, ALU.subtract, after=(m,))
            m_n = POOL.put(pool.memset, hs[0][:, :, 0:LP:P + 1], 0.0, after=(m_n,)) and m_n
            m_pad = POOL.put(pool.memset, hs[1][:, :, 0:LP:P + 1], 0.0)
            yield
            bank = take()
            b16 = bank.tensor[:, :].bitcast(BF16).rearrange("p (c t) -> p c t", c=DC)
            n13 = n1.rearrange("p (b d) -> p b d", b=GB)
            PE.wait(m_n, m_identb)
            for c in range(DC):
                for b in range(GB):
                    m = tp(b16[:, c, b * P:(b + 1) * P], n13[:, b, c * P:(c + 1) * P], mark=c + b == GB, identity=identb[:, :])
            m_nt = SC.put(act.activation, n1T, b16, ACT.Copy, after=(m,))
            banks.give(bank, m_nt)

            def along_tokens(col):
                bank = take()
                m = None
                for b in range(GB):
                    md = DVE.put(dve.tensor_scalar, dg, I, col[:, b:b + 1], None, ALU.mult, after=(m,) if m else ())
                    m = mm(bank.tensor[:, b * P:(b + 1) * P], [(onesb[:, :], dg)], after=(md,), mark=True)
                return bank, m

            DVE.wait(m2)
            bank, m = along_tokens(rs1)
            m_rs = SC.put(act.activation, rsb, bank.tensor[:, :], ACT.Copy, after=(m,))
            banks.give(bank, m_rs)
            yield
            hs_free = [[], []]
            m_top = None
            cw = w["convw"][:, :].rearrange("p (j k) -> p j k", k=3)
            PE.wait(m_nt)
            for j in range(HJ):
                bank = take()
                m = mm(bank.tensor[:, :], [(w1q[:, c, j * P:(j + 1) * P], n1T[:, c, :]) for c in range(DC)], mark=True)
                h = hs[j % 2]
                m_h = DVE.put(dve.tensor_tensor, h[:, :, 1:P + 1], bank.tensor[:, :].rearrange("p (b t) -> p b t", b=GB),
                              rsb.rearrange("p (b t) -> p b t", b=GB), ALU.mult, after=(m, m_rs, m_pad, *hs_free[j % 2]))
                banks.give(bank, m_h)
                cj = c_[j].rearrange("p (b t) -> p b t", b=GB)
                m_c = SC.put(act.activation, cj, h[:, :, 1:P + 1], ACT.Identity, bias=w["convb"][:, j:j + 1],
                             scale=cw[:, j, 1:2], after=(m_h,))
                yield
                m = DVE.put(dve.scalar_tensor_tensor, cj, h[:, :, 0:P], cw[:, j, 0:1], cj, ALU.mult, ALU.add, after=(m_c,))
                m = DVE.put(dve.scalar_tensor_tensor, cj, h[:, :, 2:P + 2], cw[:, j, 2:3], cj, ALU.mult, ALU.add, after=(m,))
                hs_free[j % 2] = [m]
                mt = SC.put(act.activation, th[j % 2], c_[j], ACT.Tanh, scale=0.5, after=(m,))
                yield
                m = DVE.put(dve.scalar_tensor_tensor, c_[j], th[j % 2], 1.0, c_[j], ALU.add, ALU.mult, after=(mt,))
                if j == 0:
                    m_top = SC.put(act.activation, top, c_[j], ACT.Abs, after=(m,))
                else:
                    m = SC.put(act.activation, th[j % 2], c_[j], ACT.Abs, after=(m,))
                    m_top = DVE.put(dve.tensor_tensor, top, th[j % 2], top, ALU.max, after=(m, m_top))
                    SC.wait(m_top)
            bank = take()
            for b in range(GB):
                m = tp(bank.tensor[:, b * P:(b + 1) * P], top[:, b * P:(b + 1) * P], after=(m_top,), mark=b == GB - 1)
            m = DVE.put(dve.tensor_reduce, am, bank.tensor[:, :].rearrange("p (b k) -> p b k", b=GB), X, ALU.max, after=(m,))
            banks.give(bank, m)
            m = DVE.put(dve.tensor_scalar, am, am, 0.5, 1e-5, ALU.mult, ALU.max, after=(m,))
            m1 = DVE.put(dve.reciprocal, sc1, am, after=(m,))
            m1 = DVE.put(dve.tensor_scalar, sc1, sc1, 127.0 * 0.5, None, ALU.mult, after=(m1,))
            m_r2 = DVE.put(dve.tensor_scalar, rs2, am, wmean[:, 1:2], 1.0 / 127.0, ALU.mult, ALU.mult, after=(m1,))
            DVE.wait(m_r2)
            bank, m = along_tokens(sc1)
            DVE.wait(m)
            yield
            m_q = []
            for j in range(HJ):
                m = DVE.put(dve.tensor_tensor, c_[j], c_[j], bank.tensor[:, :], ALU.mult)
                if j == HJ - 1:
                    banks.give(bank, m)
                m_q.append(DVE.put(dve.tensor_scalar, n2[j], c_[j], MAGIC, MAGIC, ALU.add, ALU.subtract, after=(m,)))
                if j % 2:
                    yield
            pairs = []
            for h in range(2):
                bank = take()
                for b in (2 * h, 2 * h + 1):
                    m = mm(bank.tensor[:, (b % 2) * D:(b % 2 + 1) * D], [(n2[j][:, b * P:(b + 1) * P], w2q[:, j, :])
                                                                           for j in range(HJ)], after=m_q, mark=b % 2 == 1)
                pairs.append((bank, m))
                yield
            return (yield from norm(x, pairs, rs2, (m_r2,)))

        identb = sb("identb", [P, P], BF16)

        setup()
        m_identb = DVE.put(dve.tensor_copy, identb[:, :], I)
        x_out = [[] for _ in range(4)]
        ended = {}

        def load_x(g):
            xt = xs[g % 4]
            src = io["x"][g * T:(g + 1) * T, :].rearrange("(b t) d -> t b d", b=GB)
            return s_x[g % 4].dma(SP, sp.dma_start, xt[:, :, :], src, after=x_out[g % 4])

        def station_a(g):
            m = load_x(g)
            for s in (DVE, PE):
                s.wait(m)
            ended["A", g] = yield from windowed(g, xs[g % 4], [m] * GB, ended.get(("A", g - 1), setup_done))

        def station_b(g):
            x = xs[g % 4]
            r = yield from cross(g, x, ended["A", g], ended.get(("B", g - 1), setup_done))
            r = yield from experts(g, x, r)
            ended["B", g] = yield from decayed(g, x, r)

        def station_c(g):
            x = xs[g % 4]
            r = yield from memory(g, x, ended["B", g], ended.get(("C", g - 1), setup_done))
            r = yield from feed_forward(g, x, r)
            ended["C", g] = r
            m = s_out.dma(SP, sp.dma_start, out[g * T:(g + 1) * T, :].rearrange("(b t) d -> t b d", b=GB), x[:, :, :], after=r)
            x_out[g % 4] = [m]
            last_out[0] = m

        last_out = [None]
        setup_done = [m_identb]
        steps = {}
        for rnd in range(NG + 2):
            work = []
            for name, station, g in (("C", station_c, rnd - 2), ("B", station_b, rnd - 1), ("A", station_a, rnd)):
                if 0 <= g < NG:
                    work.append([name, station(g), 0, steps.get(name, 60)])
            while work:
                job = min(work, key=lambda j: j[2] / j[3])
                try:
                    next(job[1])
                    job[2] += 1
                except StopIteration:
                    steps[job[0]] = job[2] + 1
                    work.remove(job)
        SP.wait(last_out[0])

        with nc.Block() as block:
            @block.sync
            def _(eng):
                SP.play(eng)

            @block.tensor
            def _(eng):
                PE.play(eng)

            @block.vector
            def _(eng):
                DVE.play(eng)

            @block.scalar
            def _(eng):
                SC.play(eng)

            @block.gpsimd
            def _(eng):
                POOL.play(eng)


def constants():
    f = np.float32
    p = np.arange(P)
    half = ROT // 2
    inv = (1.0 / f(10000.0) ** (np.arange(half, dtype=f) * f(2.0) / f(ROT))).astype(f)
    ang = (p.astype(f)[:, None] * inv).astype(f)
    cos, sin = np.cos(ang).astype(f), np.sin(ang).astype(f)
    diff = p[:, None] - p[None, :]
    bit = [((np.maximum(diff, 0) >> i) & 1).astype(f) for i in range(7)]
    q, k = p[:, None] % ES, np.arange(ES)[None, :]
    same = (q // NS == k // NS) & (k % NS <= q % NS)
    pos = np.zeros((P, 1), f)
    pos[:WIN * H, 0] = np.repeat(np.linspace(0.0, 1.0, WIN, dtype=f), H)
    swap = np.zeros((P, ROT), f)
    swap[(np.arange(ROT) + half) % ROT, np.arange(ROT)] = 1.0
    return {
        "ident": np.eye(P, dtype=f),
        "headsum": (p[:, None] // DH == np.arange(HC)[None, :]).astype(f),
        "parity": (p[:, None] % 32 // DH == np.arange(2)[None, :]).astype(f),
        "iota16": np.tile(np.arange(1, NS + 1, dtype=f), (P, 1)),
        "iota128": np.tile(np.arange(P, dtype=f), (P, 1)),
        "pos": pos,
        "cos": np.concatenate([cos, cos], 1), "sin": np.concatenate([-sin, sin], 1),
        "swap": swap,
        "blk": np.where(same, f(0), f(FAR)).astype(f),
        "bits": np.concatenate(bit + [1 - b for b in bit] + [(diff >= 0).astype(f)], 1),
    }


def laid_out(a):
    def rows(m):
        c = m.shape[0] // P
        return m.reshape(c, P, -1).transpose(1, 0, 2).reshape(P, -1)

    def per_head(m):
        return np.tile(m.reshape(H, -1), (WIN, 1))

    def by_group(m):
        return m.reshape(NG, T, DC, P).transpose(0, 3, 2, 1).reshape(NG, P, DC * T)

    bq = a["L1_attn_bqkv"]
    bias_rows = np.zeros((P, D), np.float32)
    for at, row in ((0, a["L0_attn_bo"]), (32, a["L0_xattn_bv"]), (64, bq[2 * D:]), (96, a["L1_attn_bproj"])):
        bias_rows[at] = row
    wkv = a["L1_xattn_Wkv"]
    return {
        "x": a["x"].reshape(NSEQ * P, D), "xT": by_group(a["x"]), "ctxT": by_group(a["ctx_1024"]),
        "wq0": rows(a["L0_attn_wq"].T), "wk0": rows(a["L0_attn_wk"].T), "wv0": rows(a["L0_attn_wv"].T),
        "wo0": rows(a["L0_attn_wo"].T),
        "c1": per_head(a["L0_attn_cw1"]), "b1": per_head(a["L0_attn_cb1"]), "c2": per_head(a["L0_attn_cw2"]),
        "b2": per_head(a["L0_attn_cb2"]), "c3": per_head(a["L0_attn_cw3"]), "b3": per_head(a["L0_attn_cb3"]),
        "raw_q": rows(a["L0_xattn_Wq"]), "raw_k": rows(a["L0_xattn_Wk"]), "wv0x": rows(a["L0_xattn_Wv"].T),
        "xmask": a["mask_SxS2_fk0"],
        "wr": rows(a["L0_ffn_Wr"].T),
        "wqkv_e": a["L0_ffn_Wqkv"].reshape(NE, DC, P, 3 * HP).transpose(2, 1, 0, 3).reshape(P, -1),
        "wo_e": a["L0_ffn_Wo"].transpose(1, 0, 2).reshape(P, -1),
        "wqkv1": rows(a["L1_attn_Wqkv"]), "bqk": bq[:2 * D].reshape(4, P).T, "wp1": rows(a["L1_attn_Wproj"]),
        "gamma": np.broadcast_to(a["L1_attn_gamma"].reshape(1, 1), (P, 1)),
        "wq1x": rows(a["L1_xattn_Wq"].T), "wkrep": rows(np.tile(wkv[:DH].T, (1, HC))), "wv1x": rows(wkv[DH:].T),
        "wc1x": rows(a["L1_xattn_Wc"].T),
        "raw1": rows(a["L1_ffn_w1"].T), "raw2": rows(a["L1_ffn_w2"].T),
        "convw": a["L1_ffn_conv_w"].reshape(HJ, P, 3).transpose(1, 0, 2).reshape(P, -1),
        "convb": a["L1_ffn_conv_b"].reshape(HJ, P).T,
        "rows": bias_rows,
    }


def kernel(**inputs):
    import concourse.bacc as bacc
    from concourse.bass_utils import run_bass_kernel_spmd

    nc = bacc.Bacc("TRN2", target_bir_lowering=False, num_devices=1)
    arrays = {**laid_out({k: np.asarray(v) for k, v in inputs.items()}), **constants()}
    arrays = {k: np.ascontiguousarray(v) for k, v in arrays.items()}
    io = {k: nc.dram_tensor(f"in_{k}", v.shape, mybir.dt.from_np(v.dtype), kind="ExternalInput").ap()
          for k, v in arrays.items()}
    out = nc.dram_tensor("y", (NSEQ * P, D), F32, kind="ExternalOutput").ap()
    build(nc, io, out)
    r = run_bass_kernel_spmd(nc, [{f"in_{k}": v for k, v in arrays.items()}], core_ids=[0])
    return r.results[0]["y"].reshape(NSEQ, P, D)
```

```python
from contextlib import ExitStack

import numpy as np

import concourse.bass as bass
from concourse import mybir

F32 = mybir.dt.float32
BF16 = mybir.dt.bfloat16
U32 = mybir.dt.uint32
ALU = mybir.AluOpType
ACT = mybir.ActivationFunctionType
X = mybir.AxisListType.X

P = 128
D = 256
DC = D // P
NSEQ = 32
GB = 2
NG = NSEQ // GB
T = GB * P
H = 16
DH = D // H
HC = H // DC
WIN = 7
PAD = WIN // 2
NE = 8
NS = P // 8
HP = 128
ROT = 64
ES = GB * NS
EQ = P // ES
EJ = NE // EQ
W2 = DC * T
HID = 1024
HJ = HID // P
SLIDE = WIN * H - HC
CH = 32
EPS = 1e-5
MAGIC = 12582912.0
FAR = -1e30


class Mark:

    def __init__(self, sem, value):
        self.sem, self.value = sem, value


class Stream:

    def __init__(self, sem):
        self.sem, self.count, self.queue, self.seen = sem, 0, [], {}

    def wait(self, *marks):
        for mark in marks:
            if self.seen.get(mark.sem.name, 0) < mark.value:
                self.seen[mark.sem.name] = mark.value
                self.queue.append((None, (mark.sem, mark.value), {}, None))

    def put(self, builder, *args, after=(), mark=True, **kw):
        self.wait(*after)
        self.queue.append((builder, args, kw, (self.sem, 1) if mark else None))
        if mark:
            self.count += 1
            return Mark(self.sem, self.count)

    def play(self, engine):
        for builder, args, kw, inc in self.queue:
            if builder is None:
                engine.wait_ge(*args)
            else:
                instruction = builder(*args, **kw)
                if inc:
                    instruction.then_inc(*inc)


class Landing:

    def __init__(self, sem):
        self.sem, self.count = sem, 0

    def dma(self, stream, start, out, in_, after=()):
        stream.wait(*after)
        self.count += 16
        stream.queue.append((start, (out, in_), {}, (self.sem, 16)))
        return Mark(self.sem, self.count)


class Bank:

    def __init__(self, tensor):
        self.tensor, self.released = tensor, []


class Banks:

    def __init__(self, tensors):
        self.free = [Bank(t) for t in tensors]

    def take(self):
        return self.free.pop(0)

    def give(self, bank, *marks):
        bank.released = list(marks)
        self.free.append(bank)


class Area:

    def __init__(self, tensor, size):
        self.tensor, self.size, self.at = tensor, size, 0

    def reset(self):
        self.at = 0

    def carve(self, n):
        assert self.at + n <= self.size, (self.at, n, self.size)
        self.at += n
        return self.tensor[:, self.at - n:self.at]


def bc(ap, axis, n):
    v = ap.unsqueeze(axis)
    shape = list(v.shape)
    shape[axis] = n
    return v.broadcast_to(shape)


def build(nc, io, out):
    ctx = ExitStack()
    with ctx:
        def sb(name, shape, dt=F32):
            return ctx.enter_context(nc.sbuf_tensor(name, shape, dt))

        def sem(name):
            return ctx.enter_context(nc.semaphore(name))

        PE, DVE, SC, POOL, SP = (Stream(sem(f"{n}_done")) for n in ("pe", "dve", "act", "pool", "sp"))
        banks = Banks([ctx.enter_context(nc.psum_tensor(f"bank{i}", [P, 512], F32)) for i in range(8)])
        dve, act, pool, pe, sp = nc.vector, nc.scalar, nc.gpsimd, nc.tensor, nc.sync

        NX = 6
        xs = [sb(f"x{i}", [P, GB, D]) for i in range(NX)]
        areas = {name: Area(sb(f"area{name}", [P, n]), n)
                 for name, n in (("A", 7776), ("B", 5600), ("C", 2900), ("D", 6700), ("E", 5776))}
        w = {}
        for name, cols in (("wq0", DC * D), ("wk0", DC * D), ("wv0", DC * D), ("wo0", DC * D),
                           ("wv0x", DC * D), ("wqkv_e", DC * NE * 3 * HP), ("wo_e", NE * D),
                           ("wq1x", DC * D), ("wkrep", DC * P),
                           ("wv1x", DC * DH), ("wc1x", DC * D), ("rows", D),
                           ("convw", HJ * 3), ("convb", HJ), ("xmask", P), ("ident", P),
                           ("cos_sin", 2 * ROT), ("blk", P), ("head_of", H), ("part", 3), ("headsum", 2 * SLIDE + HC), ("parity", 2),
                           ("iota16", NS), ("iota128", P), ("pos", 1)):
            w[name] = sb("w_" + name, [P, cols])
        onesb = sb("onesb", [P, P])
        wr_pad = sb("wr_pad", [P, DC, 32])
        w_cross = sb("w_cross", [P, DC, D])
        w_qk = sb("w_qk", [P, DC, D])
        w_vp = sb("w_vp", [P, DC, D])
        picked = sb("picked", [P, GB, GB * P])
        b_key = sb("b_key", [P, DC])
        u_row = sb("u_row", [P, DC])
        bb = sb("bb", [P, 1])
        ones_bf = sb("ones_bf", [P, P], BF16)
        bias_parts = sb("bias_parts", [P, D], BF16)
        head_of = sb("head_of", [P, H], BF16)
        bias_rest, bias_round = sb("bias_rest", [P, D]), sb("bias_round", [P, D], BF16)
        conn = sb("conn", [P, WIN * H])
        decay = sb("decay", [P, P])
        w1q = sb("w1q", [P, DC, HID], BF16)
        w2q = sb("w2q", [P, HJ, D], BF16)
        wmean = sb("wmean", [P, 2])
        small = sb("small", [P, 8])
        halves = sb("halves", [P, GB])

        def chunked(name):
            return w[name][:, :].rearrange("p (c n) -> p c n", c=DC)

        in_early, in_early2, in_late, in_late2 = (Landing(sem(n)) for n in (
            "weights_in_early", "setup_in_early", "weights_in_late", "setup_in_late"))
        s_x = [Landing(sem(f"x_in{i}")) for i in range(NX)]
        s_xt, s_ctxb, s_ctxd = Landing(sem("xt_in")), Landing(sem("ctx_b_in")), Landing(sem("ctx_d_in"))
        s_shift, s_out = Landing(sem("shift_in")), [Landing(sem(f"y_out{i}")) for i in range(NX)]

        I = w["ident"][:, :]

        def mm(out_ap, pairs, after=(), mark=False):
            PE.wait(*after)
            n = len(pairs)
            for i, (l, r) in enumerate(pairs):
                m = PE.put(pe.matmul, out_ap, l, r, start=i == 0, stop=i == n - 1, mark=mark and i == n - 1)
            return m

        def tp(out_ap, in_ap, after=(), mark=False):
            return PE.put(pe.transpose, out_ap, in_ap, I, after=after, mark=mark)

        def take():
            bank = banks.take()
            PE.wait(*bank.released)
            return bank

        def copy_out(dst, src, bank, after, func=ACT.Copy, **kw):
            m = SC.put(act.activation, dst, src, func, after=after, **kw)
            banks.give(bank, m)
            return m

        def blocks(t, n=DC):
            return t.rearrange("p (c t) -> p c t", c=n)

        def setup_early():
            m_ones = POOL.put(pool.memset, onesb[:, :], 1.0)
            POOL.put(pool.memset, halves[:, :], -0.5)
            m_ones = POOL.put(pool.memset, ones_bf[:, :], 1.0)
            area = areas["E"]
            c1, b1, c2, b2, c3, b3 = (area.carve(n) for n in (CH, CH, CH * CH, CH, CH, 1))
            cw, h1, h2, cwt, s1 = (area.carve(n) for n in (CH * CH, CH, CH, 1, 1))
            n112 = WIN * H
            diag, mx, den = area.carve(n112), area.carve(H), area.carve(H)
            for name in ("ident", "headsum", "pos", "wq0", "wk0", "wv0", "rows", "part", "wo0"):
                m_w = in_early.dma(SP, sp.dma_start, w[name][:, :], io[name])
            for dst, src in ((c1[0:n112], "c1"), (b1[0:n112], "b1"),
                             (c2[0:n112], "c2"), (b2[0:n112], "b2"), (c3[0:n112], "c3"), (b3[0:n112], "b3")):
                m_setup = in_early2.dma(SP, sp.dma_start, dst, io[src])
            PE.wait(m_w, m_ones)
            yield
            m = DVE.put(dve.scalar_tensor_tensor, h1[0:n112], c1[0:n112], w["pos"][0:n112, 0:1], b1[0:n112], ALU.mult,
                        ALU.add, after=(m_setup, m_w))
            m = SC.put(act.activation, h1[0:n112], h1[0:n112], ACT.Gelu, after=(m,))
            m = DVE.put(dve.tensor_tensor, cw[0:n112].rearrange("p (j i) -> p j i", i=CH),
                        c2[0:n112].rearrange("p (j i) -> p j i", i=CH), bc(h1[0:n112], 1, CH), ALU.mult, after=(m,))
            m = DVE.put(dve.tensor_reduce, h2[0:n112], cw[0:n112].rearrange("p (j i) -> p j i", i=CH), X, ALU.add, after=(m,))
            m = DVE.put(dve.tensor_tensor, h2[0:n112], h2[0:n112], b2[0:n112], ALU.add, after=(m,))
            m = SC.put(act.activation, h2[0:n112], h2[0:n112], ACT.Gelu, after=(m,))
            m = DVE.put(dve.tensor_tensor, h1[0:n112], h2[0:n112], c3[0:n112], ALU.mult, after=(m,))
            m = DVE.put(dve.tensor_reduce, s1[0:n112], h1[0:n112], X, ALU.add, after=(m,))
            m = DVE.put(dve.tensor_tensor, cwt[0:n112], s1[0:n112], b3[0:n112], ALU.add, after=(m,))
            m = DVE.put(dve.tensor_scalar, diag[0:n112], I[0:n112, 0:n112], cwt[0:n112, 0:1], None, ALU.mult, after=(m,))
            bank = take()
            m = mm(bank.tensor[:, 0:n112], [(onesb[0:n112, :], diag[0:n112])], after=(m, m_ones), mark=True)
            m = DVE.put(dve.tensor_copy, conn[:, :], bank.tensor[:, 0:n112], after=(m,))
            banks.give(bank, m)
            by_head = conn[:, :].rearrange("p (w h) -> p h w", h=H)
            conn3 = conn[:, :].rearrange("p (w h) -> p w h", h=H)
            m = DVE.put(dve.tensor_reduce, mx, by_head, X, ALU.max, after=(m,))
            m = DVE.put(dve.tensor_tensor, conn3, conn3, bc(mx, 1, WIN), ALU.subtract, after=(m,))
            m = SC.put(act.activation, conn[:, :], conn[:, :], ACT.Exp, after=(m,))
            m = DVE.put(dve.tensor_reduce, den, by_head, X, ALU.add, after=(m,))
            m = DVE.put(dve.reciprocal, den, den, after=(m,))
            m = DVE.put(dve.tensor_tensor, conn3, conn3, bc(den, 1, WIN), ALU.mult, after=(m,))
            DVE.wait(m)
            early_done.append(m)
            early_done.append(split_bias(slice(0, 64)))

        early_done, late_done = [], []

        def split_bias(r, after=()):
            rest, part, parts = w["rows"][r, :], bias_rest[r, :], bias_parts[r, :]
            m = DVE.put(dve.memset, part, 0.0, after=after)
            for k in range(3):
                m1 = DVE.put(dve.tensor_copy, bias_round[r, :], rest, after=(m,))
                m2 = DVE.put(dve.scalar_tensor_tensor, part, bias_round[r, :], w["part"][r, k:k + 1], part, ALU.mult,
                             ALU.add, after=(m1,))
                m = DVE.put(dve.tensor_tensor, rest, rest, bias_round[r, :], ALU.subtract, after=(m2,))
            return DVE.put(dve.tensor_copy, parts, part, after=(m2,))

        def setup_late():
            m_zero = POOL.put(pool.memset, wr_pad[:, :, :], 0.0)
            POOL.put(pool.memset, picked[:, :, :], 0.0)
            aB, aC, aD, aE = (areas[n] for n in "BCDE")
            aE.reset()
            raw_q, raw_k, q1, k1, v1, p1 = (aB.carve(DC * D) for _ in range(6))
            bits, gam, bqkv = aB.carve(15 * P), aB.carve(1), aB.carve(3 * DC)
            powers, fac, t_b = aB.carve(7), aB.carve(P), aB.carve(1)
            raw1, raw2, tmp = aC.carve(DC * HID), aD.carve(HJ * D), aD.carve(HJ * D)
            for dst, src in ((raw_q, "raw_q"), (raw_k, "raw_k"), (gam, "gamma"), (bits, "bits"), (bqkv, "bqkv1"),
                             (q1, "wq1T"), (k1, "wk1T"), (v1, "wv1T"), (p1, "wp1"), (raw1, "raw1"), (raw2, "raw2")):
                m_setup = in_late2.dma(SP, sp.dma_start, dst, io[src])
            m_setup = in_late2.dma(SP, sp.dma_start, wr_pad[:, :, 0:NE], io["wr"].rearrange("p (c n) -> p c n", c=DC),
                                   after=(m_zero,))
            for name in ("xmask", "wv0x", "cos_sin", "blk", "head_of", "iota16", "iota128", "parity",
                         "wqkv_e", "wo_e", "wq1x", "wkrep", "wv1x", "wc1x", "convw", "convb"):
                m_w = in_late.dma(SP, sp.dma_start, w[name][:, :], io[name])
            weights_late.append(m_w)
            for _ in range(24):
                yield
            PE.wait(m_setup, m_w)
            SC.wait(m_setup, m_w)
            POOL.wait(m_w)
            DVE.wait(m_w, m_setup)
            DVE.put(dve.tensor_copy, head_of[:, :], w["head_of"][:, :])
            m = DVE.put(dve.tensor_copy, powers[:, 0:1], gam)
            for i in range(1, 7):
                m = DVE.put(dve.tensor_tensor, powers[:, i:i + 1], powers[:, i - 1:i], powers[:, i - 1:i], ALU.mult, after=(m,))
            m = DVE.put(dve.tensor_scalar, decay[:, :], bits[:, 14 * P:15 * P], float(D) ** -0.5, None, ALU.mult, after=(m,))
            for i in range(7):
                m2 = DVE.put(dve.scalar_tensor_tensor, fac, bits[:, i * P:(i + 1) * P], powers[:, i:i + 1],
                             bits[:, (7 + i) * P:(8 + i) * P], ALU.mult, ALU.add, after=(m,))
                m = DVE.put(dve.tensor_tensor, decay[:, :], decay[:, :], fac, ALU.mult, after=(m2,))
            yield
            def product(dst, left, right):
                bank = take()
                for c in range(DC):
                    m = mm(bank.tensor[:, c * D:(c + 1) * D], [(left[:, n * D + c * P:n * D + (c + 1) * P],
                                                               right[:, n * D:(n + 1) * D]) for n in range(DC)], mark=True)
                return copy_out(dst[:, :, :], blocks(bank.tensor[:, :]), bank, (m,))

            product(w_cross, raw_k, raw_q)
            yield
            product(w_qk, q1, k1)
            yield
            product(w_vp, v1, p1)
            bank = take()
            for c in range(DC):
                mm(bank.tensor[:, c:c + 1], [(k1[:, n * D + c * P:n * D + (c + 1) * P], bqkv[:, n:n + 1]) for n in range(DC)])
                mm(bank.tensor[:, 2 + c:3 + c], [(q1[:, n * D + c * P:n * D + (c + 1) * P], bqkv[:, DC + n:DC + n + 1])
                                                  for n in range(DC)])
            m = mm(bank.tensor[64:96, D:2 * D],
                   [(bqkv[:, 2 * DC + n:2 * DC + n + 1].broadcast_to([P, 32]), p1[:, n * D:(n + 1) * D]) for n in range(DC)]
                   + [(onesb[64:65, 0:32], w["rows"][64:65, :])], mark=True)
            SC.put(act.activation, b_key[:, :], bank.tensor[:, 0:2], ACT.Copy, after=(m,))
            SC.put(act.activation, u_row[:, :], bank.tensor[:, 2:4], ACT.Copy)
            m_b = copy_out(w["rows"][64:96, :], bank.tensor[64:96, D:2 * D], bank, ())
            m_parts = split_bias(slice(64, 96), (m_b,))
            m = DVE.put(dve.tensor_tensor, bqkv[:, 0:DC], bqkv[:, 0:DC], bqkv[:, DC:2 * DC], ALU.mult, after=(m,))
            m = DVE.put(dve.tensor_reduce, t_b, bqkv[:, 0:DC], X, ALU.add, after=(m,))
            bank = take()
            m = mm(bank.tensor[:, 0:1], [(onesb[:, :], t_b)], after=(m,), mark=True)
            m_sc = copy_out(bb[:, :], bank.tensor[:, 0:1], bank, (m,))
            yield
            for i, (raw, q) in enumerate(((raw1, w1q[:, :, :].rearrange("p c n -> p (c n)")),
                                          (raw2, w2q[:, :, :].rearrange("p c n -> p (c n)")))):
                m = DVE.put(dve.tensor_reduce, small[:, i:i + 1], raw, X, ALU.add, apply_absolute_value=True)
                bank = take()
                m = mm(bank.tensor[:, 0:1], [(onesb[:, :], small[:, i:i + 1])], after=(m,), mark=True)
                m = DVE.put(dve.tensor_scalar, wmean[:, i:i + 1], bank.tensor[:, 0:1], 1.0 / (HID * D), 1e-5,
                            ALU.mult, ALU.max, after=(m,))
                banks.give(bank, m)
                m = DVE.put(dve.reciprocal, small[:, 2 + i:3 + i], wmean[:, i:i + 1], after=(m,))
                m = DVE.put(dve.tensor_scalar, tmp, raw, small[:, 2 + i:3 + i], MAGIC, ALU.mult, ALU.add, after=(m,))
                m = DVE.put(dve.tensor_scalar, tmp, tmp, MAGIC, 1.0, ALU.subtract, ALU.min, after=(m,))
                m = DVE.put(dve.tensor_scalar, q, tmp, -1.0, None, ALU.max, after=(m,))
                yield
            late_done.extend([m, m_sc, m_parts])

        weights_late = []

        def to_channels(x, ready, xT):
            bank = take()
            for c in range(DC):
                for b in range(GB):
                    m = tp(bank.tensor[:, c * T + b * P:c * T + (b + 1) * P], x[:, b, c * P:(c + 1) * P], after=(ready[b],),
                           mark=c + b == 2)
            return copy_out(xT, bank.tensor[:, :], bank, (m,))

        def project(weights, actT):
            bank = take()
            for m in range(DC):
                mk = mm(bank.tensor[:, m * T:(m + 1) * T],
                        [(weights[:, c, m * P:(m + 1) * P], actT[:, c, :]) for c in range(DC)], mark=m == 1)
            return bank, mk

        def bias_row(i):
            def terms(b):
                return [(ones_bf[32 * i:32 * i + 3, :], bias_parts[32 * i:32 * i + 3, :])]
            return terms

        def no_bias(b):
            return []

        def project_rows(weights, actT, extra=no_bias):
            bank = take()
            for b in range(GB):
                mk = mm(bank.tensor[:, b * D:(b + 1) * D],
                        [(actT[:, c, b * P:(b + 1) * P], weights[:, c, 0:D]) for c in range(DC)] + extra(b), mark=b == 1)
            return bank, mk

        NORM_SLOTS = 6
        bn_parts, bn_mv = sb("bn_parts", [P, NORM_SLOTS, GB, 6]), sb("bn_mv", [P, NORM_SLOTS, GB, 2])
        bn_scale = sb("bn_scale", [P, NORM_SLOTS, 2, GB])
        neg_top = sb("neg_top", [P, GB, 3, H])
        norm_slot, norm_free = [0], [[] for _ in range(NORM_SLOTS)]

        def norm(x, bank, ready, scale=None):
            rows = bank.tensor[:, :].rearrange("p (b d) -> p b d", d=D)
            slot = norm_slot[0] % NORM_SLOTS
            norm_slot[0] += 1
            st, agg, sc = bn_parts[:, slot], bn_mv[:, slot], bn_scale[:, slot]
            DVE.wait(*norm_free[slot], *ready)
            if scale is None:
                m = DVE.put(dve.tensor_tensor, x[:, :, :], rows, x[:, :, :], ALU.add)
            else:
                for b in range(GB):
                    m = DVE.put(dve.scalar_tensor_tensor, x[:, b, :], rows[:, b, :], scale[:, b:b + 1], x[:, b, :],
                                ALU.mult, ALU.add)
            banks.give(bank, m)
            DVE.wait(m)
            for b in range(GB):
                m = DVE.put(dve.bn_stats, st[:, b, :], x[:, b, :])
            DVE.wait(m)
            for b in range(GB):
                m = DVE.put(dve.bn_aggr, agg[:, b, :], st[:, b, :])
            rstd, shift = sc[:, 0, :], sc[:, 1, :]
            POOL.wait(m)
            m1 = POOL.put(pool.tensor_scalar, rstd, agg[:, :, 1], 1.0, EPS, ALU.mult, ALU.add)
            m2 = POOL.put(pool.tensor_scalar, shift, agg[:, :, 0], -1.0, 0.0, ALU.mult, ALU.add)
            m1 = POOL.put(pool.tensor_tensor, rstd, rstd, halves[:, :], ALU.pow, after=(m1, m2))
            m2 = POOL.put(pool.tensor_tensor, shift, shift, rstd, ALU.mult, after=(m1,))
            yield
            done = []
            for b in range(GB):
                if scale is None:
                    done.append(SC.put(act.activation, x[:, b, :], x[:, b, :], ACT.Identity, scale=rstd[:, b:b + 1],
                                       bias=shift[:, b:b + 1], after=(m2,)))
                else:
                    done.append(POOL.put(pool.tensor_scalar, x[:, b, :], x[:, b, :], rstd[:, b:b + 1], shift[:, b:b + 1],
                                         ALU.mult, ALU.add, after=(m2,)))
            norm_free[slot] = [done[-1]]
            yield
            return done

        def key_softmax(s, ready, sums, negmax):
            n, k = s.shape[1], s.shape[2]
            m = DVE.put(dve.tensor_reduce, negmax, s, X, ALU.max, negate=True, after=ready)
            for j in range(n):
                m_e = SC.put(act.activation, s[:, j, :], s[:, j, :], ACT.Exp, bias=negmax[:, j:j + 1],
                             accum_out=sums[:, j:j + 1], after=(m,))
            yield
            m = DVE.put(dve.reciprocal, sums, sums, after=(m_e,))
            return POOL.put(pool.tensor_tensor, s, s, bc(sums, 2, k), ALU.mult, after=(m,))

        POOL_SCORES, POOL_VALUES = (2, 5), (1, 4)
        SUMS = ((WIN, 0, 2), (WIN + 1, 1, 4), (WIN + 2, 3, 5), (WIN, WIN, 6), (WIN + 1, WIN + 1, WIN + 2), (WIN, WIN, WIN + 1))
        POOL_SUMS = (1,)
        area = areas["A"]
        xT0, qT0 = blocks(area.carve(W2)), blocks(area.carve(W2))
        LP = P + 2 * PAD
        kT0 = area.carve(DC * GB * LP).rearrange("p (c b t) -> p c b t", c=DC, b=GB)
        prods = [area.carve(W2) for _ in range(4)]
        vw = area.carve(WIN * W2).rearrange("p (w n) -> p w n", w=WIN)
        e0 = area.carve(GB * WIN * H)
        sT0 = area.carve(T)
        den0 = area.carve(3 * GB * H).rearrange("p (k n) -> p k n", k=3)
        POOL.put(pool.memset, vw, 0.0)
        m_pads = POOL.put(pool.memset, kT0, 0.0)

        def windowed(g, x, x_ready, free):
            m_xt = s_xt.dma(SP, sp.dma_start, xT0, io["xT"][g].rearrange("p (c t) -> p c t", c=DC), after=free)
            yield
            yield
            PE.wait(m_xt)
            bank, m = project(chunked("wq0"), xT0)
            m_q = copy_out(qT0, blocks(bank.tensor[:, :]), bank, (m, *free))
            bank, m = project(chunked("wk0"), xT0)
            m_k = copy_out(kT0.rearrange("p c b t -> p (c b) t")[:, :, PAD:PAD + P],
                           bank.tensor[:, :].rearrange("p (n t) -> p n t", t=P), bank, (m, m_pads))
            yield
            bank, m = project_rows(chunked("wv0"), xT0)
            m_v = copy_out(vw[:, PAD, :], bank.tensor[:, :], bank, (m,))
            for wi in range(WIN):
                o = wi - PAD
                if o:
                    lo, hi = max(0, -o), P - max(0, o)
                    m_sh = s_shift.dma(SP, sp.dma_start, vw[lo:hi, wi, :], vw[lo + o:hi + o, PAD, :],
                                       after=(m_v, m_pads))
            hbank = take()
            prod_free = [list(free) for _ in prods]
            for wi in range(WIN):
                r = wi % 4
                stream, eng = (POOL, pool) if wi in POOL_SCORES else (DVE, dve)
                m = stream.put(eng.tensor_tensor, prods[r].rearrange("p (n t) -> p n t", t=P),
                               qT0.rearrange("p c (b t) -> p (c b) t", t=P),
                               kT0.rearrange("p c b t -> p (c b) t")[:, :, wi:wi + P], ALU.mult,
                               after=(m_q, m_k, *prod_free[r]))
                PE.wait(m)
                for c in range(DC):
                    at = SLIDE - (wi * H + c * HC)
                    m = PE.put(pe.matmul, hbank.tensor[0:WIN * H, 0:T], w["headsum"][:, at:at + WIN * H],
                               prods[r][:, c * T:(c + 1) * T], start=wi + c == 0, stop=wi + c == WIN, mark=c == DC - 1)
                prod_free[r] = [m]
                if wi % 2:
                    yield
            m = copy_out(sT0[0:WIN * H], hbank.tensor[0:WIN * H, 0:T], hbank, (m,))
            yield
            sbank = take()
            scores = sbank.tensor[:, 0:GB * WIN * H].rearrange("p (b w h) -> p b w h", b=GB, w=WIN)
            PE.wait(m)
            for b in range(GB):
                m = PE.put(pe.transpose, sbank.tensor[:, b * WIN * H:(b + 1) * WIN * H], sT0[0:WIN * H, b * P:(b + 1) * P],
                           I[0:WIN * H, 0:WIN * H], mark=b == GB - 1)
            e4 = e0.rearrange("p (b w h) -> p b w h", b=GB, w=WIN)
            e_head = e4.rearrange("p b w h -> p b h w")
            mx, den1, den2 = (den0[:, i, :].rearrange("p (b h) -> p b h", b=GB) for i in range(3))
            m = DVE.put(dve.tensor_reduce, mx, scores.rearrange("p b w h -> p b h w"), X, ALU.max, after=(m,))
            m = DVE.put(dve.tensor_tensor, e4, scores, bc(mx, 2, WIN), ALU.subtract, after=(m,))
            banks.give(sbank, m)
            m = SC.put(act.activation, e0, e0, ACT.Exp, scale=float(DH) ** -0.5, after=(m,))
            yield
            m1 = DVE.put(dve.tensor_reduce, den1, e_head, X, ALU.add, after=(m,))
            m = DVE.put(dve.tensor_tensor, e0.rearrange("p (b n) -> p b n", b=GB), e0.rearrange("p (b n) -> p b n", b=GB),
                        bc(conn[:, :], 1, GB), ALU.mult, after=(m1, *early_done))
            m = DVE.put(dve.tensor_reduce, den2, e_head, X, ALU.add, after=(m,))
            m = DVE.put(dve.scalar_tensor_tensor, den0[:, 0, :], den0[:, 1, :], 1e-9, den0[:, 2, :], ALU.mult, ALU.add,
                        after=(m,))
            m = DVE.put(dve.reciprocal, den0[:, 0, :], den0[:, 0, :], after=(m,))
            m_fw = DVE.put(dve.tensor_tensor, e4, e4, bc(mx, 2, WIN), ALU.mult, after=(m,))
            yield
            weighted = []
            for wi in (0, 1, 2, 3, 4, 5, 6):
                stream, eng = (POOL, pool) if wi in POOL_VALUES else (DVE, dve)
                v4 = vw[:, wi, :].rearrange("p (b h d) -> p b h d", b=GB, h=H)
                weighted.append(stream.put(eng.tensor_tensor, v4, v4, bc(e4[:, :, wi, :], 3, DH), ALU.mult,
                                           after=(m_fw, m_v, m_sh)))
                if wi % 2:
                    yield
            part = [vw[:, wi, :] for wi in range(WIN)] + prods[0:3]
            done = weighted + [None] * 3
            for step, (dst, i, j) in enumerate(SUMS):
                stream, eng = (POOL, pool) if step in POOL_SUMS else (DVE, dve)
                done[dst] = stream.put(eng.tensor_tensor, part[dst], part[i], part[j], ALU.add,
                                       after=(done[i], done[j], *prod_free[dst - WIN]))
                if step % 2:
                    yield
            bank = take()
            PE.wait(done[WIN])
            for c in range(DC):
                for b in range(GB):
                    at = b * D + c * P
                    m = tp(bank.tensor[:, c * T + b * P:c * T + (b + 1) * P], prods[0][:, at:at + P], mark=c + b == 2)
            m = copy_out(qT0, blocks(bank.tensor[:, :]), bank, (m,))
            yield
            PE.wait(m)
            bank, m = project_rows(chunked("wo0"), qT0, bias_row(0))
            yield
            return (yield from norm(x, bank, (m, *x_ready)))

        def cross(g, x, ready, free):
            area = areas["B"]
            area.reset()
            xT, ctxT, ka, v = (area.carve(W2) for _ in range(4))
            s, pT = area.carve(T), area.carve(T)
            sums, negmax = area.carve(GB), area.carve(GB)
            m_c = s_ctxb.dma(SP, sp.dma_start, ctxT, io["ctxT"][g], after=free)
            SC.wait(*free)
            yield
            yield
            PE.wait(m_c)
            bank, m = project(w_cross, blocks(ctxT))
            m_ka = copy_out(ka, bank.tensor[:, :], bank, (m,))
            bank, m = project_rows(chunked("wv0x"), blocks(ctxT))
            m_v = copy_out(v, bank.tensor[:, :], bank, (m,))
            yield
            m_x = to_channels(x, ready, xT)
            yield
            bank = take()
            PE.wait(m_x, m_ka)
            xT, ka = blocks(xT), blocks(ka)
            for b in range(GB):
                m = mm(bank.tensor[:, b * P:(b + 1) * P], [(xT[:, c, b * P:(b + 1) * P], ka[:, c, b * P:(b + 1) * P])
                                                            for c in range(DC)], mark=b == 1)
            s3 = blocks(s, GB)
            m = DVE.put(dve.scalar_tensor_tensor, s3, blocks(bank.tensor[:, 0:T], GB),
                        float(D) ** -0.5, bc(w["xmask"][:, :], 1, GB), ALU.mult, ALU.add, after=(m, *free))
            banks.give(bank, m)
            yield
            m = yield from key_softmax(s3, (m,), sums, negmax)
            bank = take()
            for b in range(GB):
                mt = tp(bank.tensor[:, b * P:(b + 1) * P], s3[:, b, :], after=(m,), mark=b == 1)
            m = copy_out(pT, bank.tensor[:, 0:T], bank, (mt,))
            yield
            bank = take()
            PE.wait(m, m_v)
            more = bias_row(1)
            for b in range(GB):
                m = mm(bank.tensor[:, b * D:(b + 1) * D], [(pT[:, b * P:(b + 1) * P], v[:, b * D:(b + 1) * D])] + more(b),
                       mark=b == 1)
            yield
            return (yield from norm(x, bank, (m,)))

        def experts(g, x, ready):
            area = areas["B"]
            area.reset()
            xT_, pick, cs, qkv = (area.carve(n) for n in (W2, T, EJ * 2 * ROT, EJ * 3 * HP))
            turn, qkT, s, pT, pickT = (area.carve(n) for n in (EJ * 2 * ROT, EJ * 2 * P, EJ * P, EJ * P, GB * EJ * P))
            av, up = area.carve(T), area.carve(EJ * D)
            sig, r1, r2 = area.carve(P), area.carve(P), area.carve(P)
            m8, sigt, sums, negmax = area.carve(16), area.carve(GB * NE), area.carve(EJ), area.carve(EJ)
            xT = blocks(xT_)
            m_x = to_channels(x, ready, xT_)
            yield
            R = 32 * GB
            bank = take()
            PE.wait(m_x)
            for b in range(GB):
                m = mm(bank.tensor[32 * b:32 * b + 32, 0:P], [(wr_pad[:, c, :], xT[:, c, b * P:(b + 1) * P]) for c in range(DC)],
                       mark=b == 1)
            m = copy_out(sig[0:R], bank.tensor[0:R, 0:P], bank, (m,), ACT.Exp, scale=-1.0)
            yield
            m = DVE.put(dve.tensor_scalar, sig[0:R], sig[0:R], 1.0, None, ALU.add, after=(m,))
            m_sig = DVE.put(dve.reciprocal, sig[0:R], sig[0:R], after=(m,))
            m = DVE.put(dve.max, m8[0:R, 0:8], sig[0:R], after=(m_sig,))
            m = DVE.put(dve.match_replace, r1[0:R], m8[0:R, 0:8], sig[0:R], -1.0, after=(m,))
            m = DVE.put(dve.max, m8[0:R, 8:16], r1[0:R], after=(m,))
            m = DVE.put(dve.match_replace, r2[0:R], m8[0:R, 8:16], r1[0:R], -1.0, after=(m,))
            m = DVE.put(dve.tensor_scalar, r1[0:R], r2[0:R], 0.0, None, ALU.is_lt, after=(m,))
            m = DVE.put(dve.tensor_tensor_scan, r2[0:R], onesb[0:R, :], r1[0:R], 0.0, ALU.mult, ALU.add, after=(m,))
            m = DVE.put(dve.tensor_tensor, r2[0:R], r2[0:R], r1[0:R], ALU.mult, after=(m,))
            yield
            bank = take()
            PE.wait(m_sig, m)
            PE.put(pe.transpose, bank.tensor[:, 0:R], r2[0:R], I[0:R, 0:R], mark=False)
            m = PE.put(pe.transpose, bank.tensor[:, P:P + R], sig[0:R], I[0:R, 0:R])
            rank4 = blocks(bank.tensor[:, 0:R], GB)[:, :, 0:NE]
            sig4 = blocks(bank.tensor[:, P:P + R], GB)[:, :, 0:NE]
            by_slot = "p (e b s) -> p b e s"
            pick4 = pick.rearrange(by_slot, e=NE, b=GB)
            m_sg = DVE.put(dve.tensor_copy, blocks(sigt, GB), sig4, after=(m,))
            m_pick = DVE.put(dve.tensor_tensor, pick4, bc(rank4, 3, NS), bc(bc(w["iota16"][:, :], 1, NE), 1, GB),
                             ALU.is_equal)
            banks.give(bank, m_pick)
            for b in range(GB):
                m_picked = POOL.put(pool.tensor_tensor, picked[:, b, :].rearrange(by_slot, e=NE, b=GB)[:, b], pick4[:, b],
                                    bc(blocks(sigt, GB)[:, b], 2, NS), ALU.mult, after=(m_pick, m_sg))
            yield
            xg = xT_.rearrange("p (c e b s) -> p c b e s", c=DC, e=NE, b=GB)
            PE.wait(m_pick)
            bank = take()
            for c in range(DC):
                for b in range(GB):
                    m = mm(bank.tensor[:, c * T + b * P:c * T + (b + 1) * P],
                           [(x[:, b, c * P:(c + 1) * P], pick4[:, b])], mark=c + b == 2)
            for c in range(DC):
                m_xg = SC.put(act.activation, xg[:, c], bank.tensor[:, c * T:(c + 1) * T].rearrange("p (b e s) -> p b e s", b=GB, e=NE),
                              ACT.Copy, after=(m,))
            banks.give(bank, m_xg)
            bank = take()
            for j in range(EJ):
                m = mm(bank.tensor[:, j * 2 * ROT:(j + 1) * 2 * ROT], [(pick[:, j * P:(j + 1) * P], w["cos_sin"][:, :])],
                       mark=j == EJ - 1)
            m_cs = copy_out(cs, bank.tensor[:, 0:EJ * 2 * ROT], bank, (m,))
            yield
            wq = w["wqkv_e"][:, :].rearrange("p (c e n) -> p c e n", c=DC, e=NE)
            xgf = xT_.rearrange("p (c e n) -> p c e n", c=DC, e=NE)
            qkv3 = blocks(qkv, EJ)
            PE.wait(m_xg)
            for j in range(EJ):
                bank = take()
                for q in range(EQ):
                    e = j * EQ + q
                    m = mm(bank.tensor[ES * q:ES * (q + 1), 0:3 * HP], [(xgf[:, c, e, :], wq[:, c, e, :]) for c in range(DC)],
                           mark=q == EQ - 1)
                    yield
                m_qkv = copy_out(qkv3[:, j, :], bank.tensor[:, 0:3 * HP], bank, (m,))
            yield
            a = qkv3[:, :, 0:2 * HP].rearrange("p j (i n) -> p j i n", i=2)[:, :, :, 0:ROT]
            turn4 = turn.rearrange("p (j i n) -> p j i n", j=EJ, i=2)
            cs3, half = blocks(cs, EJ), ROT // 2
            DVE.wait(m_qkv, m_cs)
            for h in range(2):
                dst, other = slice(h * half, (h + 1) * half), slice((1 - h) * half, (2 - h) * half)
                m1 = DVE.put(dve.tensor_tensor, turn4[:, :, :, dst], a[:, :, :, other],
                             bc(cs3[:, :, ROT + h * half:ROT + (h + 1) * half], 2, 2), ALU.mult)
            m2 = DVE.put(dve.tensor_tensor, a, a, bc(cs3[:, :, 0:ROT], 2, 2), ALU.mult, after=(m1,))
            m_rot = DVE.put(dve.tensor_tensor, a, a, turn4, ALU.add, after=(m2,))
            yield
            bank = take()
            for j in range(EJ):
                for i in range(2):
                    at = 2 * j + i
                    m = tp(bank.tensor[:, at * P:(at + 1) * P], qkv3[:, j, i * HP:(i + 1) * HP], after=(m_rot,), mark=at == 3)
            m = copy_out(qkT, bank.tensor[:, :], bank, (m,))
            yield
            bank = take()
            PE.wait(m)
            for j in range(EJ):
                m = mm(bank.tensor[:, j * P:(j + 1) * P], [(qkT[:, 2 * j * P:(2 * j + 1) * P], qkT[:, (2 * j + 1) * P:(2 * j + 2) * P])],
                       mark=j == EJ - 1)
            s3 = blocks(s, EJ)
            m = DVE.put(dve.scalar_tensor_tensor, s3, blocks(bank.tensor[:, 0:EJ * P], EJ),
                        float(HP) ** -0.5, bc(w["blk"][:, :], 1, EJ), ALU.mult, ALU.add, after=(m,))
            banks.give(bank, m)
            yield
            m = yield from key_softmax(s3, (m,), sums, negmax)
            bank = take()
            for j in range(EJ):
                mt = tp(bank.tensor[:, j * P:(j + 1) * P], s3[:, j, :], after=(m,), mark=j == EJ - 1)
            m = copy_out(pT, bank.tensor[:, 0:EJ * P], bank, (mt,))
            yield
            bank = take()
            PE.wait(m)
            for j in range(EJ):
                m = mm(bank.tensor[:, j * P:(j + 1) * P], [(qkv3[:, j, 2 * HP:3 * HP], pT[:, j * P:(j + 1) * P])], mark=j == EJ - 1)
            m_av = copy_out(av, bank.tensor[:, 0:EJ * P], bank, (m,))
            bank = take()
            for b in range(GB):
                for j in range(EJ):
                    at = b * EJ + j
                    m = tp(bank.tensor[:, at * P:(at + 1) * P], picked[:, b, j * P:(j + 1) * P], after=(m_picked,), mark=at == 3)
            m_pt = copy_out(pickT, bank.tensor[:, :], bank, (m,))
            yield
            wo = w["wo_e"][:, :].rearrange("p (e n) -> p e n", e=NE)
            PE.wait(m_av)
            bank = take()
            for j in range(EJ):
                for q in range(EQ):
                    e = j * EQ + q
                    m = mm(bank.tensor[ES * q:ES * (q + 1), j * D:(j + 1) * D], [(av[:, e * ES:(e + 1) * ES], wo[:, e, :])],
                           mark=e == NE - 1)
                    if q % 2:
                        yield
            m_u = copy_out(up, bank.tensor[:, :], bank, (m,))
            yield
            bank = take()
            PE.wait(m_pt, m_u)
            for b in range(GB):
                m = mm(bank.tensor[:, b * D:(b + 1) * D],
                       [(pickT[:, (b * EJ + j) * P:(b * EJ + j + 1) * P], up[:, j * D:(j + 1) * D]) for j in range(EJ)],
                       mark=b == 1)
            yield
            return (yield from norm(x, bank, (m,)))

        def decayed(g, x, ready, free):
            area = areas["C"]
            area.reset()
            xT, yT, v = (area.carve(W2) for _ in range(3))
            s, pT = area.carve(T), area.carve(T)
            sums, negmax, part = area.carve(GB), area.carve(GB), area.carve(GB)
            SC.wait(*free)
            DVE.wait(*free)
            m_x = to_channels(x, ready, xT)
            xT = blocks(xT)
            yield
            PE.wait(m_x)
            bank, m = project(w_qk, xT)
            for c in range(DC):
                m_y = SC.put(act.activation, yT[:, c * T:(c + 1) * T], bank.tensor[:, c * T:(c + 1) * T], ACT.Identity,
                             bias=b_key[:, c:c + 1], after=(m,))
            banks.give(bank, m_y)
            bank, m = project_rows(w_vp, xT)
            m_v = copy_out(v, bank.tensor[:, :], bank, (m,))
            yield
            yT = blocks(yT)
            bank = take()
            PE.wait(m_y)
            for b in range(GB):
                mm(bank.tensor[:, T + b:T + b + 1], [(xT[:, c, b * P:(b + 1) * P], u_row[:, c:c + 1]) for c in range(DC)])
                m = mm(bank.tensor[:, b * P:(b + 1) * P], [(yT[:, c, b * P:(b + 1) * P], xT[:, c, b * P:(b + 1) * P])
                                                            for c in range(DC)], mark=b == 1)
            m1 = DVE.put(dve.tensor_scalar, part, bank.tensor[:, T:T + GB], bb[:, 0:1], None, ALU.add, after=(m,))
            s3 = blocks(s, GB)
            for b in range(GB):
                m = DVE.put(dve.scalar_tensor_tensor, s3[:, b, :], bank.tensor[:, b * P:(b + 1) * P], part[:, b:b + 1],
                            decay[:, :], ALU.add, ALU.mult, after=(m1,))
            banks.give(bank, m)
            yield
            m = yield from key_softmax(s3, (m,), sums, negmax)
            bank = take()
            for b in range(GB):
                mt = tp(bank.tensor[:, b * P:(b + 1) * P], s3[:, b, :], after=(m,), mark=b == 1)
            m = copy_out(pT, bank.tensor[:, 0:T], bank, (mt,))
            yield
            bank = take()
            PE.wait(m, m_v)
            more = bias_row(2)
            for b in range(GB):
                m = mm(bank.tensor[:, b * D:(b + 1) * D], [(pT[:, b * P:(b + 1) * P], v[:, b * D:(b + 1) * D])] + more(b),
                       mark=b == 1)
            yield
            return (yield from norm(x, bank, (m,)))

        def memory(g, x, ready, free):
            area = areas["D"]
            area.reset()
            xT_, ctxT, qT = (area.carve(W2) for _ in range(3))
            att = blocks(xT_, GB)
            KV = P + DH + 1
            kv = blocks(area.carve(GB * KV), GB)
            o, oT = area.carve(T), area.carve(T)
            key = area.carve(GB * 2 * P).rearrange("p (b par k) -> p b par k", b=GB, par=2)
            mv = blocks(area.carve(GB * (DH + 1)), GB)
            pT = area.carve(H * P)
            m8, i8 = area.carve(8 * GB), area.carve(8 * GB)
            negT, rec = area.carve(GB * P // 2).bitcast(BF16), area.carve(H)
            rest = area.carve(GB * H)
            rounded = area.carve(GB * H // 2).bitcast(BF16)
            m_c = s_ctxd.dma(SP, sp.dma_start, ctxT, io["ctxT"][g], after=free)
            for s in (SC, DVE, POOL):
                s.wait(*free)
            m_one = POOL.put(pool.memset, kv[:, :, P + DH:KV], 1.0)
            yield
            wk, wv = chunked("wkrep"), chunked("wv1x")
            ctxT = blocks(ctxT)
            PE.wait(m_c)
            bank = take()
            for b in range(GB):
                mm(bank.tensor[:, b * D:b * D + P], [(ctxT[:, c, b * P:(b + 1) * P], wk[:, c, :]) for c in range(DC)])
                m = mm(bank.tensor[:, b * D + P:b * D + P + DH], [(ctxT[:, c, b * P:(b + 1) * P], wv[:, c, :])
                                                                  for c in range(DC)], mark=b == 1)
            m_kv = copy_out(kv[:, :, 0:P + DH], blocks(bank.tensor[:, :], GB)[:, :, 0:P + DH], bank, (m,))
            m_x = to_channels(x, ready, xT_)
            yield
            PE.wait(m_x)
            bank, m = project(chunked("wq1x"), blocks(xT_))
            m_q = copy_out(qT, bank.tensor[:, :], bank, (m,))
            qT = blocks(qT)
            yield
            bank = take()
            PE.wait(m_q)
            for b in range(GB):
                m = mm(bank.tensor[:, b * P:(b + 1) * P], [(qT[:, c, b * P:(b + 1) * P], ctxT[:, c, b * P:(b + 1) * P])
                                                            for c in range(DC)], mark=b == 1)
            m = copy_out(o, bank.tensor[:, 0:T], bank, (m,))
            for b in range(GB):
                m = DVE.put(dve.max, m8[:, 8 * b:8 * b + 8], o[:, b * P:(b + 1) * P], after=(m,))
            i8u = i8.bitcast(U32)
            for b in range(GB):
                m = DVE.put(dve.max_index, i8u[:, 8 * b:8 * b + 8], m8[:, 8 * b:8 * b + 8], o[:, b * P:(b + 1) * P],
                            after=(m,))
            m = DVE.put(dve.tensor_tensor, blocks(o, GB), bc(blocks(i8u, GB)[:, :, 0], 2, P),
                        bc(w["iota128"][:, :], 1, GB), ALU.is_equal, after=(m,))
            yield
            bank = take()
            for b in range(GB):
                mt = tp(bank.tensor[:, b * P:(b + 1) * P], o[:, b * P:(b + 1) * P], after=(m,), mark=b == 1)
            m_ot = copy_out(oT, bank.tensor[:, 0:T], bank, (mt,))
            yield
            bank = take()
            PE.wait(m_ot, m_kv, m_one)
            for b in range(GB):
                m = mm(bank.tensor[:, b * P:(b + 1) * P], [(kv[:, b, 0:P], oT[:, b * P:(b + 1) * P])], mark=b == 1)
            m_key = None
            for b in range(GB):
                m_key = DVE.put(dve.tensor_tensor, key[:, b], bc(bank.tensor[:, b * P:(b + 1) * P], 1, 2),
                                bc(w["parity"][:, :], 2, P), ALU.mult, after=(m,))
            banks.give(bank, m_key)
            bank = take()
            for b in range(GB):
                m = mm(bank.tensor[:, b * (DH + 1):(b + 1) * (DH + 1)], [(oT[:, b * P:(b + 1) * P], kv[:, b, P:KV])],
                       mark=b == 1)
            m_mv = copy_out(mv, blocks(bank.tensor[:, 0:GB * (DH + 1)], GB), bank, (m,))
            yield
            p_free, m_att = [], []
            for b in range(GB):
                for r in range(4):
                    rows = slice(32 * r, 32 * r + 32)
                    bank = take()
                    PE.wait(m_key)
                    for c in range(DC):
                        m = mm(bank.tensor[:, c * 2 * P:(c + 1) * 2 * P],
                               [(qT[rows, c, b * P:(b + 1) * P], key[rows, b].rearrange("p par k -> p (par k)"))], mark=c == 1)
                    m_top = DVE.put(dve.tensor_reduce, neg_top[:, b, 0, 4 * r:4 * r + 4], blocks(bank.tensor[:, :], 4), X,
                                    ALU.max, negate=True, after=(m, *neg_free))
                    banks.give(bank, m_top)
                    yield
            rest, rounded = blocks(rest, GB), blocks(rounded, GB)
            m = m_top
            for k in range(2):
                m = DVE.put(dve.tensor_copy, rounded, neg_top[:, :, k, :], after=(m,))
                m = DVE.put(dve.tensor_tensor, neg_top[:, :, k + 1, :], neg_top[:, :, k, :], rounded, ALU.subtract, after=(m,))
            bank = take()
            PE.wait(m)
            for b in range(GB):
                m = tp(bank.tensor[0:3 * H, b * P:(b + 1) * P], neg_top[:, b].rearrange("p k h -> p (k h)"),
                       mark=b == GB - 1)
            neg_free[:] = [m]
            m_nt = copy_out(negT[0:3 * H], bank.tensor[0:3 * H, 0:T], bank, (m,))
            yield
            for b in range(GB):
                PE.wait(m_nt)
                m_p = []
                for r in range(4):
                    rows = slice(32 * r, 32 * r + 32)
                    bank = take()
                    for c in range(DC):
                        for par in range(2):
                            at = 2 * c + par
                            m = mm(bank.tensor[:, at * P:(at + 1) * P],
                                   [(key[rows, b, par, :], qT[rows, c, b * P:(b + 1) * P]),
                                    (head_of[0:3 * H, 4 * r + at:4 * r + at + 1].broadcast_to([3 * H, P]),
                                     negT[0:3 * H, b * P:(b + 1) * P])], mark=at == 3)
                            if par:
                                yield
                    m_p.append(SC.put(act.activation, pT[:, r * 4 * P:(r + 1) * 4 * P], bank.tensor[:, :], ACT.Exp,
                                      scale=float(DH) ** -0.5, after=(m, *p_free)))
                    banks.give(bank, m_p[-1])
                bank = take()
                PE.wait(m_mv)
                for r in range(4):
                    PE.wait(m_p[r])
                    for c in range(DC):
                        for par in range(2):
                            head, at = c * HC + 2 * r + par, 4 * r + 2 * c + par
                            m = mm(bank.tensor[:, head * (DH + 1):(head + 1) * (DH + 1)],
                                   [(pT[:, at * P:(at + 1) * P], mv[:, b, :])], mark=at == H - 1)
                        yield
                p_free = [m]
                a3 = bank.tensor[:, 0:H * (DH + 1)].rearrange("p (h n) -> p h n", h=H)
                m1 = DVE.put(dve.reciprocal, rec, a3[:, :, DH], after=(m,))
                m1 = DVE.put(dve.tensor_tensor, att[:, b, :].rearrange("p (h d) -> p h d", h=H), a3[:, :, 0:DH],
                             bc(rec, 2, DH), ALU.mult, after=(m1,))
                DVE.wait(m1)
                banks.give(bank, m1)
                m_att.append(m1)
                yield
            aT = ctxT
            m_a = to_channels(att, m_att, aT.rearrange("p c t -> p (c t)"))
            yield
            PE.wait(m_a)
            bank, m = project_rows(chunked("wc1x"), aT)
            yield
            return (yield from norm(x, bank, (m,)))

        neg_free = []

        def token_rows(scale, ready, dg):
            bank, m = take(), ready
            for b in range(GB):
                m = DVE.put(dve.tensor_scalar, dg, I, scale[:, b:b + 1], None, ALU.mult, after=(m,))
                m = mm(bank.tensor[:, b * P:(b + 1) * P], [(onesb[:, :], dg)], after=(m,), mark=True)
            return bank, m

        def feed_forward(g, x, ready, free):
            area = areas["E"]
            area.reset()
            xq, xqT = area.carve(W2), area.carve(W2 // 2).bitcast(BF16)
            dg, tscale = area.carve(P), area.carve(T)
            NJ = HJ // 2
            c_ = [area.carve(W2) for _ in range(NJ)]
            n2 = [area.carve(W2 // 2).bitcast(BF16) for _ in range(NJ)]
            th, tap, top = [area.carve(W2) for _ in range(2)], xq, area.carve(W2)
            am, sc1, rs1, rs2 = (area.carve(GB) for _ in range(4))
            POOL.wait(*free)
            SC.wait(*free)
            m = DVE.put(dve.tensor_reduce, am, x[:, :, :], X, ALU.max, apply_absolute_value=True, after=(*ready, *free))
            m = DVE.put(dve.tensor_scalar, am, am, 1e-5, None, ALU.max, after=(m,))
            m1 = DVE.put(dve.reciprocal, sc1, am, after=(m,))
            m1 = DVE.put(dve.tensor_scalar, sc1, sc1, 127.0, None, ALU.mult, after=(m1,))
            m2 = DVE.put(dve.tensor_scalar, rs1, am, wmean[:, 0:1], 1.0 / 127.0, ALU.mult, ALU.mult, after=(m1,))
            DVE.wait(m2)
            for b in range(GB):
                m = DVE.put(dve.tensor_scalar, xq[:, b * D:(b + 1) * D], x[:, b, :], sc1[:, b:b + 1], MAGIC, ALU.mult, ALU.add)
            DVE.wait(m)
            for b in range(GB):
                m = DVE.put(dve.tensor_scalar, xq[:, b * D:(b + 1) * D], xq[:, b * D:(b + 1) * D], MAGIC, None, ALU.subtract)
            yield
            bank, m_ts = token_rows(rs1, m2, dg)
            m_ts = copy_out(tscale, bank.tensor[:, 0:T], bank, (m_ts,))
            m_xq = to_channels(blocks(xq, GB), [m, m], xqT)
            xqT = blocks(xqT)
            yield
            PE.wait(m_xq)
            cw = w["convw"][:, :].rearrange("p (j k) -> p j k", k=3)
            m_top, tap_free = None, [m_xq]
            for jj in range(NJ):
                bank = take()
                for i in range(2):
                    j = 2 * jj + i
                    m = mm(bank.tensor[:, i * T:(i + 1) * T], [(w1q[:, c, j * P:(j + 1) * P], xqT[:, c, :]) for c in range(DC)],
                           mark=i == 1)
                m = DVE.put(dve.tensor_tensor, blocks(th[jj % 2], 2), blocks(bank.tensor[:, :], 2), bc(tscale, 1, 2), ALU.mult,
                            after=(m, m_ts) + ((m_top,) if m_top else ()))
                banks.give(bank, m)
                yield
                h4 = th[jj % 2].rearrange("p (i b t) -> p i b t", i=2, b=GB)
                c4 = c_[jj].rearrange("p (i b t) -> p i b t", i=2, b=GB)
                t4 = tap.rearrange("p (i b t) -> p i b t", i=2, b=GB)
                for i in range(2):
                    j = 2 * jj + i
                    m_c = SC.put(act.activation, c4[:, i], h4[:, i], ACT.Identity, bias=w["convb"][:, j:j + 1],
                                 scale=cw[:, j, 1:2], after=(m,))
                for i in range(2):
                    m_t = SC.put(act.activation, t4[:, i, :, 0:P - 1], h4[:, i, :, 1:P], ACT.Copy, scale=cw[:, 2 * jj + i, 2:3],
                                 after=tap_free)
                for i in range(2):
                    m = DVE.put(dve.scalar_tensor_tensor, c4[:, i, :, 1:P], h4[:, i, :, 0:P - 1], cw[:, 2 * jj + i, 0:1],
                                c4[:, i, :, 1:P], ALU.mult, ALU.add, after=(m_t,))
                yield
                c3, t3 = (t.rearrange("p (n t) -> p n t", t=P)[:, :, 0:P - 1] for t in (c_[jj], tap))
                m = POOL.put(pool.tensor_tensor, c3, c3, t3, ALU.add, after=(m, m_t))
                tap_free = [m]
                yield
                mt = SC.put(act.activation, th[jj % 2], c_[jj], ACT.Tanh, scale=0.5, after=(m,) + ((m_top,) if m_top else ()))
                m = DVE.put(dve.scalar_tensor_tensor, c_[jj], th[jj % 2], 1.0, c_[jj], ALU.add, ALU.mult, after=(mt,))
                if jj == 0:
                    m_top = SC.put(act.activation, top, c_[jj], ACT.Abs, after=(m,))
                else:
                    m = SC.put(act.activation, th[jj % 2], c_[jj], ACT.Abs, after=(m,))
                    m_top = DVE.put(dve.tensor_tensor, top, th[jj % 2], top, ALU.max, after=(m, m_top))
            yield
            bank = take()
            for b in range(GB):
                for i in range(2):
                    at = (2 * b + i) * P
                    m = tp(bank.tensor[:, at:at + P], top[:, i * T + b * P:i * T + (b + 1) * P], after=(m_top,), mark=b + i == 2)
            m = DVE.put(dve.tensor_reduce, am, blocks(bank.tensor[:, :], GB), X, ALU.max, after=(m,))
            banks.give(bank, m)
            m = DVE.put(dve.tensor_scalar, am, am, 0.5, 1e-5, ALU.mult, ALU.max, after=(m,))
            m1 = DVE.put(dve.reciprocal, sc1, am, after=(m,))
            m1 = DVE.put(dve.tensor_scalar, sc1, sc1, 127.0 * 0.5, None, ALU.mult, after=(m1,))
            m_r2 = DVE.put(dve.tensor_scalar, rs2, am, wmean[:, 1:2], 1.0 / 127.0, ALU.mult, ALU.mult, after=(m1,))
            bank, m = token_rows(sc1, m_r2, dg)
            yield
            m_n = []
            for jj in range(NJ):
                m = DVE.put(dve.tensor_tensor, blocks(c_[jj], 2), blocks(c_[jj], 2), bc(bank.tensor[:, 0:T], 1, 2), ALU.mult,
                            after=(m,))
                if jj == NJ - 1:
                    banks.give(bank, m)
                m_n.append(DVE.put(dve.tensor_scalar, n2[jj], c_[jj], MAGIC, MAGIC, ALU.add, ALU.subtract, after=(m,)))
                if jj % 2:
                    yield
            bank = take()
            for b in range(GB):
                m = mm(bank.tensor[:, b * D:(b + 1) * D],
                       [(n2[j // 2][:, (j % 2) * T + b * P:(j % 2) * T + (b + 1) * P], w2q[:, j, :]) for j in range(HJ)],
                       after=m_n, mark=b == 1)
            yield
            return (yield from norm(x, bank, (m, m_r2), rs2))

        x_out = [[] for _ in range(NX)]
        ended = {}

        def station_a(g):
            if g == 0:
                yield from setup_early()
            src = io["x"][g * T:(g + 1) * T, :].rearrange("(b t) d -> t b d", b=GB)
            m = s_x[g % NX].dma(SP, sp.dma_start, xs[g % NX][:, :, :], src, after=x_out[g % NX])
            ended["A", g] = yield from windowed(g, xs[g % NX], [m], ended.get(("A", g - 1), []))

        def station_b(g):
            if g < 0:
                return (yield from setup_late())
            x = xs[g % NX]
            r = yield from cross(g, x, ended["A", g], ended.get(("B", g - 1), late_done))
            ended["B", g] = yield from experts(g, x, r)

        def station_c(g):
            ended["C", g] = yield from decayed(g, xs[g % NX], ended["B", g], ended.get(("C", g - 1), late_done))

        def station_d(g):
            ended["D", g] = yield from memory(g, xs[g % NX], ended["C", g], ended.get(("D", g - 1), late_done))

        def station_e(g):
            x = xs[g % NX]
            r = yield from feed_forward(g, x, ended["D", g], ended.get(("E", g - 1), late_done))
            ended["E", g] = r
            m = s_out[g % NX].dma(SP, sp.dma_start, out[g * T:(g + 1) * T, :].rearrange("(b t) d -> t b d", b=GB), x[:, :, :],
                                  after=r)
            x_out[g % NX] = [m]

        stations = [("E", station_e, 4), ("D", station_d, 3), ("C", station_c, 2), ("B", station_b, 1), ("A", station_a, 0)]
        steps = {"A": 26, "B": 30, "C": 10, "D": 26, "E": 20}
        for rnd in range(NG + len(stations) - 1):
            work = []
            for name, station, lag in stations:
                g = rnd - lag
                if 0 <= g < NG or (name == "B" and g == -1):
                    work.append([name, station(g), 0, steps[name]])
            while work:
                job = min(work, key=lambda j: j[2] / j[3])
                try:
                    next(job[1])
                    job[2] += 1
                except StopIteration:
                    if rnd:
                        steps[job[0]] = job[2] + 1
                    work.remove(job)
        for marks in x_out:
            SP.wait(*marks)

        with nc.Block() as block:
            @block.sync
            def _(eng):
                SP.play(eng)

            @block.tensor
            def _(eng):
                PE.play(eng)

            @block.vector
            def _(eng):
                DVE.play(eng)

            @block.scalar
            def _(eng):
                SC.play(eng)

            @block.gpsimd
            def _(eng):
                POOL.play(eng)


def constants():
    f = np.float32
    p = np.arange(P)
    half = ROT // 2
    inv = (1.0 / f(10000.0) ** (np.arange(half, dtype=f) * f(2.0) / f(ROT))).astype(f)
    ang = (p.astype(f)[:, None] * inv).astype(f)
    cos, sin = np.cos(ang).astype(f), np.sin(ang).astype(f)
    diff = p[:, None] - p[None, :]
    bit = [((np.maximum(diff, 0) >> i) & 1).astype(f) for i in range(7)]
    q, k = p[:, None], p[None, :]
    same = (q // NS == k // NS) & (k <= q)
    pos = np.zeros((P, 1), f)
    pos[:WIN * H, 0] = np.repeat(np.linspace(0.0, 1.0, WIN, dtype=f), H)
    return {
        "ident": np.eye(P, dtype=f),
        "headsum": (p[:, None] // DH == np.arange(-SLIDE, HC + SLIDE)[None, :]).astype(f),
        "parity": (p[:, None] % 32 // DH == np.arange(2)[None, :]).astype(f),
        "head_of": (p[:, None] % H == np.arange(H)[None, :]).astype(f),
        "part": (p[:, None] % 32 == np.arange(3)[None, :]).astype(f),
        "iota16": np.tile(np.arange(1, NS + 1, dtype=f), (P, 1)),
        "iota128": np.tile(np.arange(P, dtype=f), (P, 1)),
        "pos": pos,
        "cos_sin": np.concatenate([cos, cos, -sin, sin], 1),
        "blk": np.where(same, f(0), f(FAR)).astype(f),
        "bits": np.concatenate(bit + [1 - b for b in bit] + [(diff >= 0).astype(f)], 1),
    }


def laid_out(a):
    def rows(m):
        c = m.shape[0] // P
        return m.reshape(c, P, -1).transpose(1, 0, 2).reshape(P, -1)

    def per_head(m):
        return np.tile(m.reshape(H, -1), (WIN, 1))

    def by_group(m):
        return m.reshape(NG, T, DC, P).transpose(0, 3, 2, 1).reshape(NG, P, DC * T)

    bq = a["L1_attn_bqkv"]
    bias_rows = np.zeros((P, D), np.float32)
    for i, name in enumerate(("L0_attn_bo", "L0_xattn_bv", "L1_attn_bproj")):
        bias_rows[32 * i:32 * i + 3] = a[name]
    wkv = a["L1_xattn_Wkv"]
    return {
        "x": a["x"].reshape(NSEQ * P, D), "xT": by_group(a["x"]), "ctxT": by_group(a["ctx_1024"]),
        "wq0": rows(a["L0_attn_wq"].T), "wk0": rows(a["L0_attn_wk"].T), "wv0": rows(a["L0_attn_wv"].T),
        "wo0": rows(a["L0_attn_wo"].T),
        "c1": per_head(a["L0_attn_cw1"]), "b1": per_head(a["L0_attn_cb1"]), "c2": per_head(a["L0_attn_cw2"]),
        "b2": per_head(a["L0_attn_cb2"]), "c3": per_head(a["L0_attn_cw3"]), "b3": per_head(a["L0_attn_cb3"]),
        "raw_q": rows(a["L0_xattn_Wq"]), "raw_k": rows(a["L0_xattn_Wk"]), "wv0x": rows(a["L0_xattn_Wv"].T),
        "xmask": a["mask_SxS2_fk0"],
        "wr": rows(a["L0_ffn_Wr"].T),
        "wqkv_e": a["L0_ffn_Wqkv"].reshape(NE, DC, P, 3 * HP).transpose(2, 1, 0, 3).reshape(P, -1),
        "wo_e": a["L0_ffn_Wo"].transpose(1, 0, 2).reshape(P, -1),
        "wq1T": rows(a["L1_attn_Wqkv"][:, :D].T), "wk1T": rows(a["L1_attn_Wqkv"][:, D:2 * D].T),
        "wv1T": rows(a["L1_attn_Wqkv"][:, 2 * D:].T), "wp1": rows(a["L1_attn_Wproj"]),
        "bqkv1": bq.reshape(3 * DC, P).T,
        "gamma": np.broadcast_to(a["L1_attn_gamma"].reshape(1, 1), (P, 1)),
        "wq1x": rows(a["L1_xattn_Wq"].T), "wkrep": rows(np.tile(wkv[:DH].T, (1, HC))), "wv1x": rows(wkv[DH:].T),
        "wc1x": rows(a["L1_xattn_Wc"].T),
        "raw1": rows(a["L1_ffn_w1"].T), "raw2": rows(a["L1_ffn_w2"].T),
        "convw": a["L1_ffn_conv_w"].reshape(HJ, P, 3).transpose(1, 0, 2).reshape(P, -1),
        "convb": a["L1_ffn_conv_b"].reshape(HJ, P).T,
        "rows": bias_rows,
    }


def kernel(**inputs):
    import concourse.bacc as bacc
    from concourse.bass_utils import run_bass_kernel_spmd

    nc = bacc.Bacc("TRN2", target_bir_lowering=False, num_devices=1)
    arrays = {**laid_out({k: np.asarray(v) for k, v in inputs.items()}), **constants()}
    arrays = {k: np.ascontiguousarray(v) for k, v in arrays.items()}
    io = {k: nc.dram_tensor(f"in_{k}", v.shape, mybir.dt.from_np(v.dtype), kind="ExternalInput").ap()
          for k, v in arrays.items()}
    out = nc.dram_tensor("y", (NSEQ * P, D), F32, kind="ExternalOutput").ap()
    build(nc, io, out)
    r = run_bass_kernel_spmd(nc, [{f"in_{k}": v for k, v in arrays.items()}], core_ids=[0])
    return r.results[0]["y"].reshape(NSEQ, P, D)
```

```python
from contextlib import ExitStack

import numpy as np

import concourse.bass as bass
from concourse import mybir

F32 = mybir.dt.float32
BF16 = mybir.dt.bfloat16
U32 = mybir.dt.uint32
ALU = mybir.AluOpType
ACT = mybir.ActivationFunctionType
X = mybir.AxisListType.X

P = 128
D = 256
DC = D // P
NSEQ = 32
GB = 2
NG = NSEQ // GB
T = GB * P
H = 16
DH = D // H
HC = H // DC
WIN = 7
PAD = WIN // 2
NE = 8
NS = P // 8
HP = 128
ROT = 64
ES = GB * NS
EQ = P // ES
EJ = NE // EQ
W2 = DC * T
HID = 1024
HJ = HID // P
SLIDE = WIN * H - HC
VC = 32
CH = 32
EPS = 1e-5
MAGIC = 12582912.0
FAR = -1e30
SIGNAL, TRANSFER = 60.0, 2200.0
SLACK = 250.0
LAGS = {"A": 0.0, "B": 1.1, "C": 2.2, "D": 3.3, "E": 4.4, "F": 5.5}


class Mark:

    def __init__(self, sem, value, time):
        self.sem, self.value, self.time = sem, value, time


class Stream:

    def __init__(self, sem, fixed=60, column=0, least=0):
        self.sem, self.count, self.queue, self.seen = sem, 0, [], {}
        self.time, self.fixed, self.column, self.least = 0.0, fixed, column, least
        self.latest = 0.0

    def wait(self, *marks):
        for mark in marks:
            self.time = max(self.time, mark.time)
            if self.seen.get(mark.sem.name, 0) < mark.value:
                self.seen[mark.sem.name] = mark.value
                self.queue.append((None, (mark.sem, mark.value), {}, None))

    def put(self, builder, *args, after=(), mark=True, **kw):
        self.wait(*after)
        self.queue.append((builder, args, kw, (self.sem, 1) if mark else None))
        self.time += self.guess(builder, args)
        self.latest = self.time
        if mark:
            self.count += 1
            return Mark(self.sem, self.count, self.time + SIGNAL)

    def guess(self, builder, args):
        columns = max(int(np.prod(a.shape[1:])) for a in args[0:2] if isinstance(a, bass.AP))
        return self.fixed + self.column * columns

    def play(self, engine):
        for builder, args, kw, inc in self.queue:
            if builder is None:
                engine.wait_ge(*args)
            else:
                instruction = builder(*args, **kw)
                if inc:
                    instruction.then_inc(*inc)


class TensorStream(Stream):
    def guess(self, builder, args):
        columns = int(np.prod(args[0].shape[1:]))
        share = 0.25 if args[1].dtype == BF16 else 0.5 if builder.__name__ == "transpose" else 1
        return max(self.column * columns, self.least) * share


class Landing:

    def __init__(self, sem):
        self.sem, self.count = sem, 0

    def dma(self, stream, start, out, in_, after=()):
        stream.wait(*after)
        self.count += 16
        stream.queue.append((start, (out, in_), {}, (self.sem, 16)))
        stream.latest = stream.time + TRANSFER
        return Mark(self.sem, self.count, stream.latest)


class Bank:

    def __init__(self, tensor):
        self.tensor, self.released = tensor, []


class Banks:

    def __init__(self, tensors):
        self.free = [Bank(t) for t in tensors]

    def take(self):
        bank = min(self.free, key=lambda b: max((m.time for m in b.released), default=0))
        self.free.remove(bank)
        return bank

    def give(self, bank, *marks):
        bank.released = list(marks)
        self.free.append(bank)


class Area:

    def __init__(self, tensor, size):
        self.tensor, self.size, self.at = tensor, size, 0

    def reset(self):
        self.at = 0

    def carve(self, n):
        assert self.at + n <= self.size, (self.at, n, self.size)
        self.at += n
        return self.tensor[:, self.at - n:self.at]


def bc(ap, axis, n):
    v = ap.unsqueeze(axis)
    shape = list(v.shape)
    shape[axis] = n
    return v.broadcast_to(shape)


def build(nc, io, out):
    ctx = ExitStack()
    with ctx:
        def sb(name, shape, dt=F32):
            return ctx.enter_context(nc.sbuf_tensor(name, shape, dt))

        def sem(name):
            return ctx.enter_context(nc.semaphore(name))

        PE = TensorStream(sem("pe_done"), column=2.4, least=305)
        DVE, SC = Stream(sem("dve_done"), 60, 1.05), Stream(sem("act_done"), 220, 0.6)
        POOL, SP = Stream(sem("pool_done"), 150, 2.0), Stream(sem("sp_done"))
        banks = Banks([ctx.enter_context(nc.psum_tensor(f"bank{i}", [P, 512], F32)) for i in range(8)])
        dve, act, pool, pe, sp = nc.vector, nc.scalar, nc.gpsimd, nc.tensor, nc.sync

        NX = 7
        xs = [sb(f"x{i}", [P, GB, D]) for i in range(NX)]
        areas = {name: Area(sb(f"area{name}", [P, n]), n)
                 for name, n in (("A", 7776), ("B", 5600), ("C", 2900), ("D", 1912), ("E", 3776), ("F", 5904))}
        w = {}
        for name, cols in (("wq0", DC * D), ("wk0", DC * D), ("wv0", DC * D), ("wo0", DC * D),
                           ("wv0x", DC * D), ("wqkv_e", DC * NE * 3 * HP), ("wo_e", NE * D),
                           ("wq1x", DC * D), ("wkv1x", DC * (P + DH)),
                           ("wc1x", DC * D), ("rows", D),
                           ("convw", HJ * 3), ("convb", HJ), ("xmask", P), ("ident", P),
                           ("cos_sin", 2 * ROT), ("blk", P), ("head_of", H), ("part", 3), ("headsum", 2 * SLIDE + HC), ("parity", 2),
                           ("iota16", NS), ("iota128", P), ("pos", 1)):
            w[name] = sb("w_" + name, [P, cols])
        onesb = sb("onesb", [P, P])
        wr_pad = sb("wr_pad", [P, DC, 32])
        w_cross = sb("w_cross", [P, DC, D])
        w_qk = sb("w_qk", [P, DC, D])
        w_vp = sb("w_vp", [P, DC, D])
        b_key = sb("b_key", [P, DC])
        u_row = sb("u_row", [P, DC])
        bb = sb("bb", [P, 1])
        picked = sb("picked", [P, GB, GB * P])
        ones_bf = sb("ones_bf", [P, P], BF16)
        bias_parts = sb("bias_parts", [P, D], BF16)
        head_of = sb("head_of", [P, H], BF16)
        bias_rest, bias_round = sb("bias_rest", [P, D]), sb("bias_round", [P, D], BF16)
        conn = sb("conn", [P, WIN * H])
        decay = sb("decay", [P, P])
        w1q = sb("w1q", [P, DC, HID], BF16)
        w2q = sb("w2q", [P, HJ, D], BF16)
        wmean = sb("wmean", [P, 2])
        small = sb("small", [P, 4])
        halves = sb("halves", [P, GB])

        def chunked(name):
            return w[name][:, :].rearrange("p (c n) -> p c n", c=DC)

        in_early, in_early2, in_late, in_late2 = (Landing(sem(n)) for n in (
            "weights_in_early", "setup_in_early", "weights_in_late", "setup_in_late"))
        s_x = [Landing(sem(f"x_in{i}")) for i in range(NX)]
        s_xt, s_ctxb, s_ctxd = Landing(sem("xt_in")), Landing(sem("ctx_b_in")), Landing(sem("ctx_d_in"))
        s_shift, s_out = Landing(sem("shift_in")), [Landing(sem(f"y_out{i}")) for i in range(NX)]

        I = w["ident"][:, :]

        def mm(out_ap, pairs, after=(), mark=False):
            PE.wait(*after)
            n = len(pairs)
            for i, (l, r) in enumerate(pairs):
                m = PE.put(pe.matmul, out_ap, l, r, start=i == 0, stop=i == n - 1, mark=mark and i == n - 1)
            return m

        def tp(out_ap, in_ap, after=(), mark=False):
            return PE.put(pe.transpose, out_ap, in_ap, I, after=after, mark=mark)

        def take():
            bank = banks.take()
            PE.wait(*bank.released)
            return bank

        def copy_out(dst, src, bank, after, func=ACT.Copy, **kw):
            m = SC.put(act.activation, dst, src, func, after=after, **kw)
            banks.give(bank, m)
            return m

        def blocks(t, n=DC):
            return t.rearrange("p (c t) -> p c t", c=n)


        def setup_early():
            m_ones = POOL.put(pool.memset, onesb[:, :], 1.0)
            POOL.put(pool.memset, halves[:, :], -0.5)
            m_ones = POOL.put(pool.memset, ones_bf[:, :], 1.0)
            area = areas["F"]
            area.reset()
            c1, b1, c2, b2, c3, b3 = (area.carve(n) for n in (CH, CH, CH * CH, CH, CH, 1))
            cw, h1, h2, cwt, s1 = (area.carve(n) for n in (CH * CH, CH, CH, 1, 1))
            n112 = WIN * H
            diag, mx, den = area.carve(n112), area.carve(H), area.carve(H)
            for name in ("ident", "headsum", "pos", "wq0", "wk0", "wv0", "rows", "part", "wo0"):
                m_w = in_early.dma(SP, sp.dma_start, w[name][:, :], io[name])
            for dst, src in ((c1[0:n112], "c1"), (b1[0:n112], "b1"),
                             (c2[0:n112], "c2"), (b2[0:n112], "b2"), (c3[0:n112], "c3"), (b3[0:n112], "b3")):
                m_setup = in_early2.dma(SP, sp.dma_start, dst, io[src])
            PE.wait(m_w, m_ones)
            yield
            m = DVE.put(dve.scalar_tensor_tensor, h1[0:n112], c1[0:n112], w["pos"][0:n112, 0:1], b1[0:n112], ALU.mult,
                        ALU.add, after=(m_setup, m_w))
            m = SC.put(act.activation, h1[0:n112], h1[0:n112], ACT.Gelu, after=(m,))
            m = DVE.put(dve.tensor_tensor, cw[0:n112].rearrange("p (j i) -> p j i", i=CH),
                        c2[0:n112].rearrange("p (j i) -> p j i", i=CH), bc(h1[0:n112], 1, CH), ALU.mult, after=(m,))
            m = DVE.put(dve.tensor_reduce, h2[0:n112], cw[0:n112].rearrange("p (j i) -> p j i", i=CH), X, ALU.add, after=(m,))
            m = DVE.put(dve.tensor_tensor, h2[0:n112], h2[0:n112], b2[0:n112], ALU.add, after=(m,))
            m = SC.put(act.activation, h2[0:n112], h2[0:n112], ACT.Gelu, after=(m,))
            m = DVE.put(dve.tensor_tensor, h1[0:n112], h2[0:n112], c3[0:n112], ALU.mult, after=(m,))
            m = DVE.put(dve.tensor_reduce, s1[0:n112], h1[0:n112], X, ALU.add, after=(m,))
            m = DVE.put(dve.tensor_tensor, cwt[0:n112], s1[0:n112], b3[0:n112], ALU.add, after=(m,))
            m = DVE.put(dve.tensor_scalar, diag[0:n112], I[0:n112, 0:n112], cwt[0:n112, 0:1], None, ALU.mult, after=(m,))
            bank = take()
            m = mm(bank.tensor[:, 0:n112], [(onesb[0:n112, :], diag[0:n112])], after=(m, m_ones), mark=True)
            m = DVE.put(dve.tensor_copy, conn[:, :], bank.tensor[:, 0:n112], after=(m,))
            banks.give(bank, m)
            by_head = conn[:, :].rearrange("p (w h) -> p h w", h=H)
            conn3 = conn[:, :].rearrange("p (w h) -> p w h", h=H)
            m = DVE.put(dve.tensor_reduce, mx, by_head, X, ALU.max, after=(m,))
            m = DVE.put(dve.tensor_tensor, conn3, conn3, bc(mx, 1, WIN), ALU.subtract, after=(m,))
            m = SC.put(act.activation, conn[:, :], conn[:, :], ACT.Exp, after=(m,))
            m = DVE.put(dve.tensor_reduce, den, by_head, X, ALU.add, after=(m,))
            m = DVE.put(dve.reciprocal, den, den, after=(m,))
            m = DVE.put(dve.tensor_tensor, conn3, conn3, bc(den, 1, WIN), ALU.mult, after=(m,))
            DVE.wait(m)
            early_done.append(m)
            early_done.append(split_bias(slice(0, 64)))

        early_done, late_done = [], []

        def split_bias(r, after=()):
            rest, part, parts = w["rows"][r, :], bias_rest[r, :], bias_parts[r, :]
            m = DVE.put(dve.memset, part, 0.0, after=after)
            for k in range(3):
                m1 = DVE.put(dve.tensor_copy, bias_round[r, :], rest, after=(m,))
                m2 = DVE.put(dve.scalar_tensor_tensor, part, bias_round[r, :], w["part"][r, k:k + 1], part, ALU.mult,
                             ALU.add, after=(m1,))
                m = DVE.put(dve.tensor_tensor, rest, rest, bias_round[r, :], ALU.subtract, after=(m2,))
            return DVE.put(dve.tensor_copy, parts, part, after=(m2,))

        def setup_late():
            m_zero = POOL.put(pool.memset, wr_pad[:, :, :], 0.0)
            POOL.put(pool.memset, picked[:, :, :], 0.0)
            aB, aC, aE, aF = (areas[n] for n in "BCEF")
            aF.at = aF.size - HJ * D
            raw_q, raw_k, q1, k1, v1, p1 = (aB.carve(DC * D) for _ in range(6))
            bits, gam, bqkv = aB.carve(15 * P), aB.carve(1), aB.carve(3 * DC)
            powers, fac, t_b = aB.carve(7), aB.carve(P), aB.carve(1)
            raw1, raw2, tmp = aC.carve(DC * HID), aE.carve(HJ * D), aF.carve(HJ * D)
            for dst, src in ((raw_q, "raw_q"), (raw_k, "raw_k"), (gam, "gamma"), (bits, "bits"), (bqkv, "bqkv1"),
                             (q1, "wq1T"), (k1, "wk1T"), (v1, "wv1T"), (p1, "wp1"), (raw1, "raw1"), (raw2, "raw2")):
                m_setup = in_late2.dma(SP, sp.dma_start, dst, io[src])
            m_setup = in_late2.dma(SP, sp.dma_start, wr_pad[:, :, 0:NE], io["wr"].rearrange("p (c n) -> p c n", c=DC),
                                   after=(m_zero,))
            for name in ("xmask", "wv0x", "cos_sin", "blk", "head_of", "iota16", "iota128", "parity",
                         "wqkv_e", "wo_e", "wq1x", "wkv1x", "wc1x", "convw", "convb"):
                m_w = in_late.dma(SP, sp.dma_start, w[name][:, :], io[name])
            for _ in range(24):
                yield
            PE.wait(m_setup, m_w)
            SC.wait(m_setup, m_w)
            POOL.wait(m_w)
            DVE.wait(m_w, m_setup)
            DVE.put(dve.tensor_copy, head_of[:, :], w["head_of"][:, :])
            m = DVE.put(dve.tensor_copy, powers[:, 0:1], gam)
            for i in range(1, 7):
                m = DVE.put(dve.tensor_tensor, powers[:, i:i + 1], powers[:, i - 1:i], powers[:, i - 1:i], ALU.mult, after=(m,))
            m = DVE.put(dve.tensor_scalar, decay[:, :], bits[:, 14 * P:15 * P], float(D) ** -0.5, None, ALU.mult, after=(m,))
            for i in range(7):
                m2 = DVE.put(dve.scalar_tensor_tensor, fac, bits[:, i * P:(i + 1) * P], powers[:, i:i + 1],
                             bits[:, (7 + i) * P:(8 + i) * P], ALU.mult, ALU.add, after=(m,))
                m = DVE.put(dve.tensor_tensor, decay[:, :], decay[:, :], fac, ALU.mult, after=(m2,))
            yield
            def product(dst, left, right):
                bank = take()
                for c in range(DC):
                    m = mm(bank.tensor[:, c * D:(c + 1) * D], [(left[:, n * D + c * P:n * D + (c + 1) * P],
                                                               right[:, n * D:(n + 1) * D]) for n in range(DC)], mark=True)
                return copy_out(dst[:, :, :], blocks(bank.tensor[:, :]), bank, (m,))

            product(w_cross, raw_k, raw_q)
            yield
            product(w_qk, q1, k1)
            yield
            product(w_vp, v1, p1)
            bank = take()
            for c in range(DC):
                mm(bank.tensor[:, c:c + 1], [(k1[:, n * D + c * P:n * D + (c + 1) * P], bqkv[:, n:n + 1]) for n in range(DC)])
                mm(bank.tensor[:, 2 + c:3 + c], [(q1[:, n * D + c * P:n * D + (c + 1) * P], bqkv[:, DC + n:DC + n + 1])
                                                  for n in range(DC)])
            m = mm(bank.tensor[64:96, D:2 * D],
                   [(bqkv[:, 2 * DC + n:2 * DC + n + 1].broadcast_to([P, 32]), p1[:, n * D:(n + 1) * D]) for n in range(DC)]
                   + [(onesb[64:65, 0:32], w["rows"][64:65, :])], mark=True)
            SC.put(act.activation, b_key[:, :], bank.tensor[:, 0:2], ACT.Copy, after=(m,))
            SC.put(act.activation, u_row[:, :], bank.tensor[:, 2:4], ACT.Copy)
            m_b = copy_out(w["rows"][64:96, :], bank.tensor[64:96, D:2 * D], bank, ())
            m_parts = split_bias(slice(64, 96), (m_b,))
            m = DVE.put(dve.tensor_tensor, bqkv[:, 0:DC], bqkv[:, 0:DC], bqkv[:, DC:2 * DC], ALU.mult, after=(m,))
            m = DVE.put(dve.tensor_reduce, t_b, bqkv[:, 0:DC], X, ALU.add, after=(m,))
            bank = take()
            m = mm(bank.tensor[:, 0:1], [(onesb[:, :], t_b)], after=(m,), mark=True)
            m_sc = copy_out(bb[:, :], bank.tensor[:, 0:1], bank, (m,))
            yield
            for i, (raw, q) in enumerate(((raw1, w1q[:, :, :].rearrange("p c n -> p (c n)")),
                                          (raw2, w2q[:, :, :].rearrange("p c n -> p (c n)")))):
                m = DVE.put(dve.tensor_reduce, small[:, i:i + 1], raw, X, ALU.add, apply_absolute_value=True)
                bank = take()
                m = mm(bank.tensor[:, 0:1], [(onesb[:, :], small[:, i:i + 1])], after=(m,), mark=True)
                m = DVE.put(dve.tensor_scalar, wmean[:, i:i + 1], bank.tensor[:, 0:1], 1.0 / (HID * D), 1e-5,
                            ALU.mult, ALU.max, after=(m,))
                banks.give(bank, m)
                m = DVE.put(dve.reciprocal, small[:, 2 + i:3 + i], wmean[:, i:i + 1], after=(m,))
                m = DVE.put(dve.tensor_scalar, tmp, raw, small[:, 2 + i:3 + i], MAGIC, ALU.mult, ALU.add, after=(m,))
                m = DVE.put(dve.tensor_scalar, tmp, tmp, MAGIC, 1.0, ALU.subtract, ALU.min, after=(m,))
                m = DVE.put(dve.tensor_scalar, q, tmp, -1.0, None, ALU.max, after=(m,))
                yield
            late_done.extend([m, m_sc, m_parts])

        def to_channels(x, ready, xT):
            bank = take()
            for c in range(DC):
                for b in range(GB):
                    m = tp(bank.tensor[:, c * T + b * P:c * T + (b + 1) * P], x[:, b, c * P:(c + 1) * P], after=(ready[b],),
                           mark=c + b == 2)
            return copy_out(xT, bank.tensor[:, :], bank, (m,))

        def project(weights, actT):
            bank = take()
            for m in range(DC):
                mk = mm(bank.tensor[:, m * T:(m + 1) * T],
                        [(weights[:, c, m * P:(m + 1) * P], actT[:, c, :]) for c in range(DC)], mark=m == 1)
            return bank, mk

        def bias_row(i):
            def terms(b):
                return [(ones_bf[32 * i:32 * i + 3, :], bias_parts[32 * i:32 * i + 3, :])]
            return terms

        def no_bias(b):
            return []

        def project_rows(weights, actT, extra=no_bias):
            bank = take()
            for b in range(GB):
                mk = mm(bank.tensor[:, b * D:(b + 1) * D],
                        [(actT[:, c, b * P:(b + 1) * P], weights[:, c, 0:D]) for c in range(DC)] + extra(b), mark=b == 1)
            return bank, mk

        NORM_SLOTS = 6
        bn_parts, bn_mv = sb("bn_parts", [P, NORM_SLOTS, GB, 6]), sb("bn_mv", [P, NORM_SLOTS, GB, 2])
        bn_scale = sb("bn_scale", [P, NORM_SLOTS, 2, GB])
        neg_top = sb("neg_top", [P, GB, 3, H])
        norm_slots = [(i, []) for i in range(NORM_SLOTS)]

        def norm(x, bank, ready, scale=None):
            rows = bank.tensor[:, :].rearrange("p (b d) -> p b d", d=D)
            slot, slot_free = norm_slots.pop(0)
            st, agg, sc = bn_parts[:, slot], bn_mv[:, slot], bn_scale[:, slot]
            DVE.wait(*slot_free, *ready)
            if scale is None:
                m = DVE.put(dve.tensor_tensor, x[:, :, :], rows, x[:, :, :], ALU.add)
            else:
                for b in range(GB):
                    m = DVE.put(dve.scalar_tensor_tensor, x[:, b, :], rows[:, b, :], scale[:, b:b + 1], x[:, b, :],
                                ALU.mult, ALU.add)
            banks.give(bank, m)
            DVE.wait(m)
            for b in range(GB):
                m = DVE.put(dve.bn_stats, st[:, b, :], x[:, b, :])
            DVE.wait(m)
            for b in range(GB):
                m = DVE.put(dve.bn_aggr, agg[:, b, :], st[:, b, :])
            rstd, shift = sc[:, 0, :], sc[:, 1, :]
            POOL.wait(m)
            m1 = POOL.put(pool.tensor_scalar, rstd, agg[:, :, 1], 1.0, EPS, ALU.mult, ALU.add)
            m2 = POOL.put(pool.tensor_scalar, shift, agg[:, :, 0], -1.0, 0.0, ALU.mult, ALU.add)
            m1 = POOL.put(pool.tensor_tensor, rstd, rstd, halves[:, :], ALU.pow, after=(m1, m2))
            m2 = POOL.put(pool.tensor_tensor, shift, shift, rstd, ALU.mult, after=(m1,))
            yield
            done = []
            for b in range(GB):
                if scale is None:
                    done.append(SC.put(act.activation, x[:, b, :], x[:, b, :], ACT.Identity, scale=rstd[:, b:b + 1],
                                       bias=shift[:, b:b + 1], after=(m2,)))
                else:
                    done.append(POOL.put(pool.tensor_scalar, x[:, b, :], x[:, b, :], rstd[:, b:b + 1], shift[:, b:b + 1],
                                         ALU.mult, ALU.add, after=(m2,)))
            norm_slots.append((slot, [done[-1]]))
            yield
            return done

        def key_softmax(s, ready, sums, negmax):
            n, k = s.shape[1], s.shape[2]
            m = DVE.put(dve.tensor_reduce, negmax, s, X, ALU.max, negate=True, after=ready)
            for j in range(n):
                m_e = SC.put(act.activation, s[:, j, :], s[:, j, :], ACT.Exp, bias=negmax[:, j:j + 1],
                             accum_out=sums[:, j:j + 1], after=(m,))
            yield
            m = DVE.put(dve.reciprocal, sums, sums, after=(m_e,))
            m = POOL.put(pool.tensor_tensor, s, s, bc(sums, 2, k), ALU.mult, after=(m,))
            yield
            return m

        POOL_SCORES, POOL_VALUES = (2, 5), (1, 4)
        SUMS = ((WIN, 0, 2), (WIN + 1, 1, 4), (WIN + 2, 3, 5), (WIN, WIN, 6), (WIN + 1, WIN + 1, WIN + 2), (WIN, WIN, WIN + 1))
        POOL_SUMS = (1,)
        area = areas["A"]
        xT0, qT0 = blocks(area.carve(W2)), blocks(area.carve(W2))
        LP = P + 2 * PAD
        kT0 = area.carve(DC * GB * LP).rearrange("p (c b t) -> p c b t", c=DC, b=GB)
        prods = [area.carve(W2) for _ in range(4)]
        vw = area.carve(WIN * W2).rearrange("p (w n) -> p w n", w=WIN)
        e0 = area.carve(GB * WIN * H)
        sT0 = area.carve(T)
        den0 = area.carve(3 * GB * H).rearrange("p (k n) -> p k n", k=3)
        POOL.put(pool.memset, vw, 0.0)
        m_pads = POOL.put(pool.memset, kT0, 0.0)

        def windowed(g, x, x_ready, free):
            m_xt = s_xt.dma(SP, sp.dma_start, xT0, io["xT"][g].rearrange("p (c t) -> p c t", c=DC), after=free)
            yield
            yield
            PE.wait(m_xt)
            bank, m = project(chunked("wq0"), xT0)
            yield
            m_q = copy_out(qT0, blocks(bank.tensor[:, :]), bank, (m, *free))
            bank, m = project(chunked("wk0"), xT0)
            yield
            m_k = copy_out(kT0.rearrange("p c b t -> p (c b) t")[:, :, PAD:PAD + P],
                           bank.tensor[:, :].rearrange("p (n t) -> p n t", t=P), bank, (m, m_pads))
            yield
            bank, m = project_rows(chunked("wv0"), xT0)
            yield
            m_v = copy_out(vw[:, PAD, :], bank.tensor[:, :], bank, (m,))
            for wi in range(WIN):
                o = wi - PAD
                if o:
                    lo, hi = max(0, -o), P - max(0, o)
                    m_sh = s_shift.dma(SP, sp.dma_start, vw[lo:hi, wi, :], vw[lo + o:hi + o, PAD, :],
                                       after=(m_v, m_pads))
            hbank = take()
            prod_free = [list(free) for _ in prods]
            m_prod = {}

            def product(wi):
                r = wi % 4
                stream, eng = (POOL, pool) if wi in POOL_SCORES else (DVE, dve)
                m_prod[wi] = stream.put(eng.tensor_tensor, prods[r].rearrange("p (n t) -> p n t", t=P),
                                        qT0.rearrange("p c (b t) -> p (c b) t", t=P),
                                        kT0.rearrange("p c b t -> p (c b) t")[:, :, wi:wi + P], ALU.mult,
                                        after=(m_q, m_k, *prod_free[r]))

            for wi in range(3):
                product(wi)
            yield
            for wi in range(WIN):
                r = wi % 4
                if wi + 3 < WIN:
                    product(wi + 3)
                PE.wait(m_prod[wi])
                for c in range(DC):
                    at = SLIDE - (wi * H + c * HC)
                    m = PE.put(pe.matmul, hbank.tensor[0:WIN * H, 0:T], w["headsum"][:, at:at + WIN * H],
                               prods[r][:, c * T:(c + 1) * T], start=wi + c == 0, stop=wi + c == WIN, mark=c == DC - 1)
                prod_free[r] = [m]
                yield
            yield
            m = copy_out(sT0[0:WIN * H], hbank.tensor[0:WIN * H, 0:T], hbank, (m,))
            yield
            sbank = take()
            scores = sbank.tensor[:, 0:GB * WIN * H].rearrange("p (b w h) -> p b w h", b=GB, w=WIN)
            PE.wait(m)
            for b in range(GB):
                m = PE.put(pe.transpose, sbank.tensor[:, b * WIN * H:(b + 1) * WIN * H], sT0[0:WIN * H, b * P:(b + 1) * P],
                           I[0:WIN * H, 0:WIN * H], mark=b == GB - 1)
            e4 = e0.rearrange("p (b w h) -> p b w h", b=GB, w=WIN)
            e_head = e4.rearrange("p b w h -> p b h w")
            mx, den1, den2 = (den0[:, i, :].rearrange("p (b h) -> p b h", b=GB) for i in range(3))
            yield
            m = DVE.put(dve.tensor_reduce, mx, scores.rearrange("p b w h -> p b h w"), X, ALU.max, after=(m,))
            m = DVE.put(dve.tensor_tensor, e4, scores, bc(mx, 2, WIN), ALU.subtract, after=(m,))
            banks.give(sbank, m)
            m = SC.put(act.activation, e0, e0, ACT.Exp, scale=float(DH) ** -0.5, after=(m,))
            yield
            m1 = DVE.put(dve.tensor_reduce, den1, e_head, X, ALU.add, after=(m,))
            m = DVE.put(dve.tensor_tensor, e0.rearrange("p (b n) -> p b n", b=GB), e0.rearrange("p (b n) -> p b n", b=GB),
                        bc(conn[:, :], 1, GB), ALU.mult, after=(m1, *early_done))
            m = DVE.put(dve.tensor_reduce, den2, e_head, X, ALU.add, after=(m,))
            m = DVE.put(dve.scalar_tensor_tensor, den0[:, 0, :], den0[:, 1, :], 1e-9, den0[:, 2, :], ALU.mult, ALU.add,
                        after=(m,))
            m = DVE.put(dve.reciprocal, den0[:, 0, :], den0[:, 0, :], after=(m,))
            m_fw = DVE.put(dve.tensor_tensor, e4, e4, bc(mx, 2, WIN), ALU.mult, after=(m,))
            yield
            weighted = []
            for wi in range(WIN):
                stream, eng = (POOL, pool) if wi in POOL_VALUES else (DVE, dve)
                v4 = vw[:, wi, :].rearrange("p (b h d) -> p b h d", b=GB, h=H)
                weighted.append(stream.put(eng.tensor_tensor, v4, v4, bc(e4[:, :, wi, :], 3, DH), ALU.mult,
                                           after=(m_fw, m_v, m_sh)))
                if wi % 2:
                    yield
            part = [vw[:, wi, :] for wi in range(WIN)] + prods[0:3]
            done = weighted + [None] * 3
            for step, (dst, i, j) in enumerate(SUMS):
                stream, eng = (POOL, pool) if step in POOL_SUMS else (DVE, dve)
                done[dst] = stream.put(eng.tensor_tensor, part[dst], part[i], part[j], ALU.add,
                                       after=(done[i], done[j], *prod_free[dst - WIN]))
                if step % 2:
                    yield
            yield
            bank = take()
            PE.wait(done[WIN])
            for c in range(DC):
                for b in range(GB):
                    at = b * D + c * P
                    m = tp(bank.tensor[:, c * T + b * P:c * T + (b + 1) * P], prods[0][:, at:at + P], mark=c + b == 2)
            yield
            m = copy_out(qT0, blocks(bank.tensor[:, :]), bank, (m,))
            yield
            PE.wait(m)
            bank, m = project_rows(chunked("wo0"), qT0, bias_row(0))
            yield
            return (yield from norm(x, bank, (m, *x_ready)))

        def cross(g, x, ready, free):
            area = areas["B"]
            area.reset()
            xT, ctxT, ka, v = (area.carve(W2) for _ in range(4))
            s, pT = area.carve(T), area.carve(T)
            sums, negmax = area.carve(GB), area.carve(GB)
            m_c = s_ctxb.dma(SP, sp.dma_start, ctxT, io["ctxT"][g], after=free)
            SC.wait(*free)
            yield
            yield
            PE.wait(m_c)
            bank, m = project(w_cross, blocks(ctxT))
            yield
            m_ka = copy_out(ka, bank.tensor[:, :], bank, (m,))
            bank, m = project_rows(chunked("wv0x"), blocks(ctxT))
            yield
            m_v = copy_out(v, bank.tensor[:, :], bank, (m,))
            yield
            m_x = to_channels(x, ready, xT)
            yield
            bank = take()
            PE.wait(m_x, m_ka)
            xT, ka = blocks(xT), blocks(ka)
            for b in range(GB):
                m = mm(bank.tensor[:, b * P:(b + 1) * P], [(xT[:, c, b * P:(b + 1) * P], ka[:, c, b * P:(b + 1) * P])
                                                            for c in range(DC)], mark=b == 1)
            s3 = blocks(s, GB)
            yield
            m = DVE.put(dve.scalar_tensor_tensor, s3, blocks(bank.tensor[:, 0:T], GB),
                        float(D) ** -0.5, bc(w["xmask"][:, :], 1, GB), ALU.mult, ALU.add, after=(m, *free))
            banks.give(bank, m)
            yield
            m = yield from key_softmax(s3, (m,), sums, negmax)
            bank = take()
            for b in range(GB):
                mt = tp(bank.tensor[:, b * P:(b + 1) * P], s3[:, b, :], after=(m,), mark=b == 1)
            yield
            m = copy_out(pT, bank.tensor[:, 0:T], bank, (mt,))
            yield
            bank = take()
            PE.wait(m, m_v)
            more = bias_row(1)
            for b in range(GB):
                m = mm(bank.tensor[:, b * D:(b + 1) * D], [(pT[:, b * P:(b + 1) * P], v[:, b * D:(b + 1) * D])] + more(b),
                       mark=b == 1)
            yield
            return (yield from norm(x, bank, (m,)))

        def experts(g, x, ready):
            area = areas["B"]
            area.reset()
            xT_, pick, cs, qkv = (area.carve(n) for n in (W2, T, EJ * 2 * ROT, EJ * 3 * HP))
            turn, qkT, s, pT, pickT = (area.carve(n) for n in (EJ * 2 * ROT, EJ * 2 * P, EJ * P, EJ * P, GB * EJ * P))
            av, up = area.carve(T), area.carve(EJ * D)
            sig, r1, r2 = area.carve(P), area.carve(P), area.carve(P)
            m8, sigt, sums, negmax = area.carve(16), area.carve(GB * NE), area.carve(EJ), area.carve(EJ)
            xT = blocks(xT_)
            m_x = to_channels(x, ready, xT_)
            yield
            R = 32 * GB
            bank = take()
            PE.wait(m_x)
            for b in range(GB):
                m = mm(bank.tensor[32 * b:32 * b + 32, 0:P], [(wr_pad[:, c, :], xT[:, c, b * P:(b + 1) * P]) for c in range(DC)],
                       mark=b == 1)
            yield
            m = copy_out(sig[0:R], bank.tensor[0:R, 0:P], bank, (m,), ACT.Exp, scale=-1.0)
            yield
            m = DVE.put(dve.tensor_scalar, sig[0:R], sig[0:R], 1.0, None, ALU.add, after=(m,))
            m_sig = DVE.put(dve.reciprocal, sig[0:R], sig[0:R], after=(m,))
            m = DVE.put(dve.max, m8[0:R, 0:8], sig[0:R], after=(m_sig,))
            m = DVE.put(dve.match_replace, r1[0:R], m8[0:R, 0:8], sig[0:R], -1.0, after=(m,))
            m = DVE.put(dve.max, m8[0:R, 8:16], r1[0:R], after=(m,))
            m = DVE.put(dve.match_replace, r2[0:R], m8[0:R, 8:16], r1[0:R], -1.0, after=(m,))
            m = DVE.put(dve.tensor_scalar, r1[0:R], r2[0:R], 0.0, None, ALU.is_lt, after=(m,))
            m = DVE.put(dve.tensor_tensor_scan, r2[0:R], onesb[0:R, :], r1[0:R], 0.0, ALU.mult, ALU.add, after=(m,))
            m = DVE.put(dve.tensor_tensor, r2[0:R], r2[0:R], r1[0:R], ALU.mult, after=(m,))
            yield
            bank = take()
            PE.wait(m_sig, m)
            PE.put(pe.transpose, bank.tensor[:, 0:R], r2[0:R], I[0:R, 0:R], mark=False)
            m = PE.put(pe.transpose, bank.tensor[:, P:P + R], sig[0:R], I[0:R, 0:R])
            rank4 = blocks(bank.tensor[:, 0:R], GB)[:, :, 0:NE]
            sig4 = blocks(bank.tensor[:, P:P + R], GB)[:, :, 0:NE]
            by_slot = "p (e b s) -> p b e s"
            pick4 = pick.rearrange(by_slot, e=NE, b=GB)
            m_sg = DVE.put(dve.tensor_copy, blocks(sigt, GB), sig4, after=(m,))
            m_pick = DVE.put(dve.tensor_tensor, pick4, bc(rank4, 3, NS), bc(bc(w["iota16"][:, :], 1, NE), 1, GB),
                             ALU.is_equal)
            banks.give(bank, m_pick)
            for b in range(GB):
                m_picked = POOL.put(pool.tensor_tensor, picked[:, b, :].rearrange(by_slot, e=NE, b=GB)[:, b], pick4[:, b],
                                    bc(blocks(sigt, GB)[:, b], 2, NS), ALU.mult, after=(m_pick, m_sg))
            yield
            xg = xT_.rearrange("p (c e b s) -> p c b e s", c=DC, e=NE, b=GB)
            PE.wait(m_pick)
            bank = take()
            for c in range(DC):
                for b in range(GB):
                    m = mm(bank.tensor[:, c * T + b * P:c * T + (b + 1) * P],
                           [(x[:, b, c * P:(c + 1) * P], pick4[:, b])], mark=c + b == 2)
            for c in range(DC):
                m_xg = SC.put(act.activation, xg[:, c], bank.tensor[:, c * T:(c + 1) * T].rearrange("p (b e s) -> p b e s", b=GB, e=NE),
                              ACT.Copy, after=(m,))
            banks.give(bank, m_xg)
            bank = take()
            for j in range(EJ):
                m = mm(bank.tensor[:, j * 2 * ROT:(j + 1) * 2 * ROT], [(pick[:, j * P:(j + 1) * P], w["cos_sin"][:, :])],
                       mark=j == EJ - 1)
            yield
            m_cs = copy_out(cs, bank.tensor[:, 0:EJ * 2 * ROT], bank, (m,))
            yield
            wq = w["wqkv_e"][:, :].rearrange("p (c e n) -> p c e n", c=DC, e=NE)
            xgf = xT_.rearrange("p (c e n) -> p c e n", c=DC, e=NE)
            qkv3 = blocks(qkv, EJ)
            PE.wait(m_xg)
            for j in range(EJ):
                bank = take()
                for q in range(EQ):
                    e = j * EQ + q
                    m = mm(bank.tensor[ES * q:ES * (q + 1), 0:3 * HP], [(xgf[:, c, e, :], wq[:, c, e, :]) for c in range(DC)],
                           mark=q == EQ - 1)
                    yield
                m_qkv = copy_out(qkv3[:, j, :], bank.tensor[:, 0:3 * HP], bank, (m,))
            yield
            a = qkv3[:, :, 0:2 * HP].rearrange("p j (i n) -> p j i n", i=2)[:, :, :, 0:ROT]
            turn4 = turn.rearrange("p (j i n) -> p j i n", j=EJ, i=2)
            cs3, half = blocks(cs, EJ), ROT // 2
            DVE.wait(m_qkv, m_cs)
            for h in range(2):
                dst, other = slice(h * half, (h + 1) * half), slice((1 - h) * half, (2 - h) * half)
                m1 = DVE.put(dve.tensor_tensor, turn4[:, :, :, dst], a[:, :, :, other],
                             bc(cs3[:, :, ROT + h * half:ROT + (h + 1) * half], 2, 2), ALU.mult)
            m2 = DVE.put(dve.tensor_tensor, a, a, bc(cs3[:, :, 0:ROT], 2, 2), ALU.mult, after=(m1,))
            m_rot = DVE.put(dve.tensor_tensor, a, a, turn4, ALU.add, after=(m2,))
            yield
            bank = take()
            for j in range(EJ):
                for i in range(2):
                    at = 2 * j + i
                    m = tp(bank.tensor[:, at * P:(at + 1) * P], qkv3[:, j, i * HP:(i + 1) * HP], after=(m_rot,), mark=at == 3)
            yield
            m = copy_out(qkT, bank.tensor[:, :], bank, (m,))
            yield
            bank = take()
            PE.wait(m)
            for j in range(EJ):
                m = mm(bank.tensor[:, j * P:(j + 1) * P], [(qkT[:, 2 * j * P:(2 * j + 1) * P], qkT[:, (2 * j + 1) * P:(2 * j + 2) * P])],
                       mark=j == EJ - 1)
            s3 = blocks(s, EJ)
            yield
            m = DVE.put(dve.scalar_tensor_tensor, s3, blocks(bank.tensor[:, 0:EJ * P], EJ),
                        float(HP) ** -0.5, bc(w["blk"][:, :], 1, EJ), ALU.mult, ALU.add, after=(m,))
            banks.give(bank, m)
            yield
            m = yield from key_softmax(s3, (m,), sums, negmax)
            bank = take()
            for j in range(EJ):
                mt = tp(bank.tensor[:, j * P:(j + 1) * P], s3[:, j, :], after=(m,), mark=j == EJ - 1)
            yield
            m = copy_out(pT, bank.tensor[:, 0:EJ * P], bank, (mt,))
            yield
            bank = take()
            PE.wait(m)
            for j in range(EJ):
                m = mm(bank.tensor[:, j * P:(j + 1) * P], [(qkv3[:, j, 2 * HP:3 * HP], pT[:, j * P:(j + 1) * P])], mark=j == EJ - 1)
            yield
            m_av = copy_out(av, bank.tensor[:, 0:EJ * P], bank, (m,))
            bank = take()
            for b in range(GB):
                for j in range(EJ):
                    at = b * EJ + j
                    m = tp(bank.tensor[:, at * P:(at + 1) * P], picked[:, b, j * P:(j + 1) * P], after=(m_picked,), mark=at == 3)
            yield
            m_pt = copy_out(pickT, bank.tensor[:, :], bank, (m,))
            yield
            wo = w["wo_e"][:, :].rearrange("p (e n) -> p e n", e=NE)
            PE.wait(m_av)
            bank = take()
            for j in range(EJ):
                for q in range(EQ):
                    e = j * EQ + q
                    m = mm(bank.tensor[ES * q:ES * (q + 1), j * D:(j + 1) * D], [(av[:, e * ES:(e + 1) * ES], wo[:, e, :])],
                           mark=e == NE - 1)
                    if q % 2:
                        yield
            yield
            m_u = copy_out(up, bank.tensor[:, :], bank, (m,))
            yield
            bank = take()
            PE.wait(m_pt, m_u)
            for b in range(GB):
                m = mm(bank.tensor[:, b * D:(b + 1) * D],
                       [(pickT[:, (b * EJ + j) * P:(b * EJ + j + 1) * P], up[:, j * D:(j + 1) * D]) for j in range(EJ)],
                       mark=b == 1)
            yield
            return (yield from norm(x, bank, (m,)))

        def decayed(g, x, ready, free):
            area = areas["C"]
            area.reset()
            xT, yT, v = (area.carve(W2) for _ in range(3))
            s, pT = area.carve(T), area.carve(T)
            sums, negmax, part = area.carve(GB), area.carve(GB), area.carve(GB)
            SC.wait(*free)
            DVE.wait(*free)
            m_x = to_channels(x, ready, xT)
            xT = blocks(xT)
            yield
            PE.wait(m_x)
            bank, m = project(w_qk, xT)
            for c in range(DC):
                m_y = SC.put(act.activation, yT[:, c * T:(c + 1) * T], bank.tensor[:, c * T:(c + 1) * T], ACT.Identity,
                             bias=b_key[:, c:c + 1], after=(m,))
            banks.give(bank, m_y)
            bank, m = project_rows(w_vp, xT)
            yield
            m_v = copy_out(v, bank.tensor[:, :], bank, (m,))
            yield
            yT = blocks(yT)
            bank = take()
            PE.wait(m_y)
            for b in range(GB):
                mm(bank.tensor[:, T + b:T + b + 1], [(xT[:, c, b * P:(b + 1) * P], u_row[:, c:c + 1]) for c in range(DC)])
                m = mm(bank.tensor[:, b * P:(b + 1) * P], [(yT[:, c, b * P:(b + 1) * P], xT[:, c, b * P:(b + 1) * P])
                                                            for c in range(DC)], mark=b == 1)
            yield
            m1 = DVE.put(dve.tensor_scalar, part, bank.tensor[:, T:T + GB], bb[:, 0:1], None, ALU.add, after=(m,))
            s3 = blocks(s, GB)
            for b in range(GB):
                m = DVE.put(dve.scalar_tensor_tensor, s3[:, b, :], bank.tensor[:, b * P:(b + 1) * P], part[:, b:b + 1],
                            decay[:, :], ALU.add, ALU.mult, after=(m1,))
            banks.give(bank, m)
            yield
            m = yield from key_softmax(s3, (m,), sums, negmax)
            bank = take()
            for b in range(GB):
                mt = tp(bank.tensor[:, b * P:(b + 1) * P], s3[:, b, :], after=(m,), mark=b == 1)
            yield
            m = copy_out(pT, bank.tensor[:, 0:T], bank, (mt,))
            yield
            bank = take()
            PE.wait(m, m_v)
            more = bias_row(2)
            for b in range(GB):
                m = mm(bank.tensor[:, b * D:(b + 1) * D], [(pT[:, b * P:(b + 1) * P], v[:, b * D:(b + 1) * D])] + more(b),
                       mark=b == 1)
            yield
            return (yield from norm(x, bank, (m,)))

        class Chosen:

            def __init__(self, i):
                self.qT = sb(f"chosen_q{i}", [P, DC, T])
                self.key = sb(f"chosen_key{i}", [P, GB, 2, P])
                self.mv = sb(f"chosen_v{i}", [P, GB, VC])

        chosen = [Chosen(i) for i in range(2)]

        def choose_memory(g, x, hand, ready, free, hand_free):
            area = areas["D"]
            area.reset()
            xT_, ctxT = area.carve(W2), area.carve(W2)
            KV = P + VC
            kv = blocks(area.carve(GB * KV), GB)
            o, oT = area.carve(T), area.carve(T)
            qT, key, mv = hand.qT, hand.key, hand.mv
            m8, i8 = area.carve(8 * GB), area.carve(8 * GB)
            for s in (SC, DVE):
                s.wait(*hand_free)
            m_c = s_ctxd.dma(SP, sp.dma_start, ctxT, io["ctxT"][g], after=free)
            for s in (SC, DVE, POOL):
                s.wait(*free)
            POOL.put(pool.memset, kv[:, :, P + DH + 1:KV], 0.0)
            m_one = POOL.put(pool.memset, kv[:, :, P + DH:P + DH + 1], 1.0)
            yield
            wkv = chunked("wkv1x")
            ctxT = blocks(ctxT)
            PE.wait(m_c)
            bank = take()
            for b in range(GB):
                m = mm(bank.tensor[:, b * D:b * D + P + DH], [(ctxT[:, c, b * P:(b + 1) * P], wkv[:, c, :])
                                                              for c in range(DC)], mark=b == 1)
            yield
            m_kv = copy_out(kv[:, :, 0:P + DH], blocks(bank.tensor[:, :], GB)[:, :, 0:P + DH], bank, (m,))
            m_x = to_channels(x, ready, xT_)
            yield
            PE.wait(m_x)
            bank, m = project(chunked("wq1x"), blocks(xT_))
            yield
            m_q = copy_out(qT[:, :, :], blocks(bank.tensor[:, :]), bank, (m,))
            yield
            bank = take()
            PE.wait(m_q)
            for b in range(GB):
                m = mm(bank.tensor[:, b * P:(b + 1) * P], [(qT[:, c, b * P:(b + 1) * P], ctxT[:, c, b * P:(b + 1) * P])
                                                            for c in range(DC)], mark=b == 1)
            yield
            m = copy_out(o, bank.tensor[:, 0:T], bank, (m,))
            for b in range(GB):
                m = DVE.put(dve.max, m8[:, 8 * b:8 * b + 8], o[:, b * P:(b + 1) * P], after=(m,))
            i8u = i8.bitcast(U32)
            for b in range(GB):
                m = DVE.put(dve.max_index, i8u[:, 8 * b:8 * b + 8], m8[:, 8 * b:8 * b + 8], o[:, b * P:(b + 1) * P],
                            after=(m,))
            m = DVE.put(dve.tensor_tensor, blocks(o, GB), bc(blocks(i8u, GB)[:, :, 0], 2, P),
                        bc(w["iota128"][:, :], 1, GB), ALU.is_equal, after=(m,))
            yield
            bank = take()
            for b in range(GB):
                mt = tp(bank.tensor[:, b * P:(b + 1) * P], o[:, b * P:(b + 1) * P], after=(m,), mark=b == 1)
            yield
            m_ot = copy_out(oT, bank.tensor[:, 0:T], bank, (mt,))
            yield
            bank = take()
            PE.wait(m_ot, m_kv, m_one)
            for b in range(GB):
                m = mm(bank.tensor[:, b * P:(b + 1) * P], [(kv[:, b, 0:P], oT[:, b * P:(b + 1) * P])], mark=b == 1)
            m_key = None
            for b in range(GB):
                m_key = DVE.put(dve.tensor_tensor, key[:, b], bc(bank.tensor[:, b * P:(b + 1) * P], 1, 2),
                                bc(w["parity"][:, :], 2, P), ALU.mult, after=(m,))
            banks.give(bank, m_key)
            bank = take()
            for b in range(GB):
                m = mm(bank.tensor[:, b * VC:(b + 1) * VC], [(oT[:, b * P:(b + 1) * P], kv[:, b, P:KV])],
                       mark=b == 1)
            yield
            m_mv = copy_out(mv[:, :, :], blocks(bank.tensor[:, 0:GB * VC], GB), bank, (m,))
            return [m_q, m_key, m_mv]

        def memory(x, hand, ready, chosen_ready, free):
            area = areas["E"]
            area.reset()
            att, aT = blocks(area.carve(W2), GB), area.carve(W2)
            pT, turned = area.carve(H * P), area.carve(W2)
            negT, rec = area.carve(GB * P // 2).bitcast(BF16), area.carve(H)
            rest = area.carve(GB * H)
            rounded = area.carve(GB * H // 2).bitcast(BF16)
            qT, key, mv = hand.qT, hand.key, hand.mv
            for s in (SC, DVE, PE):
                s.wait(*free, *chosen_ready)
            m_att = []
            for b in range(GB):
                for r in range(4):
                    rows = slice(32 * r, 32 * r + 32)
                    bank = take()
                    for c in range(DC):
                        m = mm(bank.tensor[:, c * 2 * P:(c + 1) * 2 * P],
                               [(qT[rows, c, b * P:(b + 1) * P], key[rows, b].rearrange("p par k -> p (par k)"))], mark=c == 1)
                    yield
                    m_top = DVE.put(dve.tensor_reduce, neg_top[:, b, 0, 4 * r:4 * r + 4], blocks(bank.tensor[:, :], 4), X,
                                    ALU.max, negate=True, after=(m, *neg_free))
                    banks.give(bank, m_top)
            rest, rounded = blocks(rest, GB), blocks(rounded, GB)
            m = m_top
            for k in range(2):
                m = DVE.put(dve.tensor_copy, rounded, neg_top[:, :, k, :], after=(m,))
                m = DVE.put(dve.tensor_tensor, neg_top[:, :, k + 1, :], neg_top[:, :, k, :], rounded, ALU.subtract, after=(m,))
            yield
            bank = take()
            PE.wait(m)
            for b in range(GB):
                m = tp(bank.tensor[0:3 * H, b * P:(b + 1) * P], neg_top[:, b].rearrange("p k h -> p (k h)"),
                       mark=b == GB - 1)
            neg_free[:] = [m]
            yield
            m_nt = copy_out(negT[0:3 * H], bank.tensor[0:3 * H, 0:T], bank, (m,))
            yield
            PE.wait(m_nt)
            p_free, turned_free = [[] for _ in range(4)], []
            m_p = {}

            def weights(b, r):
                rows = slice(32 * r, 32 * r + 32)
                bank = take()
                for par in range(2):
                    PE.put(pe.matmul, bank.tensor[:, par * 2 * P:(par + 1) * 2 * P], key[rows, b, par, :],
                           qT[rows, :, b * P:(b + 1) * P], start=True, stop=False, mark=False)
                    for c in range(DC):
                        at, head = 2 * par + c, 4 * r + 2 * c + par
                        m = PE.put(pe.matmul, bank.tensor[:, at * P:(at + 1) * P],
                                   head_of[0:3 * H, head:head + 1].broadcast_to([3 * H, P]),
                                   negT[0:3 * H, b * P:(b + 1) * P], start=False, stop=c == 1, mark=at == 3)
                yield
                m_p[b, r] = SC.put(act.activation, pT[:, r * 4 * P:(r + 1) * 4 * P], bank.tensor[:, :], ACT.Exp,
                                   scale=float(DH) ** -0.5, after=(m, *p_free[r]))
                banks.give(bank, m_p[b, r])

            yield from weights(0, 0)
            for b in range(GB):
                abank = take()
                for r in range(4):
                    if (b, r) != (GB - 1, 3):
                        yield from weights(b + (r + 1) // 4, (r + 1) % 4)
                    PE.wait(m_p[b, r])
                    m = mm(abank.tensor[32 * r:32 * r + VC, :], [(mv[:, b, :], pT[:, r * 4 * P:(r + 1) * 4 * P])], mark=True)
                    p_free[r] = [m]
                    yield
                m = copy_out(turned, abank.tensor[:, :], abank, (m, *turned_free))
                yield
                bank = take()
                PE.wait(m)
                for k in range(4):
                    m = tp(bank.tensor[:, k * P:(k + 1) * P], turned[:, k * P:(k + 1) * P], mark=k == 3)
                turned_free = [m]
                yield
                a4 = bank.tensor[:, :].rearrange("p (n v) -> p n v", v=VC)
                m1 = DVE.put(dve.reciprocal, rec, a4[:, :, DH], after=(m,))
                DVE.wait(m1)
                for par in range(2):
                    half = a4[:, par * HC:(par + 1) * HC, 0:DH].rearrange("p (c r) v -> p c r v", c=DC)
                    m1 = DVE.put(dve.tensor_tensor,
                                 att[:, b, :].rearrange("p (c r two d) -> p c r two d", c=DC, r=4, two=2)[:, :, :, par, :],
                                 half, bc(blocks(rec[:, par * HC:(par + 1) * HC]), 3, DH), ALU.mult)
                banks.give(bank, m1)
                m_att.append(m1)
                yield
            m_a = to_channels(att, m_att, aT)
            aT = blocks(aT)
            yield
            PE.wait(m_a)
            bank, m = project_rows(chunked("wc1x"), aT)
            yield
            return (yield from norm(x, bank, (m, *ready)))

        neg_free = []

        def token_rows(scale, ready, dg):
            for b in range(GB):
                m = DVE.put(dve.tensor_scalar, dg[:, b * P:(b + 1) * P], I, scale[:, b:b + 1], None, ALU.mult, after=ready)
            yield
            bank = take()
            return bank, mm(bank.tensor[:, 0:T], [(onesb[:, :], dg)], after=(m,), mark=True)

        def feed_forward(x, ready, free):
            area = areas["F"]
            area.reset()
            xq, xqT = area.carve(W2), area.carve(W2 // 2).bitcast(BF16)
            dg, tscale = area.carve(T), area.carve(T)
            NJ = HJ // 2
            c_ = [area.carve(W2) for _ in range(NJ)]
            n2 = [area.carve(W2 // 2).bitcast(BF16) for _ in range(NJ)]
            th, top = [area.carve(W2) for _ in range(2)] + [xq], area.carve(W2)
            am, sc1, rs1, rs2 = (area.carve(GB) for _ in range(4))
            POOL.wait(*free)
            SC.wait(*free)
            m = DVE.put(dve.tensor_reduce, am, x[:, :, :], X, ALU.max, apply_absolute_value=True, after=(*ready, *free))
            m = DVE.put(dve.tensor_scalar, am, am, 1e-5, None, ALU.max, after=(m,))
            m1 = DVE.put(dve.reciprocal, sc1, am, after=(m,))
            m1 = DVE.put(dve.tensor_scalar, sc1, sc1, 127.0, None, ALU.mult, after=(m1,))
            m2 = DVE.put(dve.tensor_scalar, rs1, am, wmean[:, 0:1], 1.0 / 127.0, ALU.mult, ALU.mult, after=(m1,))
            DVE.wait(m2)
            for b in range(GB):
                m = DVE.put(dve.tensor_scalar, xq[:, b * D:(b + 1) * D], x[:, b, :], sc1[:, b:b + 1], MAGIC, ALU.mult, ALU.add)
            DVE.wait(m)
            for b in range(GB):
                m = DVE.put(dve.tensor_scalar, xq[:, b * D:(b + 1) * D], xq[:, b * D:(b + 1) * D], MAGIC, None, ALU.subtract)
            yield
            bank, m_ts = yield from token_rows(rs1, (m2,), dg)
            m_ts = copy_out(tscale, bank.tensor[:, 0:T], bank, (m_ts,))
            m_xq = to_channels(blocks(xq, GB), [m, m], xqT)
            xqT = blocks(xqT)
            yield
            PE.wait(m_xq)
            cw = w["convw"][:, :].rearrange("p (j k) -> p j k", k=3)
            DVE.wait(m_xq, m_ts)
            th_free = [[] for _ in th]
            marks, tops = {}, []

            def product(jj):
                bank = take()
                for i in range(2):
                    j = 2 * jj + i
                    m = mm(bank.tensor[:, i * T:(i + 1) * T], [(w1q[:, c, j * P:(j + 1) * P], xqT[:, c, :]) for c in range(DC)],
                           mark=i == 1)
                yield
                marks[jj] = DVE.put(dve.tensor_tensor, blocks(th[jj % 3], 2), blocks(bank.tensor[:, :], 2), bc(tscale, 1, 2),
                                    ALU.mult, after=(m, *th_free[jj % 3]))
                banks.give(bank, marks[jj])

            def convolution(jj):
                h4 = th[jj % 3].rearrange("p (i b t) -> p i b t", i=2, b=GB)
                c4 = c_[jj].rearrange("p (i b t) -> p i b t", i=2, b=GB)
                for i in range(2):
                    j = 2 * jj + i
                    m = SC.put(act.activation, c4[:, i], h4[:, i], ACT.Identity, bias=w["convb"][:, j:j + 1],
                               scale=cw[:, j, 1:2], after=(marks[jj],))
                yield
                for k, dst, src in ((0, slice(1, P), slice(0, P - 1)), (2, slice(0, P - 1), slice(1, P))):
                    DVE.wait(m)
                    for i in range(2):
                        m = DVE.put(dve.scalar_tensor_tensor, c4[:, i, :, dst], h4[:, i, :, src],
                                    cw[:, 2 * jj + i, k:k + 1], c4[:, i, :, dst], ALU.mult, ALU.add)
                marks[jj] = m

            def silu(jj):
                m = SC.put(act.activation, th[jj % 3], c_[jj], ACT.Tanh, scale=0.5, after=(marks[jj],))
                yield
                marks[jj] = DVE.put(dve.scalar_tensor_tensor, c_[jj], th[jj % 3], 1.0, c_[jj], ALU.add, ALU.mult, after=(m,))

            def largest(jj):
                if jj == 0:
                    m = SC.put(act.activation, top, c_[jj], ACT.Abs, after=(marks[jj],))
                    th_free[0] = [marks[jj]]
                else:
                    m = SC.put(act.activation, th[jj % 3], c_[jj], ACT.Abs, after=(marks[jj],))
                    yield
                    m = DVE.put(dve.tensor_tensor, top, th[jj % 3], top, ALU.max, after=(m, *tops))
                    th_free[jj % 3] = [m]
                tops[:] = [m]

            for at in range(NJ + 3):
                for lag, step in ((3, largest), (2, silu), (1, convolution), (0, product)):
                    if 0 <= at - lag < NJ:
                        yield from step(at - lag)
                        yield
            m_top = tops[0]
            bank = take()
            for b in range(GB):
                for i in range(2):
                    at = (2 * b + i) * P
                    m = tp(bank.tensor[:, at:at + P], top[:, i * T + b * P:i * T + (b + 1) * P], after=(m_top,), mark=b + i == 2)
            yield
            m = DVE.put(dve.tensor_reduce, am, blocks(bank.tensor[:, :], GB), X, ALU.max, after=(m,))
            banks.give(bank, m)
            m = DVE.put(dve.tensor_scalar, am, am, 0.5, 1e-5, ALU.mult, ALU.max, after=(m,))
            m1 = DVE.put(dve.reciprocal, sc1, am, after=(m,))
            m1 = DVE.put(dve.tensor_scalar, sc1, sc1, 127.0 * 0.5, None, ALU.mult, after=(m1,))
            m_r2 = DVE.put(dve.tensor_scalar, rs2, am, wmean[:, 1:2], 1.0 / 127.0, ALU.mult, ALU.mult, after=(m1,))
            bank, m = yield from token_rows(sc1, (m_r2,), dg)
            yield
            m_n = []
            for jj in range(NJ):
                m = DVE.put(dve.tensor_tensor, blocks(c_[jj], 2), blocks(c_[jj], 2), bc(bank.tensor[:, 0:T], 1, 2), ALU.mult,
                            after=(m,))
                if jj == NJ - 1:
                    banks.give(bank, m)
                m_n.append(DVE.put(dve.tensor_scalar, n2[jj], c_[jj], MAGIC, MAGIC, ALU.add, ALU.subtract, after=(m,)))
                if jj % 2:
                    yield
            bank = take()
            for b in range(GB):
                m = mm(bank.tensor[:, b * D:(b + 1) * D],
                       [(n2[j // 2][:, (j % 2) * T + b * P:(j % 2) * T + (b + 1) * P], w2q[:, j, :]) for j in range(HJ)],
                       after=m_n, mark=b == 1)
            yield
            return (yield from norm(x, bank, (m, m_r2), rs2))

        x_out = [[] for _ in range(NX)]
        ended = {}

        def station_a(g):
            if g == 0:
                yield from setup_early()
            src = io["x"][g * T:(g + 1) * T, :].rearrange("(b t) d -> t b d", b=GB)
            m = s_x[g % NX].dma(SP, sp.dma_start, xs[g % NX][:, :, :], src, after=x_out[g % NX])
            ended["A", g] = yield from windowed(g, xs[g % NX], [m], ended.get(("A", g - 1), []))

        def station_b(g):
            if g < 0:
                return (yield from setup_late())
            x = xs[g % NX]
            r = yield from cross(g, x, ended["A", g], ended.get(("B", g - 1), late_done))
            ended["B", g] = yield from experts(g, x, r)

        def station_c(g):
            ended["C", g] = yield from decayed(g, xs[g % NX], ended["B", g], ended.get(("C", g - 1), late_done))

        def station_d(g):
            handed[g] = yield from choose_memory(g, xs[g % NX], chosen[g % 2], ended["C", g], ended.get(("D", g - 1), late_done),
                                                 ended.get(("E", g - 2), []))
            ended["D", g] = handed[g]

        def station_e(g):
            ended["E", g] = yield from memory(xs[g % NX], chosen[g % 2], ended["C", g], handed[g],
                                              ended.get(("E", g - 1), late_done))

        def station_f(g):
            x = xs[g % NX]
            r = yield from feed_forward(x, ended["E", g], ended.get(("F", g - 1), late_done))
            m = s_out[g % NX].dma(SP, sp.dma_start, out[g * T:(g + 1) * T, :].rearrange("(b t) d -> t b d", b=GB), x[:, :, :],
                                  after=r)
            x_out[g % NX] = [m]
            ended["F", g] = r

        handed = {}
        engines = (PE, DVE, SC, POOL, SP)

        class Job:

            def __init__(self, name, station, first):
                self.name, self.station, self.g, self.work, self.ready, self.held = name, station, first, None, 0.0, 0
                self.parts, self.all_parts = 0, 30

            def place(self):
                return self.g + LAGS[self.name] + self.parts / self.all_parts

            def may_go(self):
                if self.g >= NG:
                    return False
                if self.work is not None or self.g < 0:
                    return True
                if self.name == "A":
                    return self.g < NX or ("F", self.g - NX) in ended
                if self.name == "D" and self.g >= 2 and ("E", self.g - 2) not in ended:
                    return False
                return (chr(ord(self.name) - 1), self.g) in ended

            def go(self):
                if self.work is None:
                    self.work = self.station(self.g)
                    if self.g >= 0 and self.name != "A":
                        self.ready = max(m.time for m in ended[chr(ord(self.name) - 1), self.g])
                before = len(banks.free)
                for e in engines:
                    e.latest = 0.0
                try:
                    next(self.work)
                except StopIteration:
                    self.work, self.g = None, self.g + 1
                self.parts += 1
                if self.work is None:
                    self.parts, self.all_parts = 0, self.parts
                self.held += before - len(banks.free)
                self.ready = max(e.latest for e in engines)

        jobs = [Job("A", station_a, 0), Job("B", station_b, -1), Job("C", station_c, 0), Job("D", station_d, 0),
                Job("E", station_e, 0), Job("F", station_f, 0)]
        while True:
            choice = [j for j in jobs if j.may_go()]
            if not choice:
                break
            if len(banks.free) < 3:
                choice = [j for j in choice if j.held] or choice
            now = PE.time + SLACK
            job = min(choice, key=lambda j: (max(j.ready - now, 0), j.place()))
            job.go()
        for marks in x_out:
            SP.wait(*marks)

        with nc.Block() as block:
            @block.sync
            def _(eng):
                SP.play(eng)

            @block.tensor
            def _(eng):
                PE.play(eng)

            @block.vector
            def _(eng):
                DVE.play(eng)

            @block.scalar
            def _(eng):
                SC.play(eng)

            @block.gpsimd
            def _(eng):
                POOL.play(eng)


def constants():
    f = np.float32
    p = np.arange(P)
    half = ROT // 2
    inv = (1.0 / f(10000.0) ** (np.arange(half, dtype=f) * f(2.0) / f(ROT))).astype(f)
    ang = (p.astype(f)[:, None] * inv).astype(f)
    cos, sin = np.cos(ang).astype(f), np.sin(ang).astype(f)
    diff = p[:, None] - p[None, :]
    bit = [((np.maximum(diff, 0) >> i) & 1).astype(f) for i in range(7)]
    q, k = p[:, None], p[None, :]
    same = (q // NS == k // NS) & (k <= q)
    pos = np.zeros((P, 1), f)
    pos[:WIN * H, 0] = np.repeat(np.linspace(0.0, 1.0, WIN, dtype=f), H)
    return {
        "ident": np.eye(P, dtype=f),
        "headsum": (p[:, None] // DH == np.arange(-SLIDE, HC + SLIDE)[None, :]).astype(f),
        "parity": (p[:, None] % 32 // DH == np.arange(2)[None, :]).astype(f),
        "head_of": (p[:, None] % H == np.arange(H)[None, :]).astype(f),
        "part": (p[:, None] % 32 == np.arange(3)[None, :]).astype(f),
        "iota16": np.tile(np.arange(1, NS + 1, dtype=f), (P, 1)),
        "iota128": np.tile(np.arange(P, dtype=f), (P, 1)),
        "pos": pos,
        "cos_sin": np.concatenate([cos, cos, -sin, sin], 1),
        "blk": np.where(same, f(0), f(FAR)).astype(f),
        "bits": np.concatenate(bit + [1 - b for b in bit] + [(diff >= 0).astype(f)], 1),
    }


def laid_out(a):
    def rows(m):
        c = m.shape[0] // P
        return m.reshape(c, P, -1).transpose(1, 0, 2).reshape(P, -1)

    def per_head(m):
        return np.tile(m.reshape(H, -1), (WIN, 1))

    def by_group(m):
        return m.reshape(NG, T, DC, P).transpose(0, 3, 2, 1).reshape(NG, P, DC * T)

    bq = a["L1_attn_bqkv"]
    bias_rows = np.zeros((P, D), np.float32)
    for i, name in enumerate(("L0_attn_bo", "L0_xattn_bv", "L1_attn_bproj")):
        bias_rows[32 * i:32 * i + 3] = a[name]
    wkv = a["L1_xattn_Wkv"]
    return {
        "x": a["x"].reshape(NSEQ * P, D), "xT": by_group(a["x"]), "ctxT": by_group(a["ctx_1024"]),
        "wq0": rows(a["L0_attn_wq"].T), "wk0": rows(a["L0_attn_wk"].T), "wv0": rows(a["L0_attn_wv"].T),
        "wo0": rows(a["L0_attn_wo"].T),
        "c1": per_head(a["L0_attn_cw1"]), "b1": per_head(a["L0_attn_cb1"]), "c2": per_head(a["L0_attn_cw2"]),
        "b2": per_head(a["L0_attn_cb2"]), "c3": per_head(a["L0_attn_cw3"]), "b3": per_head(a["L0_attn_cb3"]),
        "raw_q": rows(a["L0_xattn_Wq"]), "raw_k": rows(a["L0_xattn_Wk"]), "wv0x": rows(a["L0_xattn_Wv"].T),
        "xmask": a["mask_SxS2_fk0"],
        "wr": rows(a["L0_ffn_Wr"].T),
        "wqkv_e": a["L0_ffn_Wqkv"].reshape(NE, DC, P, 3 * HP).transpose(2, 1, 0, 3).reshape(P, -1),
        "wo_e": a["L0_ffn_Wo"].transpose(1, 0, 2).reshape(P, -1),
        "wq1T": rows(a["L1_attn_Wqkv"][:, :D].T), "wk1T": rows(a["L1_attn_Wqkv"][:, D:2 * D].T),
        "wv1T": rows(a["L1_attn_Wqkv"][:, 2 * D:].T), "wp1": rows(a["L1_attn_Wproj"]),
        "bqkv1": bq.reshape(3 * DC, P).T,
        "gamma": np.broadcast_to(a["L1_attn_gamma"].reshape(1, 1), (P, 1)),
        "wq1x": rows(a["L1_xattn_Wq"].T), "wkv1x": rows(np.concatenate([np.tile(wkv[:DH].T, (1, HC)), wkv[DH:].T], 1)),
        "wc1x": rows(a["L1_xattn_Wc"].T),
        "raw1": rows(a["L1_ffn_w1"].T), "raw2": rows(a["L1_ffn_w2"].T),
        "convw": a["L1_ffn_conv_w"].reshape(HJ, P, 3).transpose(1, 0, 2).reshape(P, -1),
        "convb": a["L1_ffn_conv_b"].reshape(HJ, P).T,
        "rows": bias_rows,
    }


def kernel(**inputs):
    import concourse.bacc as bacc
    from concourse.bass_utils import run_bass_kernel_spmd

    nc = bacc.Bacc("TRN2", target_bir_lowering=False, num_devices=1)
    arrays = {**laid_out({k: np.asarray(v) for k, v in inputs.items()}), **constants()}
    arrays = {k: np.ascontiguousarray(v) for k, v in arrays.items()}
    io = {k: nc.dram_tensor(f"in_{k}", v.shape, mybir.dt.from_np(v.dtype), kind="ExternalInput").ap()
          for k, v in arrays.items()}
    out = nc.dram_tensor("y", (NSEQ * P, D), F32, kind="ExternalOutput").ap()
    build(nc, io, out)
    r = run_bass_kernel_spmd(nc, [{f"in_{k}": v for k, v in arrays.items()}], core_ids=[0])
    return r.results[0]["y"].reshape(NSEQ, P, D)
```
